# Optimizing a Trainium2 kernel written in Bass

```python
import numpy as np
import jax
import jax.numpy as jnp

def _softmax(x, axis=-1):
    return jax.nn.softmax(x, axis=axis)

def _gelu(x):
    return jax.nn.gelu(x, approximate=True)

def _silu(x):
    return jax.nn.silu(x)

def _sigmoid(x):
    return jax.nn.sigmoid(x)

def _layernorm(x, axis=-1, eps=1e-05):
    m = jnp.mean(x, axis=axis, keepdims=True)
    v = jnp.var(x, axis=axis, keepdims=True)
    return (x - m) / jnp.sqrt(v + eps)

def _scatter_add(tgt, idx, src, axis=0):
    return tgt.at[idx].add(src)

def _segment_sum(src, seg, n):
    return jax.ops.segment_sum(src, seg, n)
kernel_name = 'mk_xattn_ffn_d1_seqx_r2_a51850'

def setup_inputs(seed: int=0):
    np.random.seed(seed)
    _w = jnp.asarray

    def _rec_inputs():
        import jax
        import jax.numpy as jnp
        _rk = jax.random.key(seed)
        x = -0.0002928 + 1 * jax.random.normal(jax.random.fold_in(_rk, 1), (8, 512, 512), jnp.float32)
        _lenS = 512 - jax.random.randint(jax.random.fold_in(_rk, 7), (8,), 0, max(1, 512 // 4) + 1, jnp.int32)
        _lenS2 = 512 - jax.random.randint(jax.random.fold_in(_rk, 8), (8,), 0, max(1, 512 // 4) + 1, jnp.int32)
        _ctx_1024P = jax.random.normal(jax.random.fold_in(_rk, 11), (8, 16, 512), jnp.float32)
        _ctx_1024c = jax.random.dirichlet(jax.random.fold_in(_rk, 511), 0.3 * jnp.ones((16,), jnp.float32), (8, 512))
        _ctx_1024t = jnp.einsum('bsk,bkd->bsd', _ctx_1024c, _ctx_1024P)
        _ctx_1024t = _ctx_1024t * jax.lax.rsqrt(jnp.mean(jnp.square(_ctx_1024t)) + 1e-12) * 0.953939
        ctx_1024 = -1.39393e-06 + 0.999914 * (_ctx_1024t + 0.3 * jax.random.normal(jax.random.fold_in(_rk, 611), (8, 512, 512), jnp.float32))
        return (x, ctx_1024)
    x, ctx_1024 = _rec_inputs()

    def _L0_xattn_setup():
        import jax, jax.numpy as jnp
        import numpy as np
        EMBED_DIM = 512
        NUM_HEADS = 16
        HEAD_DIM = EMBED_DIM // NUM_HEADS
        key = jax.random.key(seed)
        ks = jax.random.split(key, 11)
        B, S, D = (2, 1024, EMBED_DIM)
        scale = 1.0 / np.sqrt(D)
        inp = {'query': jax.random.normal(ks[0], (B, S, D), jnp.float32), 'key': jax.random.normal(ks[1], (B, S, D), jnp.float32), 'value': jax.random.normal(ks[2], (B, S, D), jnp.float32), 'Wq': jax.random.normal(ks[3], (D, D), jnp.float32) * scale, 'bq': jnp.zeros((D,), jnp.float32), 'Wk': jax.random.normal(ks[4], (D, D), jnp.float32) * scale, 'bk': jnp.zeros((D,), jnp.float32), 'Wv': jax.random.normal(ks[5], (D, D), jnp.float32) * scale, 'bv': jnp.zeros((D,), jnp.float32), 'Wo': jax.random.normal(ks[6], (D, D), jnp.float32) * scale, 'bo': jnp.zeros((D,), jnp.float32)}
        return inp
    _L0_xattn_all = _L0_xattn_setup()
    _L0_xattn_in = {k: v for k, v in _L0_xattn_all.items() if k in ('Wq', 'bq', 'Wk', 'bk', 'Wv', 'bv', 'Wo', 'bo')}
    del _L0_xattn_all

    def _L0_ffn_setup():
        import jax, jax.numpy as jnp
        import numpy as np
        ALPHA = 1.702
        LIMIT = 7.0
        K = 2
        key = jax.random.key(seed)
        ks = jax.random.split(key, 4)
        B, S, H, E, I = (1, 512, 512, 8, 512)
        return {'hidden_states': jax.random.normal(ks[0], (B, S, H), jnp.float32), 'router_weight': jax.random.normal(ks[1], (E, H), jnp.float32), 'router_bias': jnp.zeros((E,), jnp.float32), 'gate_up_proj': jax.random.normal(ks[2], (E, H, 2 * I), jnp.float32) * 0.02, 'gate_up_bias': jnp.zeros((E, 2 * I), jnp.float32), 'down_proj': jax.random.normal(ks[3], (E, I, H), jnp.float32) * 0.02, 'down_bias': jnp.zeros((E, H), jnp.float32)}
    _L0_ffn_all = _L0_ffn_setup()
    _L0_ffn_in = {k: v for k, v in _L0_ffn_all.items() if k in ('router_weight', 'router_bias', 'gate_up_proj', 'gate_up_bias', 'down_proj', 'down_bias')}
    del _L0_ffn_all
    return {'x': x, 'ctx_1024': ctx_1024, 'L0_xattn_Wq': _L0_xattn_in['Wq'], 'L0_xattn_bq': _L0_xattn_in['bq'], 'L0_xattn_Wk': _L0_xattn_in['Wk'], 'L0_xattn_bk': _L0_xattn_in['bk'], 'L0_xattn_Wv': _L0_xattn_in['Wv'], 'L0_xattn_bv': _L0_xattn_in['bv'], 'L0_xattn_Wo': _L0_xattn_in['Wo'], 'L0_xattn_bo': _L0_xattn_in['bo'], 'L0_ffn_router_weight': _L0_ffn_in['router_weight'], 'L0_ffn_router_bias': _L0_ffn_in['router_bias'], 'L0_ffn_gate_up_proj': _L0_ffn_in['gate_up_proj'], 'L0_ffn_gate_up_bias': _L0_ffn_in['gate_up_bias'], 'L0_ffn_down_proj': _L0_ffn_in['down_proj'], 'L0_ffn_down_bias': _L0_ffn_in['down_bias']}

def reference(x, ctx_1024, L0_xattn_Wq, L0_xattn_bq, L0_xattn_Wk, L0_xattn_bk, L0_xattn_Wv, L0_xattn_bv, L0_xattn_Wo, L0_xattn_bo, L0_ffn_router_weight, L0_ffn_router_bias, L0_ffn_gate_up_proj, L0_ffn_gate_up_bias, L0_ffn_down_proj, L0_ffn_down_bias):
    import jax
    import jax.numpy as jnp

    def _L0_xattn_ref(query, key, value, Wq, bq, Wk, bk, Wv, bv, Wo, bo):
        import jax, jax.numpy as jnp
        import numpy as np
        EMBED_DIM = 512
        NUM_HEADS = 16
        HEAD_DIM = EMBED_DIM // NUM_HEADS
        B, S, D = query.shape
        H, Hd = (NUM_HEADS, HEAD_DIM)

        def split_heads(x):
            return x.reshape(B, S, H, Hd).transpose(0, 2, 1, 3)
        Q = split_heads(query @ Wq.T + bq)
        K = split_heads(key @ Wk.T + bk)
        V = split_heads(value @ Wv.T + bv)
        scores = jnp.einsum('bhqd,bhkd->bhqk', Q, K) / np.sqrt(Hd).astype(jnp.float32)
        attn = jax.nn.softmax(scores, axis=-1)
        out = jnp.einsum('bhqk,bhkd->bhqd', attn, V)
        out = out.transpose(0, 2, 1, 3).reshape(B, S, D)
        return out @ Wo.T + bo

    def _L0_ffn_ref(hidden_states, router_weight, router_bias, gate_up_proj, gate_up_bias, down_proj, down_bias):
        import jax, jax.numpy as jnp
        import numpy as np
        ALPHA = 1.702
        LIMIT = 7.0
        K = 2
        B, S, H = hidden_states.shape
        E = router_weight.shape[0]
        I = down_proj.shape[1]
        T = B * S
        flat = hidden_states.reshape(T, H)
        logits = flat @ router_weight.T + router_bias
        scores = jax.nn.softmax(logits, axis=-1)
        topk_vals, topk_idx = jax.lax.top_k(scores, K)
        w = jnp.zeros((T, E), scores.dtype).at[jnp.arange(T)[:, None], topk_idx].set(topk_vals)
        gu = jnp.einsum('th,ehf->tef', flat, gate_up_proj) + gate_up_bias
        gate = jnp.minimum(gu[..., :I], LIMIT)
        up = jnp.clip(gu[..., I:], -LIMIT, LIMIT)
        glu = gate * jax.nn.sigmoid(gate * ALPHA)
        act = (up + 1.0) * glu
        down = jnp.einsum('tei,eih->teh', act, down_proj) + down_bias
        out = jnp.einsum('teh,te->th', down, w)
        return out.reshape(B, S, H)
    x = x + _L0_xattn_ref(_layernorm(x, axis=-1), ctx_1024, ctx_1024, L0_xattn_Wq, L0_xattn_bq, L0_xattn_Wk, L0_xattn_bk, L0_xattn_Wv, L0_xattn_bv, L0_xattn_Wo, L0_xattn_bo)
    x = x + _L0_ffn_ref(_layernorm(x, axis=-1), L0_ffn_router_weight, L0_ffn_router_bias, L0_ffn_gate_up_proj, L0_ffn_gate_up_bias, L0_ffn_down_proj, L0_ffn_down_bias)
    return x

_drawn_inputs = setup_inputs


def setup_inputs(seed=0):
    import zlib

    import numpy as np

    out = dict(_drawn_inputs(seed))
    spreads = {'L0_xattn_bq': (0.0, 0.384),
     'L0_xattn_bk': (0.0, 2.0),
     'L0_xattn_bv': (0.0, 0.1),
     'L0_xattn_bo': (0.0, 0.1),
     'L0_ffn_router_bias': (0.0, 2.0),
     'L0_ffn_gate_up_bias': (0.0, 0.303),
     'L0_ffn_down_bias': (0.0, 0.1)}
    factors = {}
    for name, (base, spread) in spreads.items():
        noise = np.random.default_rng([zlib.crc32(name.encode()), seed]).standard_normal(out[name].shape)
        drawn = base * np.exp(spread * noise) if base else spread * noise
        out[name] = jnp.asarray(drawn.astype(out[name].dtype))
    for name, factor in factors.items():
        out[name] = (out[name] * factor).astype(out[name].dtype)
    return out
```

```python
from contextlib import ExitStack

import concourse.bass as bass
from concourse import mybir

ALU = mybir.AluOpType
ACT = mybir.ActivationFunctionType
AX = mybir.AxisListType
F32 = mybir.dt.float32
F32R = mybir.dt.float32r
BF16 = mybir.dt.bfloat16
I32 = mybir.dt.int32
U32 = mybir.dt.uint32

P = 128
LN_EPS = 1e-5
HEADS = 16
GROUP = 4
HD = 32
TOP_K = 2
ALPHA = 1.702
LIMIT = 7.0
FTOK = 256


class Count:

    def __init__(self, sem, step=1, ahead=1):
        self.sem, self.step, self.per_turn, self.ahead = sem, step, 0, ahead

    def did(self):
        self.per_turn += self.step
        return self.per_turn

    def open(self, eng, first_turn=0):
        eng.sem_inc(self.sem, (first_turn + 1) * self.per_turn)

    def wait(self, eng, turn, mark, go=None):
        self._wait(eng, turn * self.per_turn + (self.ahead * self.per_turn + mark), go)

    def wait_before(self, eng, turn, mark, go=None):
        self._wait(eng, turn * self.per_turn + mark, go)

    def _wait(self, eng, value, go):
        if go is not None:
            value = value if isinstance(value, int) else eng.to_reg(value)
            eng.wait_ge(go, 1)
        eng.wait_ge(self.sem, value)


class Turn:

    def __init__(self, sem, tag):
        self.q = {n: [] for n in ("sp", "act", "dve", "pe", "pool")}
        self.count = {n: Count(sem(f"{tag}_{n}")) for n in ("act", "dve", "pe", "pool")}
        self.act, self.dve, self.pe, self.pool = self.count.values()
        self.marks = {}

    def step(self, engine, waits, emit, go=None):
        count = self.count[engine]

        def f(e, turn):
            for c, m in waits:
                c.wait(e, turn, m, go)
            emit(e).then_inc(count.sem, 1)
        self.q[engine].append(f)
        return count, count.did()

    def run(self, engine, eng, turn):
        for f in self.q[engine]:
            f(eng, turn)


def attention_stage(nc, x, ctx_t, w_t, bq, bk, bv, bo, router_w, router_b, x2_dram, xln_dram, logits, ident, s_go):
    B, S, D = x.shape
    C = D // P
    T = S // P
    E = router_w.shape[0]
    scale = 1.0 / float(HD) ** 0.5

    with ExitStack() as ctx:
        sb = lambda name, shape, dt=F32: ctx.enter_context(nc.sbuf_tensor(name, shape, dt))
        psum = lambda name, shape: ctx.enter_context(nc.psum_tensor(name, shape, F32))
        sem = lambda name: ctx.enter_context(nc.semaphore(name))

        wq, wk, wv, wo = (sb(n, [P, C, D]) for n in ("wq", "wk", "wv", "wo"))
        rw_rows = sb("rw_rows", [P, E, D])
        rb_rows = sb("rb_rows", [P, E])
        bv_rows = sb("bv_rows", [P, D])
        bo_rows = sb("bo_rows", [P, D])
        bq_col = sb("bq_col", [P, C])
        bk_col = sb("bk_col", [P, C])
        x_in = sb("x_in", [P, T, D])
        x2 = sb("x2", [P, T, D])
        ctxT = sb("ctxT", [P, C, S])
        xT = sb("xT", [P, C, S])
        hi = {n: [sb(f"{n}_hi{i}", [P, S], F32R) for i in range(2)] for n in "qk"}
        lo = {n: [sb(f"{n}_lo{i}", [P, S], F32R) for i in range(2)] for n in "qk"}
        qs = [sb(f"qs{c}", [P, GROUP, S], F32R) for c in range(C)]
        ks = [sb(f"ks{c}", [P, GROUP, S], F32R) for c in range(C)]
        v = sb("v", [P, T, D])
        pt = [sb(f"pt{i}", [P, GROUP, S]) for i in range(2)]
        oT = sb("oT", [P, C, S])
        inv = sb("inv", [P, S])
        ones = sb("ones", [P, HD])
        negmax = sb("negmax", [P, C, GROUP * T])
        m_hi = sb("m_hi", [GROUP * T, P], F32R)
        m_lo = sb("m_lo", [GROUP * T, P], F32R)
        stats = sb("stats", [P, 2, T, 6])
        mv = sb("mv", [P, 2, T, 2])
        var_eps = sb("var_eps", [P, 2, T])
        rstd = sb("rstd", [P, 2, T])
        minus_half = sb("minus_half", [P, T])
        eps_col = sb("eps_col", [P, T])
        lg = sb("lg", [P, T, E])

        work = [psum(f"work{i}", [P, S]) for i in range(2)]
        st = [psum(f"st{i}", [P, 2, S]) for i in range(2)]
        o_ps = psum("o_ps", [P, S])
        sum_ps = psum("sum_ps", [P, S])

        s_const = sem("s_const")
        s_init = sem("s_init")
        g = Turn(sem, "att")
        pe, act, dve, pool = g.pe, g.act, g.dve, g.pool
        x_load, ctx_load, res_load = (Count(sem(n), 16) for n in ("s_x", "s_ctx", "s_res"))
        stack = [Count(sem(f"s_stack{c}"), 16) for c in range(C)]
        mrow = Count(sem("s_mrow"), 16)
        x2_store, xln_store = Count(sem("s_x2"), 16), Count(sem("s_xln"), 16)

        marks = g.marks
        bank_use = [0]
        bank_freed = [None, None]

        def take_bank():
            i = bank_use[0] % 2
            bank_use[0] += 1
            freed = bank_freed[i]
            if freed is None:
                g.q["pe"].append(lambda e, b, i=i: last_reader[i][0].wait_before(e, b, last_reader[i][1]))
            else:
                g.q["pe"].append(lambda e, b, f=freed: f[0].wait(e, b, f[1]))
            return i

        def free_bank(i, count, mark):
            bank_freed[i] = (count, mark)

        last_reader = {}

        def norm_stats(g, src, slot, first_wait):
            for t in range(T):
                def f(e, b, t=t):
                    if t == 0:
                        first_wait(e, b)
                    e.bn_stats(stats[:, slot, t, :], src[:, t, :]).then_inc(g.dve.sem, 1)
                g.q["dve"].append(f)
                g.marks["bn", slot, t] = g.dve.did()
            for t in range(T):
                g.marks["mv", slot] = g.step("dve", [(g.dve, g.marks["bn", slot, t])],
                                             lambda e, t=t: e.bn_aggr(mv[:, slot, t, :], stats[:, slot, t, :]), s_go)
            r = g.step("pool", [g.marks["mv", slot]],
                       lambda e: e.tensor_tensor(var_eps[:, slot, :], mv[:, slot, :, 1], eps_col[:, :], ALU.add))
            g.marks["rstd", slot] = g.step("pool", [r], lambda e: e.tensor_tensor(rstd[:, slot, :], var_eps[:, slot, :],
                                                                                 minus_half[:, :], ALU.pow))

        def norm_apply(g, dst, src, slot, t, first_wait=None):
            def f(e, b):
                if first_wait:
                    first_wait(e, b)
                g.pool.wait(e, b, g.marks["rstd", slot][1])
                e.tensor_scalar(dst[:, t, :], src[:, t, :], mv[:, slot, t, 0:1], rstd[:, slot, t:t + 1],
                                ALU.subtract, ALU.mult).then_inc(g.dve.sem, 1)
            g.q["dve"].append(f)
            return g.dve.did()

        def transpose_x():
            for c in range(C):
                i = take_bank()
                def f(e, b, c=c, i=i):
                    dve.wait_before(e, b, marks["ln1"])
                    for t in range(T):
                        ins = e.transpose(work[i][:, t * P:(t + 1) * P], x_in[:, t, c * P:(c + 1) * P], ident[:, :])
                    ins.then_inc(pe.sem, 1)
                g.q["pe"].append(f)
                done = pe.did()
                def on_act(e, b, c=c, i=i, done=done):
                    pe.wait(e, b, done)
                    e.activation(xT[:, c, :], work[i][:, :], ACT.Copy).then_inc(act.sem, 1)
                g.q["act"].append(on_act)
                free_bank(i, act, act.did())
            marks["x_turned"] = done
            marks["xT"] = act.per_turn

        def project_qk(name, c):
            w, src, bias = (wq, xT, bq_col) if name == "q" else (wk, ctxT, bk_col)
            i = take_bank()
            def f(e, b):
                if name == "q":
                    act.wait(e, b, marks["xT"])
                else:
                    ctx_load.wait_before(e, b, marks["ctx_next"])
                for k in range(C):
                    ins = e.matmul(work[i][:, :], w[:, k, c * P:(c + 1) * P], src[:, k, :], start=(k == 0), stop=(k == C - 1))
                ins.then_inc(pe.sem, 1)
            g.q["pe"].append(f)
            done = pe.did()
            h, l = hi[name][c % 2], lo[name][c % 2]
            def on_act(e, b):
                pe.wait(e, b, done)
                if c >= 2:
                    stack[c - 2].wait(e, b, marks["stack", c - 2])
                else:
                    stack[c + 2].wait_before(e, b, marks["stack", c + 2])
                e.activation(h[:, :], work[i][:, :], ACT.Identity, bias=bias[:, c:c + 1]).then_inc(act.sem, 1)
            g.q["act"].append(on_act)
            h_done = act.did()
            def d(e, b):
                act.wait(e, b, h_done)
                e.scalar_tensor_tensor(out=l[:, :], in0=work[i][:, :], scalar=bias[:, c:c + 1], in1=h[:, :].bitcast(F32),
                                       op0=ALU.add, op1=ALU.subtract).then_inc(dve.sem, 1)
            g.q["dve"].append(d)
            l_done = dve.did()
            free_bank(i, dve, l_done)
            dst = qs[c] if name == "q" else ks[c]
            parts = (h, h, l) if name == "q" else (h, l, h)
            def s(e, b):
                dve.wait(e, b, l_done, s_go)
                pe.wait_before(e, b, marks["c_end", c])
                for g3 in range(3):
                    for r in range(GROUP):
                        e.dma_start(dst[HD * g3:HD * (g3 + 1), r, :].bitcast(F32),
                                    parts[g3][HD * r:HD * (r + 1), :].bitcast(F32)).then_inc(stack[c].sem, 16)
            g.q["sp"].append(s)
            for _ in range(3 * GROUP):
                marks["stack", c] = stack[c].did()

        def project_v(c):
            i = take_bank()
            def f(e, b):
                ctx_load.wait_before(e, b, marks["ctx_next"])
                for t in range(T):
                    for k in range(C):
                        ins = e.matmul(work[i][:, t * P:(t + 1) * P], ctxT[:, k, t * P:(t + 1) * P],
                                       wv[:, k, c * P:(c + 1) * P], start=(k == 0), stop=(k == C - 1))
                ins.then_inc(pe.sem, 1)
            g.q["pe"].append(f)
            done = pe.did()
            def d(e, b):
                pe.wait(e, b, done)
                e.tensor_tensor(v[:, :, c * P:(c + 1) * P], work[i][:, :].rearrange("p (t n) -> p t n", t=T),
                                bv_rows[:, c * P:(c + 1) * P].unsqueeze(1).to_broadcast([P, T, P]), ALU.add).then_inc(dve.sem, 1)
            g.q["dve"].append(d)
            marks["v", c] = dve.did()
            free_bank(i, dve, marks["v", c])

        def row_max(c, h):
            for t in range(T):
                i = take_bank()
                def f(e, b, i=i, t=t):
                    stack[c].wait(e, b, marks["stack", c])
                    e.matmul(work[i][:, :], qs[c][0:3 * HD, h, t * P:(t + 1) * P], ks[c][0:3 * HD, h, :],
                             start=True, stop=True).then_inc(pe.sem, 1)
                g.q["pe"].append(f)
                done = pe.did()
                def d(e, b, i=i, t=t, done=done):
                    pe.wait(e, b, done)
                    e.tensor_reduce(negmax[:, c, h * T + t:h * T + t + 1], work[i][:, :], AX.X, ALU.max,
                                    negate=True).then_inc(dve.sem, 1)
                g.q["dve"].append(d)
                marks["max", c] = dve.did()
                free_bank(i, dve, marks["max", c])

        def turn_max(c):
            i = take_bank()
            R = GROUP * T
            def f(e, b):
                dve.wait(e, b, marks["max", c])
                e.transpose(work[i][0:R, 0:P], negmax[:, c, :], ident[:, :]).then_inc(pe.sem, 1)
            g.q["pe"].append(f)
            done = pe.did()
            def on_act(e, b):
                pe.wait(e, b, done)
                if c:
                    mrow.wait(e, b, marks["mrow", c - 1])
                else:
                    mrow.wait_before(e, b, marks["mrow", C - 1])
                e.activation(m_hi[:, :], work[i][0:R, 0:P], ACT.Copy).then_inc(act.sem, 1)
            g.q["act"].append(on_act)
            h_done = act.did()
            def d(e, b):
                act.wait(e, b, h_done)
                e.tensor_tensor(m_lo[:, :], work[i][0:R, 0:P], m_hi[:, :].bitcast(F32), ALU.subtract).then_inc(dve.sem, 1)
            g.q["dve"].append(d)
            l_done = dve.did()
            free_bank(i, dve, l_done)
            def s(e, b):
                dve.wait(e, b, l_done)
                for row, src in ((3 * HD, m_hi), (3 * HD + 1, m_lo)):
                    e.dma_start(qs[c][row:row + 1, :, :].rearrange("a h n -> a (h n)").bitcast(F32),
                                src[:, :].bitcast(F32)).then_inc(mrow.sem, 16)
            g.q["sp"].append(s)
            mrow.did()
            marks["mrow", c] = mrow.did()

        exp_marks = []
        pv_marks = []

        def exp_scores(c, k):
            n = c * T + k
            for p in range(2):
                def f(e, b, p=p):
                    if p == 0 and k == 0:
                        mrow.wait(e, b, marks["mrow", c])
                    if n:
                        act.wait(e, b, exp_marks[2 * (n - 1) + p])
                    else:
                        act.wait_before(e, b, exp_marks[2 * (C * T - 1) + p])
                    for j in range(2):
                        h = 2 * p + j
                        ins = e.matmul(st[p][:, j, :], ks[c][0:3 * HD + 2, h, k * P:(k + 1) * P],
                                       qs[c][0:3 * HD + 2, h, :], start=True, stop=True)
                    ins.then_inc(pe.sem, 1)
                g.q["pe"].append(f)
                done = pe.did()
                def on_act(e, b, p=p, done=done):
                    pe.wait(e, b, done)
                    if n >= 2:
                        pe.wait(e, b, pv_marks[n - 2])
                    else:
                        pe.wait_before(e, b, pv_marks[n - 2 + C * T])
                    e.activation(pt[k % 2][:, 2 * p:2 * p + 2, :], st[p][:, :, :], ACT.Exp, scale=scale).then_inc(act.sem, 1)
                g.q["act"].append(on_act)
                exp_marks.append(act.did())

        def weigh_values(c, k):
            n = c * T + k
            def f(e, b):
                if k == 0:
                    dve.wait(e, b, marks["v", c])
                    if c:
                        dve.wait(e, b, marks["norm", c - 1])
                    else:
                        dve.wait_before(e, b, marks["norm", C - 1])
                act.wait(e, b, exp_marks[2 * n + 1])
                for h in range(GROUP):
                    rows = slice(HD * h, HD * (h + 1))
                    e.matmul(o_ps[rows, :], v[:, k, c * P + HD * h:c * P + HD * (h + 1)], pt[k % 2][:, h, :],
                             start=(k == 0), stop=(k == T - 1))
                for h in range(GROUP):
                    rows = slice(HD * h, HD * (h + 1))
                    ins = e.matmul(sum_ps[rows, :], ones[:, :], pt[k % 2][:, h, :], start=(k == 0), stop=(k == T - 1))
                ins.then_inc(pe.sem, 1)
            g.q["pe"].append(f)
            pv_marks.append(pe.did())

        def normalise(c):
            m = dve.did()
            def d(e, b):
                pe.wait(e, b, pv_marks[c * T + T - 1])
                e.reciprocal(inv[:, :], sum_ps[:, :]).then_inc(dve.sem, 1)
                dve.wait(e, b, m)
                if c == 0:
                    xln_store.wait(e, b, marks["xln_store"])
                e.tensor_tensor(oT[:, c, :], o_ps[:, :], inv[:, :], ALU.mult).then_inc(dve.sem, 1)
            g.q["dve"].append(d)
            marks["norm", c] = dve.did()
            marks["c_end", c] = pv_marks[c * T + T - 1]

        def project_out(t):
            i = take_bank()
            def f(e, b):
                dve.wait(e, b, marks["norm", C - 1])
                for c in range(C):
                    ins = e.matmul(work[i][:, :], oT[:, c, t * P:(t + 1) * P], wo[:, c, :], start=(c == 0), stop=(c == C - 1))
                ins.then_inc(pe.sem, 1)
            g.q["pe"].append(f)
            done = pe.did()
            def d(e, b):
                pe.wait(e, b, done)
                pool.wait(e, b, marks["x_bo"])
                e.tensor_tensor(x2[:, t, :], work[i][:, :], x2[:, t, :], ALU.add).then_inc(dve.sem, 1)
            g.q["dve"].append(d)
            marks["x2", t] = dve.did()
            marks["out_pe"] = done
            free_bank(i, dve, marks["x2", t])

        def post_apply(g, t, first_wait=None):
            g.marks["ln2", t] = norm_apply(g, oT, x2, 1, t, first_wait)

        def post_logits(g, t, experts):
            for n in experts:
                g.marks["logits"] = g.step("dve", [g.marks.get("logits", (g.dve, 0)), (g.dve, g.marks["ln2", t])], lambda e, n=n: e.tensor_tensor_reduce(
                    out=inv[:, :], in0=oT[:, t, :], in1=rw_rows[:, n, :], scale=1.0, scalar=0.0,
                    op0=ALU.mult, op1=ALU.add, accum_out=lg[:, t, n:n + 1]))

        def post_store(g, xln_store, x2_store):
            def s(e, b):
                g.dve.wait(e, b, g.marks["ln2", T - 1], s_go)
                e.dma_start(xln_dram[bass.ds(b, 1), :, :].rearrange("a (t p) n -> p (a t) n", p=P), oT[:, :, :]).then_inc(xln_store.sem, 16)
                e.dma_start(x2_dram[bass.ds(b, 1), :, :].rearrange("a (t p) n -> p (a t) n", p=P), x2[:, :, :]).then_inc(x2_store.sem, 16)
            g.q["sp"].append(s)
            g.marks["xln_store"] = xln_store.did()
            g.marks["x2_store"] = x2_store.did()
            def d(e, b):
                g.dve.wait(e, b, g.marks["logits"][1])
                e.tensor_tensor(logits[:, bass.ds(b * T, T), :], lg[:, :, :],
                                rb_rows[:, :].unsqueeze(1).to_broadcast([P, T, E]), ALU.add).then_inc(g.dve.sem, 1)
            g.q["dve"].append(d)
            g.dve.did()

        def load_ctx():
            def s(e, b):
                pe.wait(e, b, marks["proj_end"], s_go)
                e.dma_start(ctxT[:, :, :], ctx_t[bass.ds((b + 1) % B, 1), :, :].rearrange("a (c p) n -> p (a c) n", p=P)).then_inc(ctx_load.sem, 16)
            g.q["sp"].append(s)

        def load_x():
            def s(e, b):
                pe.wait(e, b, marks["x_turned"], s_go)
                e.dma_start(x_in[:, :, :], x[bass.ds((b + 1) % B, 1), :, :].rearrange("a (t p) n -> p (a t) n", p=P)).then_inc(x_load.sem, 16)
            g.q["sp"].append(s)
            marks["x_load"] = x_load.did()

        def load_residual():
            def s(e, b):
                x2_store.wait(e, b, marks["x2_store"], s_go)
                dve.wait(e, b, marks["ln2", T - 1], s_go)
                e.dma_start(x2[:, :, :], x[bass.ds(b, 1), :, :].rearrange("a (t p) n -> p (a t) n", p=P)).then_inc(res_load.sem, 16)
            g.q["sp"].append(s)
            m = res_load.did()
            def on_pool(e, b):
                res_load.wait(e, b, m)
                e.tensor_tensor(x2[:, :, :], x2[:, :, :], bo_rows[:, :].unsqueeze(1).to_broadcast([P, T, D]), ALU.add).then_inc(pool.sem, 1)
            g.q["pool"].append(on_pool)
            marks["x_bo"] = pool.did()

        norm_stats(g, x2, 1, lambda e, b: dve.wait_before(e, b, marks["x2", T - 1]))
        transpose_x()
        load_x()
        for t in range(T):
            post_apply(g, t, lambda e, b: pe.wait_before(e, b, marks["out_pe"]))
        halves = [(t, range(n, n + E // 2)) for t in range(T) for n in (0, E // 2)]
        for c in (0, 1):
            for work_of in (lambda: project_qk("q", c), lambda: project_qk("k", c), lambda: project_v(c)):
                work_of()
                post_logits(g, *halves.pop(0))
        while halves:
            post_logits(g, *halves.pop(0))
        post_store(g, xln_store, x2_store)
        load_residual()

        plan = {
            ("q", 2): [(row_max, 0, 0)], ("k", 2): [(row_max, 0, 1)], ("v", 2): [(row_max, 0, 2)],
            ("q", 3): [(row_max, 0, 3)], ("k", 3): [(row_max, 1, 0), (turn_max, 0)], ("v", 3): [(row_max, 1, 1)],
            (0, 0): [(row_max, 1, 2)], (0, 1): [(row_max, 1, 3)], (0, 2): [(row_max, 2, 0), (turn_max, 1)], (0, 3): [(row_max, 2, 1)],
            (1, 0): [(row_max, 2, 2)], (1, 1): [(row_max, 2, 3)], (1, 2): [(row_max, 3, 0), (turn_max, 2)], (1, 3): [(row_max, 3, 1)],
            (2, 0): [(row_max, 3, 2)], (2, 1): [(row_max, 3, 3)], (2, 2): [(turn_max, 3)],
        }

        def between(key):
            for step, *args in plan.get(key, []):
                step(*args)

        for c in (2, 3):
            project_qk("q", c); between(("q", c))
            project_qk("k", c); between(("k", c))
            project_v(c); between(("v", c))
        marks["proj_end"] = pe.per_turn
        load_ctx()
        tiles = [(c, k) for c in range(C) for k in range(T)]
        exp_scores(*tiles[0])
        for n, (c, k) in enumerate(tiles):
            if n + 1 < len(tiles):
                exp_scores(*tiles[n + 1])
            weigh_values(c, k)
            between((c, k))
            if k == T - 1:
                normalise(c)
        for t in range(T):
            project_out(t)
        norm_stats(g, x_in, 0, lambda e, b: x_load.wait(e, b, marks["x_load"]))
        for t in range(T):
            marks["ln1"] = norm_apply(g, x_in, x_in, 0, t)
        marks["ctx_next"] = ctx_load.did()
        for i in range(2):
            last_reader[i] = bank_freed[i]
        assert bank_use[0] % 2 == 0

        head = Turn(sem, "head")
        norm_stats(head, x_in, 0, lambda e, b: e.wait_ge(s_const, N_CONST))
        for t in range(T):
            norm_apply(head, x_in, x_in, 0, t)
        tail = Turn(sem, "tail")
        tail_xln, tail_x2 = Count(sem("tail_xln"), 16), Count(sem("tail_x2"), 16)
        norm_stats(tail, x2, 1, lambda e, b: None)
        for t in range(T):
            post_apply(tail, t)
            post_logits(tail, t, range(E))
        post_store(tail, tail_xln, tail_x2)

        consts = [(x_in, x[0].rearrange("(t p) n -> p t n", p=P)), (ctxT, ctx_t[0].rearrange("(c p) n -> p c n", p=P))]
        consts += [(dst, src.rearrange("(c p) n -> p c n", p=P)) for dst, src in zip((wq, wk, wv, wo), w_t)]
        consts += [(bq_col, bq), (bk_col, bk)]
        rows = [(bv_rows[:, :], bv), (bo_rows[:, :], bo), (rb_rows[:, :], router_b),
                (rw_rows[:, :, :].rearrange("p e n -> p (e n)"), router_w.rearrange("e n -> (e n)"))]
        N_CONST = 16 * (len(consts) + len(rows))

        with nc.Block() as block:
            @block.sync
            def _(e):
                for dst, src in consts:
                    e.dma_start(dst[:], src).then_inc(s_const, 16)
                for dst, src in rows:
                    e.dma_start(dst, src.partition_broadcast(P)).then_inc(s_const, 16)
                e.wait_ge(s_const, N_CONST)

            @block.gpsimd
            def _(e):
                head.pool.open(e)
                fills = [(minus_half[:, :], -0.5), (eps_col[:, :], LN_EPS), (ones[:, :], 1.0), (x2[:, :, :], 0.0)]
                fills += [(ks[c][3 * HD:P, :, :].bitcast(F32), 1.0) for c in range(C)]
                for n, (dst, value) in enumerate(fills):
                    e.memset(dst, value).then_inc(s_init, 1)
                    e.wait_ge(s_init, n + 1)
                head.run("pool", e, 0)

            @block.vector
            def _(e):
                head.dve.open(e)
                head.run("dve", e, 0)

        with nc.Block() as block:
            @block.sync
            def _(e):
                for c in (x_load, ctx_load, res_load, mrow, x2_store, xln_store, *stack):
                    c.open(e)
                with e.Fori(0, B) as b:
                    g.run("sp", e, b)
                ctx_load.wait(e, B - 1, marks["ctx_next"])
                xln_store.wait(e, B - 1, marks["xln_store"])
                x2_store.wait(e, B - 1, marks["x2_store"])

            for name, run in (("gpsimd", "pool"), ("vector", "dve"), ("scalar", "act"), ("tensor", "pe")):
                deco = {"gpsimd": block.gpsimd, "vector": block.vector, "scalar": block.scalar, "tensor": block.tensor}[name]

                @deco
                def _(e, run=run):
                    {"pool": pool, "dve": dve, "act": act, "pe": pe}[run].open(e)
                    with e.Fori(0, B) as b:
                        g.run(run, e, b)

        with nc.Block() as block:
            @block.sync
            def _(e):
                tail_xln.open(e, B)
                tail_x2.open(e, B)
                tail.run("sp", e, B)
                tail_xln.wait(e, B, tail.marks["xln_store"])
                tail_x2.wait(e, B, tail.marks["x2_store"])

            @block.vector
            def _(e):
                tail.dve.open(e, B)
                tail.run("dve", e, B)

            @block.gpsimd
            def _(e):
                tail.pool.open(e, B)
                tail.run("pool", e, B)


def routing_stage(nc, logits, skip, w12, pos, tile_expert, tile_changed, token_of, n_tiles):
    NT, E = logits.shape[1] - skip, logits.shape[2]
    KT = TOP_K * NT
    SLOTS = token_of.shape[1]
    SHIFT = P.bit_length() - 1
    TILE_SHIFT = FTOK.bit_length() - 1

    with ExitStack() as ctx:
        sb = lambda name, shape, dt=F32: ctx.enter_context(nc.sbuf_tensor(name, shape, dt))
        psum = lambda name, shape: ctx.enter_context(nc.psum_tensor(name, shape, F32))
        sem = lambda name: ctx.enter_context(nc.semaphore(name))
        g = Turn(sem, "route")

        iota_i = sb("iota_i", [P, P], I32)
        part_i = sb("part_i", [P, 1], I32)
        iota_f = sb("iota_f", [P, P])
        iota_b = sb("iota_b", [P, P], BF16)
        part_f = sb("part_f", [P, 1])
        expert_less = sb("expert_less", [P, E])
        tri = sb("tri", [P, P], BF16)
        ones_b = sb("ones_b", [P, P], BF16)
        keep = sb("keep", [P, E, NT])
        ones_e = sb("ones_e", [P, E])
        best = sb("best", [P, TOP_K, NT])
        pick = sb("pick", [P, NT])
        scratch = sb("scratch", [P, NT, E])
        masked = sb("masked", [P, NT, E])
        hot = [sb(f"hot{i}", [P, NT, E]) for i in range(TOP_K)]
        hots = sb("hots", [P, NT, E], BF16)
        expo = sb("expo", [P, NT, E])
        expo2 = sb("expo2", [P, NT])
        inv_sum = sb("inv_sum", [P, NT])
        tile_count = sb("tile_count", [P, E, NT])
        running = sb("running", [P, E, NT])
        before = sb("before", [P, E, NT])
        padded = sb("padded", [P, E])
        padded_i = sb("padded_i", [P, E], I32)
        tiles_of = sb("tiles_of", [P, E])
        tile_end = sb("tile_end", [P, E])
        start = sb("start", [P, E])
        place = sb("place", [P, NT, E])
        pos_f = sb("pos_f", [P, TOP_K, NT])
        col_i = sb("col_i", [P, KT], I32)
        row_i = sb("row_i", [P, KT], I32)
        col_b = sb("col_b", [P, KT], BF16)
        row_b = sb("row_b", [P, KT], BF16)
        col_hot = sb("col_hot", [P, KT, 2, SLOTS], BF16)
        row_hot = sb("row_hot", [P, KT, P], BF16)
        low = sb("low", [P, SLOTS])
        ended = sb("ended", [P, n_tiles, E])
        expert_f = sb("expert_f", [P, n_tiles])
        changed_f = sb("changed_f", [P, n_tiles])
        count_ps = psum("count_ps", [P, 2, NT * E])
        list_ps = psum("list_ps", [P, 2 * SLOTS])

        L = logits[:, skip:, :]
        e_of = lambda a: a.unsqueeze(2).to_broadcast([P, NT, E])
        t_of = lambda a: a.unsqueeze(1).to_broadcast([P, NT, E])
        V = lambda waits, emit: g.step("dve", waits, emit)

        p0 = g.step("pool", [], lambda e: e.iota(iota_i[:, :], [[1, P]], base=0, channel_multiplier=0))
        p1 = g.step("pool", [p0], lambda e: e.iota(part_i[:, :], [[1, 1]], base=0, channel_multiplier=1))
        p2 = g.step("pool", [p1], lambda e: e.memset(ones_b[:, :], 1.0))
        tri_on = g.step("pool", [p2], lambda e: e.affine_select(out=tri[:, :], in_=ones_b[:, :], compare_op=ALU.is_gt, fill=0.0,
                                                               base=0, pattern=[[1, P]], channel_multiplier=-1))
        p3 = g.step("pool", [tri_on], lambda e: e.memset(keep[:, :, :], 1.0))
        p4 = g.step("pool", [p3], lambda e: e.memset(keep[:, :, 0:1], 0.0))
        p5 = g.step("pool", [p4], lambda e: e.memset(ones_e[:, :], 1.0))
        f0 = V([p0], lambda e: e.tensor_copy(iota_f[:, :], iota_i[:, :]))
        f1 = V([p1], lambda e: e.tensor_copy(part_f[:, :], part_i[:, :]))
        f2 = V([f0], lambda e: e.tensor_copy(iota_b[:, :], iota_f[:, :]))
        f3 = V([f0], lambda e: e.tensor_scalar(expert_less[:, :], iota_f[:, 0:E], -float(E), None, ALU.add))

        source, last = L, f3
        for s in range(TOP_K):
            d = V([last], lambda e, s=s, source=source: e.tensor_reduce(best[:, s, :], source, AX.X, ALU.max))
            d = V([d], lambda e, s=s, source=source: e.tensor_tensor(scratch[:, :, :], source, e_of(best[:, s, :]), ALU.is_equal))
            d = V([d], lambda e: e.tensor_tensor(scratch[:, :, :], scratch[:, :, :], t_of(expert_less[:, :]), ALU.mult))
            d = V([d], lambda e: e.tensor_reduce(pick[:, :], scratch[:, :, :], AX.X, ALU.min))
            last = V([d], lambda e, s=s: e.tensor_tensor(hot[s][:, :, :], t_of(expert_less[:, :]), e_of(pick[:, :]), ALU.is_equal))
            if s == 0:
                last = V([last], lambda e: e.scalar_tensor_tensor(out=masked[:, :, :], in0=hot[0][:, :, :], scalar=-1e30, in1=L,
                                                                  op0=ALU.mult, op1=ALU.add))
                source = masked[:, :, :]
        hots_on = V([last], lambda e: e.tensor_tensor(hots[:, :, :], hot[0][:, :, :], hot[1][:, :, :], ALU.add))

        d = V([last], lambda e: e.tensor_tensor(expo[:, :, :], L, e_of(best[:, 0, :]), ALU.subtract))
        d2 = V([last], lambda e: e.tensor_tensor(expo2[:, :], best[:, 1, :], best[:, 0, :], ALU.subtract))
        a1 = g.step("act", [d], lambda e: e.activation(expo[:, :, :], expo[:, :, :], ACT.Exp))
        a2 = g.step("act", [d2], lambda e: e.activation(expo2[:, :], expo2[:, :], ACT.Exp))
        d = V([a1], lambda e: e.tensor_reduce(inv_sum[:, :], expo[:, :, :], AX.X, ALU.add))
        d = V([d], lambda e: e.reciprocal(w12[:, 0, :], inv_sum[:, :]))
        V([d, a2], lambda e: e.tensor_tensor(w12[:, 1, :], expo2[:, :], w12[:, 0, :], ALU.mult))

        flat = hots[:, :, :].rearrange("p t e -> p (t e)")
        c1 = g.step("pe", [hots_on, tri_on], lambda e: e.matmul(count_ps[:, 0, :], tri[:, :], flat, start=True, stop=True))
        c2 = g.step("pe", [], lambda e: e.matmul(count_ps[:, 1, :], ones_b[:, :], flat, start=True, stop=True))
        d = V([c2], lambda e: e.tensor_copy(tile_count[:, :, :], count_ps[:, 1, :].rearrange("p (t e) -> p e t", e=E)))
        d = V([d, p4], lambda e: e.tensor_tensor_scan(running[:, :, :].rearrange("p e t -> p (e t)"),
                                                      keep[:, :, :].rearrange("p e t -> p (e t)"),
                                                      tile_count[:, :, :].rearrange("p e t -> p (e t)"), 0.0, ALU.mult, ALU.add))
        d_run = V([d], lambda e: e.tensor_tensor(before[:, :, :], running[:, :, :], tile_count[:, :, :], ALU.subtract))
        d = V([d], lambda e: e.tensor_scalar(padded[:, :], running[:, :, NT - 1], float(FTOK - 1), None, ALU.add))
        d = V([d], lambda e: e.tensor_copy(padded_i[:, :], padded[:, :]))
        d = V([d], lambda e: e.tensor_scalar(padded_i[:, :], padded_i[:, :], TILE_SHIFT, None, ALU.arith_shift_right))
        d = V([d], lambda e: e.tensor_copy(tiles_of[:, :], padded_i[:, :]))
        d_end = V([d, p5], lambda e: e.tensor_tensor_scan(tile_end[:, :], ones_e[:, :], tiles_of[:, :], 0.0, ALU.mult, ALU.add))
        d = V([d_end], lambda e: e.tensor_tensor(start[:, :], tile_end[:, :], tiles_of[:, :], ALU.subtract))
        d = V([d], lambda e: e.tensor_scalar(start[:, :], start[:, :], float(FTOK), None, ALU.mult))
        d = V([c1, d_run], lambda e: e.tensor_tensor(place[:, :, :], count_ps[:, 0, :].rearrange("p (t e) -> p t e", e=E),
                                                     before[:, :, :].rearrange("p e t -> p t e"), ALU.add))
        d_place = V([d], lambda e: e.tensor_tensor(place[:, :, :], place[:, :, :], t_of(start[:, :]), ALU.add))
        for s in range(TOP_K):
            d = V([d_place], lambda e, s=s: e.tensor_tensor(hot[s][:, :, :], hot[s][:, :, :], place[:, :, :], ALU.mult))
            d = V([d], lambda e, s=s: e.tensor_reduce(pos_f[:, s, :], hot[s][:, :, :], AX.X, ALU.add))
        d_pos = V([d], lambda e: e.tensor_copy(pos[:, :, :], pos_f[:, :, :]))

        d = V([d_end], lambda e: e.tensor_tensor(ended[:, :, :], iota_f[:, 0:n_tiles].unsqueeze(2).to_broadcast([P, n_tiles, E]),
                                                 tile_end[:, :].unsqueeze(1).to_broadcast([P, n_tiles, E]), ALU.is_ge))
        d = V([d], lambda e: e.tensor_reduce(expert_f[:, :], ended[:, :, :], AX.X, ALU.add))
        d_exp = V([d], lambda e: e.tensor_scalar(expert_f[:, :], expert_f[:, :], float(E - 1), None, ALU.min))
        V([d_exp], lambda e: e.tensor_copy(tile_expert[0:1, :], expert_f[0:1, :]))
        d = V([], lambda e: e.memset(changed_f[:, 0:2], 1.0))
        d = V([d, d_exp], lambda e: e.tensor_tensor(changed_f[:, 2:], expert_f[:, 2:], expert_f[:, :-2], ALU.not_equal))
        V([d], lambda e: e.tensor_copy(tile_changed[0:1, :], changed_f[0:1, :]))

        flat_pos = pos[:, :, :].rearrange("p s t -> p (s t)")
        d = V([d_pos], lambda e: e.tensor_scalar(col_i[:, :], flat_pos, SHIFT, None, ALU.arith_shift_right))
        d2 = V([d_pos], lambda e: e.tensor_scalar(row_i[:, :], flat_pos, P - 1, None, ALU.bitwise_and))
        d = V([d], lambda e: e.tensor_copy(col_b[:, :], col_i[:, :]))
        d2 = V([d2], lambda e: e.tensor_copy(row_b[:, :], row_i[:, :]))
        d_row = V([d2, f2], lambda e: e.tensor_tensor(row_hot[:, :, :], iota_b[:, :].unsqueeze(1).to_broadcast([P, KT, P]),
                                                      row_b[:, :].unsqueeze(2).to_broadcast([P, KT, P]), ALU.is_equal))
        d = V([d], lambda e: e.tensor_tensor(col_hot[:, :, 1, :], iota_b[:, 0:SLOTS].unsqueeze(1).to_broadcast([P, KT, SLOTS]),
                                             col_b[:, :].unsqueeze(2).to_broadcast([P, KT, SLOTS]), ALU.is_equal))
        for s in range(TOP_K):
            cols = slice(s * NT, (s + 1) * NT)
            d3 = V([d, f2], lambda e, cols=cols: e.tensor_tensor(
                col_hot[:, cols, 0, :], col_hot[:, cols, 1, :],
                iota_b[:, 0:NT].unsqueeze(2).to_broadcast([P, NT, SLOTS]), ALU.mult))
        d4 = V([d3, f1], lambda e: e.tensor_scalar(col_hot[:, :, 1, :], col_hot[:, :, 1, :], part_f[:, 0:1], None, ALU.mult))
        for n in range(KT):
            c = g.step("pe", [d_row, d4] if n == 0 else [], lambda e, n=n: e.matmul(
                list_ps[:, :], row_hot[:, n, :], col_hot[:, n, :, :].rearrange("p a c -> p (a c)"), start=(n == 0), stop=(n == KT - 1)))
        d = V([c], lambda e: e.tensor_scalar(low[:, :], list_ps[:, SLOTS:], float(skip * P), None, ALU.add))
        V([d], lambda e: e.scalar_tensor_tensor(out=token_of[:, :], in0=list_ps[:, 0:SLOTS], scalar=float(P), in1=low[:, :],
                                                op0=ALU.mult, op1=ALU.add))

        with nc.Block() as block:
            for name in ("pool", "dve", "act", "pe"):
                deco = {"pool": block.gpsimd, "dve": block.vector, "act": block.scalar, "pe": block.tensor}[name]

                @deco
                def _(e, name=name):
                    g.count[name].open(e)
                    g.run(name, e, 0)


def expert_stage(nc, xln_dram, y_dram, w_gate_up, w_down, b_gate_up, b_down, tile_expert, tile_changed, token_of, ident, n_tiles, s_go):
    E, D, F2 = w_gate_up.shape
    F = F2 // 2
    KD, KF = D // P, F // P
    SUB = FTOK // P
    rows = xln_dram.rearrange("b s d -> (b s) d")

    with ExitStack() as ctx:
        sb = lambda name, shape, dt=F32: ctx.enter_context(nc.sbuf_tensor(name, shape, dt))
        psum = lambda name, shape: ctx.enter_context(nc.psum_tensor(name, shape, F32))
        sem = lambda name: ctx.enter_context(nc.semaphore(name))
        g = Turn(sem, "ffn")
        pe, act, dve, pool, marks = g.pe, g.act, g.dve, g.pool, g.marks
        w_load = [Count(sem(f"s_w{s}"), 16) for s in range(2)]
        gather = [Count(sem(f"s_gather{s}"), 16, ahead=0) for s in range(2)]
        store = [Count(sem(f"s_y{s}"), 16) for s in range(2)]

        wg = [sb(f"wg{s}", [P, KD, F2]) for s in range(2)]
        wd = [sb(f"wd{s}", [P, KF, D]) for s in range(2)]
        bg = [sb(f"bg{s}", [P, F2 // P]) for s in range(2)]
        bd = [sb(f"bd{s}", [P, D]) for s in range(2)]
        bu1 = [sb(f"bu1{s}", [P, KF]) for s in range(2)]
        idx = [sb(f"idx{s}", [P, SUB], I32) for s in range(2)]
        xg = [sb(f"xg{s}", [P, SUB, D]) for s in range(2)]
        xgT = [sb(f"xgT{s}", [P, KD, FTOK]) for s in range(2)]
        gate = [sb(f"gate{i}", [P, FTOK]) for i in range(2)]
        sig = [sb(f"sig{i}", [P, FTOK]) for i in range(2)]
        up = [sb(f"up{i}", [P, FTOK]) for i in range(2)]
        hid = [sb(f"hid{s}", [P, KF, FTOK]) for s in range(2)]
        y = [sb(f"y{s}", [P, SUB, D]) for s in range(2)]
        t_ps = [psum(f"t_ps{i}", [P, 2, FTOK]) for i in range(KD // 2)]
        gu_ps = [psum(f"gu_ps{i}", [P, 2, FTOK]) for i in range(2)]
        d_ps = [psum(f"d_ps{i}", [P, D]) for i in range(2)]

        def fetch(s):
            def copy(e, b):
                pe.wait_before(e, b, marks["turned", s])
                e.tensor_copy(idx[s][:, :], token_of[:, bass.ds(b * (2 * SUB) + s * SUB, SUB)]).then_inc(pool.sem, 1)
            g.q["pool"].append(copy)
            m = pool.did()
            def rows_in(e, b):
                pool.wait(e, b, m, s_go)
                for i in range(SUB):
                    e.indirect_dma_start(out=xg[s][:, i, :], out_offset=None, in_=rows,
                                         in_offset=bass.IndirectOffsetOnAxis(ap=idx[s][:, i:i + 1].bitcast(U32), axis=0)).then_inc(gather[s].sem, 16)
            g.q["pool"].append(rows_in)
            for _ in range(SUB):
                marks["gather", s] = gather[s].did()

        def issue_weights(e, s, tile):
            expert = e.value_load(tile_expert[0:1, tile], min_val=0, max_val=E - 1)
            changed = e.value_load(tile_changed[0:1, tile], min_val=0, max_val=1)
            for dst, src in ((wg[s][:, :, :], w_gate_up[bass.ds(expert, 1), :, :].rearrange("a (k p) f -> p (a k) f", p=P)),
                             (wd[s][:, :, :], w_down[bass.ds(expert, 1), :, :].rearrange("a (k p) f -> p (a k) f", p=P)),
                             (bg[s][:, :], b_gate_up[bass.ds(expert, 1), :, :].rearrange("a p c -> p (a c)")),
                             (bd[s][:, :], b_down[bass.ds(expert, 1), :].to_broadcast([P, D]))):
                e.dma_start(dst, src, cond=changed).then_inc(w_load[s].sem, 16)

        def load_weights(s, ahead):
            def f(e, b):
                before = (lambda c, m: c.wait(e, b, m, s_go)) if ahead else (lambda c, m: c.wait_before(e, b, m, s_go))
                before(pe, marks["down", s])
                before(dve, marks["y", s])
                issue_weights(e, s, bass.ds((b + ahead) * 2 + s, 1))
            g.q["sp"].append(f)
            for _ in range(4):
                marks["w", s] = w_load[s].did()

        def weights_in(e, b, s):
            (w_load[s].wait if s else w_load[s].wait_before)(e, b, marks["w", s])

        def turn_rows(s):
            for half in range(KD // 2):
                def f(e, b, half=half):
                    gather[s].wait(e, b, marks["gather", s])
                    if s:
                        act.wait(e, b, marks["xgT", 0, half])
                    else:
                        act.wait_before(e, b, marks["xgT", 1, half])
                    for k in range(2):
                        for i in range(SUB):
                            c = 2 * half + k
                            ins = e.transpose(t_ps[half][:, k, i * P:(i + 1) * P], xg[s][:, i, c * P:(c + 1) * P], ident[:, :])
                    ins.then_inc(pe.sem, 1)
                g.q["pe"].append(f)
                done = marks["turned", s] = pe.did()
                def a(e, b, half=half, done=done):
                    pe.wait(e, b, done)
                    e.activation(xgT[s][:, 2 * half:2 * half + 2, :], t_ps[half][:, :, :], ACT.Copy).then_inc(act.sem, 1)
                g.q["act"].append(a)
                marks["xgT", s, half] = act.did()

        def gate_up(s):
            def plus_one(e, b):
                weights_in(e, b, s)
                e.tensor_scalar(bu1[s][:, :], bg[s][:, KF:], 1.0, None, ALU.add).then_inc(dve.sem, 1)
            g.q["dve"].append(plus_one)
            bu1_on = dve.did()
            for f in range(KF):
                i = f % 2
                n = s * KF + f
                def p(e, b, f=f, i=i, n=n):
                    if f == 0:
                        weights_in(e, b, s)
                        act.wait(e, b, marks["xgT", s, KD // 2 - 1])
                    if n >= 2:
                        dve.wait(e, b, marks["up", n - 2])
                    else:
                        dve.wait_before(e, b, marks["up", n - 2 + 2 * KF])
                    for part in range(2):
                        for k in range(KD):
                            cols = slice(part * F + f * P, part * F + (f + 1) * P)
                            ins = e.matmul(gu_ps[i][:, part, :], wg[s][:, k, cols], xgT[s][:, k, :], start=(k == 0), stop=(k == KD - 1))
                    ins.then_inc(pe.sem, 1)
                g.q["pe"].append(p)
                made = (pe, pe.did())
                def clip_gate(e, b, i=i, f=f, n=n, made=made):
                    made[0].wait(e, b, made[1])
                    if n >= 2:
                        dve.wait(e, b, marks["hid_of", n - 2])
                    else:
                        dve.wait_before(e, b, marks["hid_of", n - 2 + 2 * KF])
                    e.tensor_scalar(gate[i][:, :], gu_ps[i][:, 0, :], bg[s][:, f:f + 1], LIMIT, ALU.add, ALU.min).then_inc(dve.sem, 1)
                g.q["dve"].append(clip_gate)
                g1 = (dve, dve.did())
                s1 = g.step("act", [g1], lambda e, i=i: e.activation(sig[i][:, :], gate[i][:, :], ACT.Sigmoid, scale=ALPHA))
                u1 = g.step("dve", [made, (dve, bu1_on)], lambda e, i=i, f=f: e.tensor_scalar(
                    up[i][:, :], gu_ps[i][:, 1, :], bu1[s][:, f:f + 1], LIMIT + 1.0, ALU.add, ALU.min))
                marks["up", n] = u1[1]
                if f:
                    glu(s, f - 1, *pending)
                pending = (s1, u1)
            glu(s, KF - 1, *pending)

        def glu(s, f, s1, u1):
            i = f % 2
            g2 = g.step("dve", [s1], lambda e: e.tensor_tensor(gate[i][:, :], gate[i][:, :], sig[i][:, :], ALU.mult))
            def h(e, b):
                pe.wait_before(e, b, marks["down", s])
                dve.wait(e, b, g2[1])
                e.scalar_tensor_tensor(out=hid[s][:, f, :], in0=up[i][:, :], scalar=1.0 - LIMIT, in1=gate[i][:, :],
                                       op0=ALU.max, op1=ALU.mult).then_inc(dve.sem, 1)
            g.q["dve"].append(h)
            marks["hid", s] = marks["hid_of", s * KF + f] = dve.did()

        def down(s):
            for i in range(SUB):
                def p(e, b, i=i):
                    dve.wait(e, b, marks["hid", s])
                    if s:
                        dve.wait(e, b, marks["y", 0, i])
                    else:
                        dve.wait_before(e, b, marks["y", 1, i])
                    for k in range(KF):
                        ins = e.matmul(d_ps[i][:, :], hid[s][:, k, i * P:(i + 1) * P], wd[s][:, k, :], start=(k == 0), stop=(k == KF - 1))
                    ins.then_inc(pe.sem, 1)
                g.q["pe"].append(p)
                done = marks["down", s] = pe.did()
                def d(e, b, i=i, done=done):
                    pe.wait(e, b, done)
                    store[s].wait_before(e, b, marks["store", s])
                    e.tensor_tensor(y[s][:, i, :], d_ps[i][:, :], bd[s][:, :], ALU.add).then_inc(dve.sem, 1)
                g.q["dve"].append(d)
                marks["y", s, i] = marks["y", s] = dve.did()

        def store_rows(s):
            def f(e, b):
                dve.wait(e, b, marks["y", s], s_go)
                e.dma_start(y_dram[bass.ds(b * 2 + s, 1), :, :].rearrange("a (i p) n -> p (a i) n", p=P), y[s][:, :, :]).then_inc(store[s].sem, 16)
            g.q["act" if s else "sp"].append(f)
            marks["store", s] = store[s].did()

        fetch(0)
        fetch(1)
        turn_rows(0)
        load_weights(1, 0)
        gate_up(0)
        turn_rows(1)
        down(0)
        store_rows(0)
        first_tile = {n: len(g.q[n]) for n in g.q}
        load_weights(0, 1)
        gate_up(1)
        down(1)
        store_rows(1)
        pairs = n_tiles // 2
        odd = n_tiles % 2
        assert odd

        with nc.Block() as block:
            @block.sync
            def _(e):
                for c in (w_load[1], *store):
                    c.open(e)
                issue_weights(e, 0, slice(0, 1))
                with e.Fori(0, pairs) as b:
                    g.run("sp", e, b)
                g.q["sp"][1](e, pairs)
                store[0].wait(e, pairs, marks["store", 0])
                store[1].wait(e, pairs - 1, marks["store", 1])

            for name in ("pool", "dve", "act", "pe"):
                deco = {"pool": block.gpsimd, "dve": block.vector, "act": block.scalar, "pe": block.tensor}[name]

                @deco
                def _(e, name=name):
                    g.count[name].open(e)
                    with e.Fori(0, pairs) as b:
                        g.run(name, e, b)
                    for f in g.q[name][:first_tile[name]]:
                        f(e, pairs)


def combine_stage(nc, x2_dram, y_dram, out, w12, pos, s_go):
    _, S, D = x2_dram.shape
    B = out.shape[0]
    T = S // P
    y_rows = y_dram.rearrange("a b d -> (a b) d")
    TT = 2 * T

    with ExitStack() as ctx:
        sb = lambda name, shape, dt=F32: ctx.enter_context(nc.sbuf_tensor(name, shape, dt))
        sem = lambda name: ctx.enter_context(nc.semaphore(name))
        g = Turn(sem, "mix")
        dve, pool, marks = g.dve, g.pool, g.marks
        res = [sb(f"res{i}", [P, T, D]) for i in range(2)]
        ya = sb("ya", [P, TOP_K, TT, D])
        idx = sb("idx", [P, TOP_K, TT], I32)
        w = sb("w", [P, TOP_K, TT])
        load = [Count(sem(f"s_res{i}"), 16) for i in range(2)]
        store = [Count(sem(f"s_out{i}"), 16) for i in range(2)]
        gathered = [Count(sem(f"s_ya{t}"), 16, ahead=0) for t in range(TT)]

        def copies():
            def f(e, b):
                dve.wait_before(e, b, marks["mixed", TT - 1])
                e.tensor_copy(w[:, :, :], w12[:, :, bass.ds(b * TT, TT)]).then_inc(pool.sem, 1)
                e.tensor_copy(idx[:, :, :], pos[:, :, bass.ds(b * TT, TT)]).then_inc(pool.sem, 1)
            g.q["pool"].append(f)
            marks["w"] = pool.did()
            marks["idx"] = pool.did()

        def gather(t):
            def f(e, b):
                if t == 0:
                    pool.wait(e, b, marks["idx"])
                dve.wait_before(e, b, marks["mixed", t], s_go)
                for s in range(TOP_K):
                    e.indirect_dma_start(out=ya[:, s, t, :], out_offset=None, in_=y_rows,
                                         in_offset=bass.IndirectOffsetOnAxis(ap=idx[:, s, t:t + 1].bitcast(U32), axis=0)).then_inc(gathered[t].sem, 16)
            g.q["pool"].append(f)
            for _ in range(TOP_K):
                marks["ya", t] = gathered[t].did()

        def load_residual(i):
            def f(e, b):
                store[i].wait_before(e, b, marks["store", i], s_go)
                e.dma_start(res[i][:, :, :], x2_dram[bass.ds(b * 2 + (i + 1), 1), :, :].rearrange("a (t p) n -> p (a t) n", p=P)).then_inc(load[i].sem, 16)
            g.q["sp"].append(f)
            marks["load", i] = load[i].did()

        def mix(t):
            i = t // T
            def f(e, b):
                load[i].wait(e, b, marks["load", i])
                gathered[t].wait(e, b, marks["ya", t])
                pool.wait(e, b, marks["w"])
                e.scalar_tensor_tensor(out=res[i][:, t % T, :], in0=ya[:, 0, t, :], scalar=w[:, 0, t:t + 1],
                                       in1=res[i][:, t % T, :], op0=ALU.mult, op1=ALU.add).then_inc(dve.sem, 1)
            g.q["dve"].append(f)
            m = (dve, dve.did())
            marks["mixed", t] = g.step("dve", [m], lambda e: e.scalar_tensor_tensor(
                out=res[i][:, t % T, :], in0=ya[:, 1, t, :], scalar=w[:, 1, t:t + 1],
                in1=res[i][:, t % T, :], op0=ALU.mult, op1=ALU.add))[1]

        def store_out(i):
            def f(e, b):
                dve.wait(e, b, marks["mixed", (i + 1) * T - 1], s_go)
                e.dma_start(out[bass.ds(b * 2 + i, 1), :, :].rearrange("a (t p) n -> p (a t) n", p=P), res[i][:, :, :]).then_inc(store[i].sem, 16)
            g.q["sp"].append(f)
            marks["store", i] = store[i].did()

        copies()
        load_residual(0)
        load_residual(1)
        for t in range(TT):
            gather(t)
            mix(t)
        store_out(0)
        store_out(1)

        with nc.Block() as block:
            @block.sync
            def _(e):
                for c in (*load, *store):
                    c.open(e)
                with e.Fori(0, B // 2) as b:
                    g.run("sp", e, b)
                for i in range(2):
                    store[i].wait(e, B // 2 - 1, marks["store", i])

            @block.gpsimd
            def _(e):
                pool.open(e)
                with e.Fori(0, B // 2) as b:
                    g.run("pool", e, b)

            @block.vector
            def _(e):
                dve.open(e)
                with e.Fori(0, B // 2) as b:
                    g.run("dve", e, b)


def build(nc, x, ctx_t, wq_t, bq, wk_t, bk, wv_t, bv, wo_t, bo, router_w, router_b, w_gate_up, b_gate_up, w_down, b_down, out):
    B, S, D = x.shape
    E = router_w.shape[0]
    T = S // P
    NT = B * T
    n_tiles = (TOP_K * B * S - E) // FTOK + E
    slots = -(-n_tiles // 2) * 2 * (FTOK // P)
    x2_dram = nc.dram_tensor("x2_dram", (B + 1, S, D), F32, kind="Internal").ap()
    xln_dram = nc.dram_tensor("xln_dram", (B + 1, S, D), F32, kind="Internal").ap()
    y_dram = nc.dram_tensor("y_dram", (n_tiles, FTOK, D), F32, kind="Internal").ap()

    with ExitStack() as ctx:
        sb = lambda name, shape, dt=F32: ctx.enter_context(nc.sbuf_tensor(name, shape, dt))
        logits = sb("logits", [P, NT + T, E])
        ident = sb("ident", [P, P])
        w12 = sb("w12", [P, TOP_K, NT])
        pos = sb("pos", [P, TOP_K, NT], I32)
        tile_expert = sb("tile_expert", [1, n_tiles], I32)
        tile_changed = sb("tile_changed", [1, n_tiles], I32)
        token_of = sb("token_of", [P, slots], I32)
        s_ident = ctx.enter_context(nc.semaphore("s_ident"))
        s_go = ctx.enter_context(nc.semaphore("s_go"))

        with nc.Block() as block:
            @block.gpsimd
            def _(e):
                e.memset(ident[:, :], 0.0).then_inc(s_ident, 1)
                e.wait_ge(s_ident, 1)
                e.affine_select(out=ident[:, :], in_=ident[:, :], compare_op=ALU.not_equal, fill=1.0,
                                base=0, pattern=[[-1, P]], channel_multiplier=1).then_inc(s_ident, 1)
                e.wait_ge(s_ident, 2)
                e.sem_inc(s_go, 1)

        attention_stage(nc, x, ctx_t, (wq_t, wk_t, wv_t, wo_t), bq, bk, bv, bo, router_w, router_b, x2_dram, xln_dram, logits, ident, s_go)
        routing_stage(nc, logits, T, w12, pos, tile_expert, tile_changed, token_of, n_tiles)
        expert_stage(nc, xln_dram, y_dram, w_gate_up, w_down, b_gate_up, b_down, tile_expert, tile_changed, token_of, ident, n_tiles, s_go)
        combine_stage(nc, x2_dram, y_dram, out, w12, pos, s_go)


_INS = ["x", "ctx_t", "wq_t", "bq", "wk_t", "bk", "wv_t", "bv", "wo_t", "bo", "router_w", "router_b",
        "w_gate_up", "b_gate_up", "w_down", "b_down"]


def kernel(**i):
    import numpy as np
    import concourse.bacc as bacc
    from concourse.bass_utils import run_bass_kernel_spmd

    lay = np.ascontiguousarray
    a = {k: np.asarray(v) for k, v in i.items()}
    column = lambda v: lay(v.reshape(-1, P).T)
    gub = a["L0_ffn_gate_up_bias"]
    arrays = {
        "x": lay(a["x"]),
        "ctx_t": lay(a["ctx_1024"].transpose(0, 2, 1)),
        "wq_t": lay(a["L0_xattn_Wq"].T), "wk_t": lay(a["L0_xattn_Wk"].T),
        "wv_t": lay(a["L0_xattn_Wv"].T), "wo_t": lay(a["L0_xattn_Wo"].T),
        "bq": column(a["L0_xattn_bq"]), "bk": column(a["L0_xattn_bk"]),
        "bv": lay(a["L0_xattn_bv"]), "bo": lay(a["L0_xattn_bo"]),
        "router_w": lay(a["L0_ffn_router_weight"]), "router_b": lay(a["L0_ffn_router_bias"]),
        "w_gate_up": lay(a["L0_ffn_gate_up_proj"]),
        "b_gate_up": lay(gub.reshape(gub.shape[0], -1, P).transpose(0, 2, 1)),
        "w_down": lay(a["L0_ffn_down_proj"]), "b_down": lay(a["L0_ffn_down_bias"]),
    }
    nc = bacc.Bacc("TRN2", target_bir_lowering=False, num_devices=1)
    args = [nc.dram_tensor(n, arrays[n].shape, mybir.dt.from_np(arrays[n].dtype), kind="ExternalInput").ap() for n in _INS]
    out = nc.dram_tensor("out", arrays["x"].shape, F32, kind="ExternalOutput").ap()
    build(nc, *args, out)
    r = run_bass_kernel_spmd(nc, [arrays], core_ids=[0])
    return r.results[0]["out"]
```

```python
from contextlib import ExitStack

import concourse.bass as bass
from concourse import mybir

ALU = mybir.AluOpType
ACT = mybir.ActivationFunctionType
AX = mybir.AxisListType
F32 = mybir.dt.float32
F32R = mybir.dt.float32r
BF16 = mybir.dt.bfloat16
I32 = mybir.dt.int32
U32 = mybir.dt.uint32

P = 128
LN_EPS = 1e-5
HEADS = 16
GROUP = 4
HD = 32
TOP_K = 2
ALPHA = 1.702
LIMIT = 7.0
FTOK = 256


class Count:

    def __init__(self, sem, step=1, ahead=1):
        self.sem, self.step, self.per_turn, self.ahead = sem, step, 0, ahead

    def did(self):
        self.per_turn += self.step
        return self.per_turn

    def open(self, eng, first_turn=0):
        eng.sem_inc(self.sem, (first_turn + 1) * self.per_turn)

    def wait(self, eng, turn, mark, go=None):
        self._wait(eng, turn * self.per_turn + (self.ahead * self.per_turn + mark), go)

    def wait_before(self, eng, turn, mark, go=None):
        self._wait(eng, turn * self.per_turn + mark, go)

    def _wait(self, eng, value, go):
        if go is not None:
            value = value if isinstance(value, int) else eng.to_reg(value)
            eng.wait_ge(go, 1)
        eng.wait_ge(self.sem, value)


class Turn:

    def __init__(self, sem, tag):
        self.q = {n: [] for n in ("sp", "act", "dve", "pe", "pool")}
        self.count = {n: Count(sem(f"{tag}_{n}")) for n in ("act", "dve", "pe", "pool")}
        self.act, self.dve, self.pe, self.pool = self.count.values()
        self.marks = {}

    def step(self, engine, waits, emit, go=None):
        count = self.count[engine]

        def f(e, turn):
            for c, m in waits:
                c.wait(e, turn, m, go)
            emit(e).then_inc(count.sem, 1)
        self.q[engine].append(f)
        return count, count.did()

    def run(self, engine, eng, turn):
        for f in self.q[engine]:
            f(eng, turn)


def attention_stage(nc, x, ctx_t, w_t, bq, bk, bv, bo, router_w, router_b, x2_dram, xln_dram, logits, ident, s_go):
    B, S, D = x.shape
    C = D // P
    T = S // P
    E = router_w.shape[0]
    scale = 1.0 / float(HD) ** 0.5

    with ExitStack() as ctx:
        sb = lambda name, shape, dt=F32: ctx.enter_context(nc.sbuf_tensor(name, shape, dt))
        psum = lambda name, shape: ctx.enter_context(nc.psum_tensor(name, shape, F32))
        sem = lambda name: ctx.enter_context(nc.semaphore(name))

        wq, wk, wv, wo = (sb(n, [P, C, D]) for n in ("wq", "wk", "wv", "wo"))
        rw_rows = sb("rw_rows", [P, E, D])
        rb_rows = sb("rb_rows", [P, E])
        bv_rows = sb("bv_rows", [P, D])
        bo_rows = sb("bo_rows", [P, D])
        bq_col = sb("bq_col", [P, C])
        bk_col = sb("bk_col", [P, C])
        x_in = sb("x_in", [P, T, D])
        x2 = sb("x2", [P, T, D])
        ctxT = sb("ctxT", [P, C, S])
        xT = sb("xT", [P, C, S])
        hi = {n: [sb(f"{n}_hi{i}", [P, S], F32R) for i in range(2)] for n in "qk"}
        lo = {n: [sb(f"{n}_lo{i}", [P, S], F32R) for i in range(2)] for n in "qk"}
        qs = [sb(f"qs{c}", [P, GROUP, S], F32R) for c in range(C)]
        ks = [sb(f"ks{c}", [P, GROUP, S], F32R) for c in range(C)]
        v = sb("v", [P, T, D])
        pt = [sb(f"pt{i}", [P, GROUP, S]) for i in range(2)]
        oT = sb("oT", [P, C, S])
        o_sum = sb("o_sum", [P, 2, S])
        products = sb("products", [P, D])
        ones = sb("ones", [P, HD])
        negmax = sb("negmax", [P, C, GROUP * T])
        m_hi = sb("m_hi", [GROUP * T, P], F32R)
        m_lo = sb("m_lo", [GROUP * T, P], F32R)
        stats = sb("stats", [P, 2, T, 6])
        mv = sb("mv", [P, 2, T, 2])
        var_eps = sb("var_eps", [P, 2, T])
        rstd = sb("rstd", [P, 2, T])
        minus_half = sb("minus_half", [P, T])
        eps_col = sb("eps_col", [P, T])
        lg = sb("lg", [P, T, E])

        work = [psum(f"work{i}", [P, S]) for i in range(2)]
        st = [psum(f"st{i}", [P, 2, S]) for i in range(2)]
        o_ps = psum("o_ps", [P, S])
        sum_ps = psum("sum_ps", [P, S])

        s_const = sem("s_const")
        s_init = sem("s_init")
        g = Turn(sem, "att")
        pe, act, dve, pool = g.pe, g.act, g.dve, g.pool
        x_load, ctx_load, res_load = (Count(sem(n), 16) for n in ("s_x", "s_ctx", "s_res"))
        stack = [Count(sem(f"s_stack{c}"), 16) for c in range(C)]
        mrow = [Count(sem(f"s_mrow{c}"), 16, ahead=0) for c in range(C)]
        x2_store, xln_store = Count(sem("s_x2"), 16), Count(sem("s_xln"), 16)

        marks = g.marks
        last_used = {"work": 1, "st": 1}
        last_reader = {}

        def take(ring, i=None):
            i = 1 - last_used[ring] if i is None else i
            last_used[ring] = i
            key = (ring, i)
            if key in last_reader:
                g.q["pe"].append(lambda e, b, f=last_reader[key]: f[0].wait(e, b, f[1]))
            else:
                g.q["pe"].append(lambda e, b: last_reader[key][0].wait_before(e, b, last_reader[key][1]))
            return i

        def take_bank():
            return take("work")

        def free_bank(i, count, mark):
            last_reader["work", i] = (count, mark)

        light = []

        def gap(n=1):
            for _ in range(n):
                if light:
                    step, *args = light.pop(0)
                    step(*args)

        def norm_stats(g, src, slot, t, first_wait=None):
            def f(e, b):
                if first_wait:
                    first_wait(e, b)
                e.bn_stats(stats[:, slot, t, :], src[:, t, :]).then_inc(g.dve.sem, 1)
            g.q["dve"].append(f)
            g.marks["bn", slot, t] = g.dve.did()

        def norm_rstd(g, slot):
            for t in range(T):
                g.marks["mv", slot] = g.step("dve", [(g.dve, g.marks["bn", slot, t])],
                                             lambda e, t=t: e.bn_aggr(mv[:, slot, t, :], stats[:, slot, t, :]), s_go)
            r = g.step("pool", [g.marks["mv", slot]],
                       lambda e: e.tensor_tensor(var_eps[:, slot, :], mv[:, slot, :, 1], eps_col[:, :], ALU.add))
            g.marks["rstd", slot] = g.step("pool", [r], lambda e: e.tensor_tensor(rstd[:, slot, :], var_eps[:, slot, :],
                                                                                 minus_half[:, :], ALU.pow))

        def norm_apply(g, dst, src, slot, t, first_wait):
            def f(e, b):
                first_wait(e, b)
                e.tensor_scalar(dst[:, t, :], src[:, t, :], mv[:, slot, t, 0:1], rstd[:, slot, t:t + 1],
                                ALU.subtract, ALU.mult).then_inc(g.dve.sem, 1)
            g.q["dve"].append(f)
            return g.dve.did()

        def transpose_x():
            for c in range(C):
                i = take_bank()
                def f(e, b, c=c, i=i):
                    dve.wait_before(e, b, marks["ln1"])
                    for t in range(T):
                        ins = e.transpose(work[i][:, t * P:(t + 1) * P], x_in[:, t, c * P:(c + 1) * P], ident[:, :])
                    ins.then_inc(pe.sem, 1)
                g.q["pe"].append(f)
                done = pe.did()
                def on_act(e, b, c=c, i=i, done=done):
                    pe.wait(e, b, done)
                    e.activation(xT[:, c, :], work[i][:, :], ACT.Identity).then_inc(act.sem, 1)
                g.q["act"].append(on_act)
                free_bank(i, act, act.did())
            marks["x_turned"] = done
            marks["xT"] = act.per_turn

        def project_qk(name, c):
            w, src, bias = (wq, xT, bq_col) if name == "q" else (wk, ctxT, bk_col)
            i = take_bank()
            for k in range(C):
                def f(e, b, k=k):
                    if k == 0 and name == "q":
                        act.wait(e, b, marks["xT"])
                    elif k == 0:
                        ctx_load.wait_before(e, b, marks["ctx_next"])
                    ins = e.matmul(work[i][:, :], w[:, k, c * P:(c + 1) * P], src[:, k, :], start=(k == 0), stop=(k == C - 1))
                    if k == C - 1:
                        ins.then_inc(pe.sem, 1)
                g.q["pe"].append(f)
                if k < C - 1:
                    gap()
            done = pe.did()
            h, l = hi[name][c % 2], lo[name][c % 2]
            def on_act(e, b):
                pe.wait(e, b, done)
                if c >= 2:
                    stack[c - 2].wait(e, b, marks["stack", c - 2])
                else:
                    stack[c + 2].wait_before(e, b, marks["stack", c + 2])
                e.activation(h[:, :], work[i][:, :], ACT.Identity, bias=bias[:, c:c + 1]).then_inc(act.sem, 1)
            g.q["act"].append(on_act)
            h_done = act.did()
            def d(e, b):
                act.wait(e, b, h_done)
                e.scalar_tensor_tensor(out=l[:, :], in0=work[i][:, :], scalar=bias[:, c:c + 1], in1=h[:, :].bitcast(F32),
                                       op0=ALU.add, op1=ALU.subtract).then_inc(dve.sem, 1)
            g.q["dve"].append(d)
            l_done = dve.did()
            free_bank(i, dve, l_done)
            dst = qs[c] if name == "q" else ks[c]
            parts = ((0, h), (1, h), (2, l)) if name == "q" else ((0, h), (2, h), (1, l))
            def s(e, b):
                act.wait(e, b, h_done, s_go)
                pe.wait_before(e, b, marks["c_end", c], s_go)
                for g3, src in parts:
                    if src is l:
                        dve.wait(e, b, l_done, s_go)
                    for r in range(GROUP):
                        e.dma_start(dst[HD * g3:HD * (g3 + 1), r, :].bitcast(F32),
                                    src[HD * r:HD * (r + 1), :].bitcast(F32)).then_inc(stack[c].sem, 16)
            g.q["sp"].append(s)
            gap()
            for _ in range(3 * GROUP):
                marks["stack", c] = stack[c].did()

        def project_v(c):
            i = take_bank()
            for t in range(T):
                def f(e, b, t=t):
                    if t == 0:
                        ctx_load.wait_before(e, b, marks["ctx_next"])
                    for k in range(C):
                        ins = e.matmul(work[i][:, t * P:(t + 1) * P], ctxT[:, k, t * P:(t + 1) * P],
                                       wv[:, k, c * P:(c + 1) * P], start=(k == 0), stop=(k == C - 1))
                    if t == T - 1:
                        ins.then_inc(pe.sem, 1)
                g.q["pe"].append(f)
                if t < T - 1:
                    gap()
            done = pe.did()
            def d(e, b):
                pe.wait(e, b, done)
                e.tensor_tensor(v[:, :, c * P:(c + 1) * P], work[i][:, :].rearrange("p (t n) -> p t n", t=T),
                                bv_rows[:, c * P:(c + 1) * P].unsqueeze(1).to_broadcast([P, T, P]), ALU.add).then_inc(dve.sem, 1)
            g.q["dve"].append(d)
            marks["v", c] = dve.did()
            free_bank(i, dve, marks["v", c])
            gap()

        def row_max(c, h, t, n=1):
            i = take("st") if n == 2 else take("work")
            bank = st[i] if n == 2 else work[i][:, :].unsqueeze(1)
            def f(e, b):
                stack[c].wait(e, b, marks["stack", c])
                for j in range(n):
                    ins = e.matmul(bank[:, j, :], qs[c][0:3 * HD, h, (t + j) * P:(t + j + 1) * P], ks[c][0:3 * HD, h, :],
                                   start=True, stop=True)
                ins.then_inc(pe.sem, 1)
            g.q["pe"].append(f)
            done = pe.did()
            def d(e, b):
                pe.wait(e, b, done)
                e.tensor_reduce(negmax[:, c, h * T + t:h * T + t + n], bank[:, 0:n, :], AX.X, ALU.max,
                                negate=True).then_inc(dve.sem, 1)
            g.q["dve"].append(d)
            marks["max", c] = dve.did()
            last_reader["st" if n == 2 else "work", i] = (dve, marks["max", c])
            piece()

        def turn_max(c):
            i = take_bank()
            R = GROUP * T
            def f(e, b):
                dve.wait(e, b, marks["max", c])
                e.transpose(work[i][0:R, 0:P], negmax[:, c, :], ident[:, :]).then_inc(pe.sem, 1)
            g.q["pe"].append(f)
            done = pe.did()
            def on_act(e, b):
                pe.wait(e, b, done)
                if c:
                    mrow[c - 1].wait(e, b, marks["mrow", c - 1])
                else:
                    pe.wait_before(e, b, marks["c_end", C - 1])
                e.activation(m_hi[:, :], work[i][0:R, 0:P], ACT.Identity).then_inc(act.sem, 1)
            g.q["act"].append(on_act)
            h_done = act.did()
            def d(e, b):
                act.wait(e, b, h_done)
                e.tensor_tensor(m_lo[:, :], work[i][0:R, 0:P], m_hi[:, :].bitcast(F32), ALU.subtract).then_inc(dve.sem, 1)
            g.q["dve"].append(d)
            l_done = dve.did()
            free_bank(i, dve, l_done)
            def on_pool(e, b):
                dve.wait(e, b, l_done, s_go)
                pe.wait_before(e, b, marks["c_end", c], s_go)
                for row, src in ((3 * HD, m_hi), (3 * HD + 1, m_lo)):
                    e.dma_start(qs[c][row:row + 1, :, :].rearrange("a h n -> a (h n)").bitcast(F32),
                                src[:, :].bitcast(F32)).then_inc(mrow[c].sem, 16)
            g.q["pool"].append(on_pool)
            mrow[c].did()
            marks["mrow", c] = mrow[c].did()

        exp_marks = []
        pv_marks = []

        def exp_scores(c, k):
            n = c * T + k
            for p in range(2):
                take("st", p)
                def f(e, b, p=p):
                    if p == 0 and k == 0:
                        mrow[c].wait(e, b, marks["mrow", c])
                    for j in range(2):
                        h = 2 * p + j
                        ins = e.matmul(st[p][:, j, :], ks[c][0:3 * HD + 2, h, k * P:(k + 1) * P],
                                       qs[c][0:3 * HD + 2, h, :], start=True, stop=True)
                    ins.then_inc(pe.sem, 1)
                g.q["pe"].append(f)
                done = pe.did()
                def on_act(e, b, p=p, done=done):
                    pe.wait(e, b, done)
                    if n >= 2:
                        pe.wait(e, b, pv_marks[n - 2])
                    else:
                        pe.wait_before(e, b, pv_marks[n - 2 + C * T])
                    e.activation(pt[k % 2][:, 2 * p:2 * p + 2, :], st[p][:, :, :], ACT.Exp, scale=scale).then_inc(act.sem, 1)
                g.q["act"].append(on_act)
                exp_marks.append(act.did())
                last_reader["st", p] = (act, exp_marks[-1])
                gap()

        def weigh_values(c, k):
            n = c * T + k
            def values(e, b):
                if k == 0:
                    dve.wait(e, b, marks["v", c])
                    if c:
                        act.wait(e, b, marks["copied", c - 1, 0])
                    else:
                        act.wait_before(e, b, marks["copied", C - 1, 0])
                act.wait(e, b, exp_marks[2 * n + 1])
                for h in range(GROUP):
                    rows = slice(HD * h, HD * (h + 1))
                    e.matmul(o_ps[rows, :], v[:, k, c * P + HD * h:c * P + HD * (h + 1)], pt[k % 2][:, h, :],
                             start=(k == 0), stop=(k == T - 1))
            g.q["pe"].append(values)
            gap()
            def sums(e, b):
                for h in range(GROUP):
                    rows = slice(HD * h, HD * (h + 1))
                    ins = e.matmul(sum_ps[rows, :], ones[:, :], pt[k % 2][:, h, :], start=(k == 0), stop=(k == T - 1))
                ins.then_inc(pe.sem, 1)
            g.q["pe"].append(sums)
            pv_marks.append(pe.did())

        pieces = []

        def piece(n=1):
            for _ in range(n):
                if pieces:
                    pieces.pop(0)()

        def normalise(c):
            done = marks["c_end", c] = pv_marks[c * T + T - 1]
            for i, src in ((1, sum_ps), (0, o_ps)):
                def on_act(e, b, i=i, src=src):
                    pe.wait(e, b, done)
                    if c:
                        dve.wait(e, b, marks["norm", c - 1, T - 1])
                    else:
                        dve.wait_before(e, b, marks["norm", C - 1, T - 1])
                    e.activation(o_sum[:, i, :], src[:, :], ACT.Identity).then_inc(act.sem, 1)
                g.q["act"].append(on_act)
                marks["copied", c, i] = act.did()
            for t in range(T):
                def divide(t=t):
                    cols = slice(t * P, (t + 1) * P)
                    r = g.step("dve", [(act, marks["copied", c, 1])],
                               lambda e: e.reciprocal(o_sum[:, 1, cols], o_sum[:, 1, cols]))
                    def f(e, b):
                        act.wait(e, b, marks["copied", c, 0])
                        dve.wait(e, b, r[1])
                        if c == 0:
                            xln_store.wait(e, b, marks["xln_store"])
                        e.tensor_tensor(oT[:, c, cols], o_sum[:, 0, cols], o_sum[:, 1, cols], ALU.mult).then_inc(dve.sem, 1)
                    g.q["dve"].append(f)
                    marks["norm", c, t] = dve.did()
                pieces.append(divide)

        def project_out(t):
            i = take_bank()
            def f(e, b):
                for c in range(C):
                    if c == C - 1:
                        dve.wait(e, b, marks["norm", c, t])
                    elif t == 0:
                        dve.wait(e, b, marks["norm", c, T - 1])
                    ins = e.matmul(work[i][:, :], oT[:, c, t * P:(t + 1) * P], wo[:, c, :], start=(c == 0), stop=(c == C - 1))
                ins.then_inc(pe.sem, 1)
            g.q["pe"].append(f)
            done = pe.did()
            def d(e, b):
                pe.wait(e, b, done)
                pool.wait(e, b, marks["x_bo"])
                e.tensor_tensor(x2[:, t, :], work[i][:, :], x2[:, t, :], ALU.add).then_inc(dve.sem, 1)
            g.q["dve"].append(d)
            marks["x2", t] = dve.did()
            marks["out_pe"] = done
            free_bank(i, dve, marks["x2", t])
            norm_stats(g, x2, 1, t, lambda e, b: dve.wait(e, b, marks["x2", t]))

        def post_apply(g, t, first_wait=None):
            g.marks["ln2", t] = norm_apply(g, oT, x2, 1, t, first_wait)

        def post_logits(g, t, experts):
            for n in experts:
                g.marks["logits"] = g.step("dve", [g.marks.get("logits", (g.dve, 0)), (g.dve, g.marks["ln2", t])], lambda e, n=n: e.tensor_tensor_reduce(
                    out=products[:, :], in0=oT[:, t, :], in1=rw_rows[:, n, :], scale=1.0, scalar=0.0,
                    op0=ALU.mult, op1=ALU.add, accum_out=lg[:, t, n:n + 1]))

        def post_store(g, xln_store, x2_store):
            def s(e, b):
                g.dve.wait(e, b, g.marks["ln2", T - 1], s_go)
                e.dma_start(xln_dram[bass.ds(b, 1), :, :].rearrange("a (t p) n -> p (a t) n", p=P), oT[:, :, :]).then_inc(xln_store.sem, 16)
                e.dma_start(x2_dram[bass.ds(b, 1), :, :].rearrange("a (t p) n -> p (a t) n", p=P), x2[:, :, :]).then_inc(x2_store.sem, 16)
            g.q["sp"].append(s)
            g.marks["xln_store"] = xln_store.did()
            g.marks["x2_store"] = x2_store.did()
            def d(e, b):
                g.dve.wait(e, b, g.marks["logits"][1])
                e.tensor_tensor(logits[:, bass.ds(b * T, T), :], lg[:, :, :],
                                rb_rows[:, :].unsqueeze(1).to_broadcast([P, T, E]), ALU.add).then_inc(g.dve.sem, 1)
            g.q["dve"].append(d)
            g.dve.did()

        def load_ctx():
            def s(e, b):
                pe.wait(e, b, marks["proj_end"], s_go)
                e.dma_start(ctxT[:, :, :], ctx_t[bass.ds((b + 1) % B, 1), :, :].rearrange("a (c p) n -> p (a c) n", p=P)).then_inc(ctx_load.sem, 16)
            g.q["sp"].append(s)

        def load_x():
            def s(e, b):
                pe.wait(e, b, marks["x_turned"], s_go)
                e.dma_start(x_in[:, :, :], x[bass.ds((b + 1) % B, 1), :, :].rearrange("a (t p) n -> p (a t) n", p=P)).then_inc(x_load.sem, 16)
            g.q["sp"].append(s)
            marks["x_load"] = x_load.did()

        def load_residual():
            def s(e, b):
                x2_store.wait(e, b, marks["x2_store"], s_go)
                dve.wait(e, b, marks["ln2", T - 1], s_go)
                e.dma_start(x2[:, :, :], x[bass.ds(b, 1), :, :].rearrange("a (t p) n -> p (a t) n", p=P)).then_inc(res_load.sem, 16)
            g.q["sp"].append(s)
            marks["res_load"] = res_load.did()

        def add_bias():
            def on_pool(e, b):
                res_load.wait(e, b, marks["res_load"])
                e.tensor_tensor(x2[:, :, :], x2[:, :, :], bo_rows[:, :].unsqueeze(1).to_broadcast([P, T, D]), ALU.add).then_inc(pool.sem, 1)
            g.q["pool"].append(on_pool)
            marks["x_bo"] = pool.did()

        transpose_x()
        load_x()
        def ln2_ready(e, b):
            pool.wait_before(e, b, marks["rstd", 1][1])
            pe.wait_before(e, b, marks["out_pe"])
        todo = [(t, n) for t in range(T) for n in range(E)]

        def logits_of(count):
            for _ in range(count):
                t, n = todo.pop(0)
                post_logits(g, t, [n])

        for t in range(T):
            post_apply(g, t, ln2_ready)
        for c, share in ((0, (2, 3, 5)), (1, (5, 5, 5))):
            project_qk("q", c)
            logits_of(share[0])
            project_qk("k", c)
            logits_of(share[1])
            project_v(c)
            logits_of(share[2])
        for c in (2, 3):
            if c == 2:
                light += [(lambda: None,)] * 4
                light += [(row_max, 0, h, t, 2) for h in range(GROUP) for t in range(0, T, 2)]
                project_qk("q", c)
                logits_of(2)
                project_qk("k", c)
                logits_of(3)
                project_v(c)
                logits_of(2)
                post_store(g, xln_store, x2_store)
            else:
                light += [(turn_max, 0)] + [(row_max, 1, h, t, 2) for h in range(GROUP) for t in range(0, T, 2)]
                project_qk("q", c)
                project_qk("k", c)
                project_v(c)
        gap(len(light))
        assert not todo
        marks["proj_end"] = pe.per_turn
        load_ctx()
        load_residual()
        light += [(turn_max, 1)]
        light += [(row_max, 2, h, t) for h in range(GROUP) for t in range(T)]
        light += [(row_max, 3, 0, 0), (row_max, 3, 0, 1), (turn_max, 2)]
        light += [(row_max, 3, h, t) for h in range(GROUP) for t in range(T)][2:]
        light += [(lambda: None,)] * 2 + [(turn_max, 3)]
        tiles = [(c, k) for c in range(C) for k in range(T)]
        exp_scores(*tiles[0])
        for n, (c, k) in enumerate(tiles):
            if n + 1 < len(tiles):
                exp_scores(*tiles[n + 1])
            weigh_values(c, k)
            if k == T - 1:
                piece(T)
                normalise(c)
            gap()
            if c == C - 2 and k == 2:
                for t in range(T):
                    norm_stats(g, x_in, 0, t, lambda e, b: x_load.wait(e, b, marks["x_load"]))
                norm_rstd(g, 0)
            if c == C - 1 and k == 0:
                for t in range(T):
                    marks["ln1"] = norm_apply(g, x_in, x_in, 0, t, lambda e, b: pool.wait(e, b, marks["rstd", 0][1]))
        assert not light
        add_bias()
        piece(T)
        for t in range(T):
            project_out(t)
        norm_rstd(g, 1)
        marks["ctx_next"] = ctx_load.did()

        head = Turn(sem, "head")
        for t in range(T):
            norm_stats(head, x_in, 0, t, lambda e, b: e.wait_ge(s_const, N_CONST))
        norm_rstd(head, 0)
        for t in range(T):
            norm_apply(head, x_in, x_in, 0, t, lambda e, b: head.pool.wait(e, b, head.marks["rstd", 0][1]))
        tail = Turn(sem, "tail")
        tail_xln, tail_x2 = Count(sem("tail_xln"), 16), Count(sem("tail_x2"), 16)
        for t in range(T):
            post_apply(tail, t, lambda e, b: None)
            post_logits(tail, t, range(E))
        post_store(tail, tail_xln, tail_x2)

        consts = [(x_in, x[0].rearrange("(t p) n -> p t n", p=P)), (ctxT, ctx_t[0].rearrange("(c p) n -> p c n", p=P))]
        consts += [(dst, src.rearrange("(c p) n -> p c n", p=P)) for dst, src in zip((wq, wk, wv, wo), w_t)]
        consts += [(bq_col, bq), (bk_col, bk)]
        rows = [(bv_rows[:, :], bv), (bo_rows[:, :], bo), (rb_rows[:, :], router_b),
                (rw_rows[:, :, :].rearrange("p e n -> p (e n)"), router_w.rearrange("e n -> (e n)"))]
        N_CONST = 16 * (len(consts) + len(rows))

        with nc.Block() as block:
            @block.sync
            def _(e):
                for dst, src in consts:
                    e.dma_start(dst[:], src).then_inc(s_const, 16)
                for dst, src in rows:
                    e.dma_start(dst, src.partition_broadcast(P)).then_inc(s_const, 16)
                e.wait_ge(s_const, N_CONST)

            @block.gpsimd
            def _(e):
                head.pool.open(e)
                fills = [(minus_half[:, :], -0.5), (eps_col[:, :], LN_EPS), (ones[:, :], 1.0), (x2[:, :, :], 0.0)]
                fills += [(mv[:, 1, :, :], 0.0), (rstd[:, 1, :], 0.0)]
                fills += [(ks[c][3 * HD:P, :, :].bitcast(F32), 1.0) for c in range(C)]
                for n, (dst, value) in enumerate(fills):
                    e.memset(dst, value).then_inc(s_init, 1)
                    e.wait_ge(s_init, n + 1)
                head.run("pool", e, 0)

            @block.vector
            def _(e):
                head.dve.open(e)
                head.run("dve", e, 0)

        with nc.Block() as block:
            @block.sync
            def _(e):
                for c in (x_load, ctx_load, res_load, x2_store, xln_store, *stack):
                    c.open(e)
                with e.Fori(0, B) as b:
                    g.run("sp", e, b)
                ctx_load.wait(e, B - 1, marks["ctx_next"])
                xln_store.wait(e, B - 1, marks["xln_store"])
                x2_store.wait(e, B - 1, marks["x2_store"])

            for name, run in (("gpsimd", "pool"), ("vector", "dve"), ("scalar", "act"), ("tensor", "pe")):
                deco = {"gpsimd": block.gpsimd, "vector": block.vector, "scalar": block.scalar, "tensor": block.tensor}[name]

                @deco
                def _(e, run=run):
                    {"pool": pool, "dve": dve, "act": act, "pe": pe}[run].open(e)
                    with e.Fori(0, B) as b:
                        g.run(run, e, b)

        with nc.Block() as block:
            @block.sync
            def _(e):
                tail_xln.open(e, B)
                tail_x2.open(e, B)
                tail.run("sp", e, B)
                tail_xln.wait(e, B, tail.marks["xln_store"])
                tail_x2.wait(e, B, tail.marks["x2_store"])

            @block.vector
            def _(e):
                tail.dve.open(e, B)
                tail.run("dve", e, B)


def routing_stage(nc, logits, skip, w12, pos, tile_expert, tile_changed, token_of, n_tiles):
    NT, E = logits.shape[1] - skip, logits.shape[2]
    KT = TOP_K * NT
    SLOTS = token_of.shape[1]
    SHIFT = P.bit_length() - 1
    TILE_SHIFT = FTOK.bit_length() - 1

    with ExitStack() as ctx:
        sb = lambda name, shape, dt=F32: ctx.enter_context(nc.sbuf_tensor(name, shape, dt))
        psum = lambda name, shape: ctx.enter_context(nc.psum_tensor(name, shape, F32))
        sem = lambda name: ctx.enter_context(nc.semaphore(name))
        g = Turn(sem, "route")

        iota_i = sb("iota_i", [P, P], I32)
        part_i = sb("part_i", [P, 1], I32)
        iota_f = sb("iota_f", [P, P])
        iota_b = sb("iota_b", [P, P], BF16)
        part_f = sb("part_f", [P, 1])
        expert_less = sb("expert_less", [P, E])
        tri = sb("tri", [P, P], BF16)
        ones_b = sb("ones_b", [P, P], BF16)
        keep = sb("keep", [P, E, NT])
        ones_e = sb("ones_e", [P, E])
        best = sb("best", [P, TOP_K, NT])
        pick = sb("pick", [P, NT])
        scratch = sb("scratch", [P, NT, E])
        masked = sb("masked", [P, NT, E])
        hot = [sb(f"hot{i}", [P, NT, E]) for i in range(TOP_K)]
        hots = sb("hots", [P, NT, E], BF16)
        expo = sb("expo", [P, NT, E])
        expo2 = sb("expo2", [P, NT])
        inv_sum = sb("inv_sum", [P, NT])
        tile_count = sb("tile_count", [P, E, NT])
        running = sb("running", [P, E, NT])
        before = sb("before", [P, E, NT])
        padded = sb("padded", [P, E])
        padded_i = sb("padded_i", [P, E], I32)
        tiles_of = sb("tiles_of", [P, E])
        tile_end = sb("tile_end", [P, E])
        start = sb("start", [P, E])
        place = sb("place", [P, NT, E])
        pos_f = sb("pos_f", [P, TOP_K, NT])
        col_i = sb("col_i", [P, KT], I32)
        row_i = sb("row_i", [P, KT], I32)
        col_b = sb("col_b", [P, KT], BF16)
        row_b = sb("row_b", [P, KT], BF16)
        col_hot = sb("col_hot", [P, KT, 2, SLOTS], BF16)
        row_hot = sb("row_hot", [P, KT, P], BF16)
        low = sb("low", [P, SLOTS])
        ended = sb("ended", [P, n_tiles, E])
        expert_f = sb("expert_f", [P, n_tiles])
        changed_f = sb("changed_f", [P, n_tiles])
        count_ps = psum("count_ps", [P, 2, NT * E])
        list_ps = psum("list_ps", [P, 2 * SLOTS])

        L = logits[:, skip:, :]
        e_of = lambda a: a.unsqueeze(2).to_broadcast([P, NT, E])
        t_of = lambda a: a.unsqueeze(1).to_broadcast([P, NT, E])
        V = lambda waits, emit: g.step("dve", waits, emit)

        p0 = g.step("pool", [], lambda e: e.iota(iota_i[:, :], [[1, P]], base=0, channel_multiplier=0))
        p1 = g.step("pool", [p0], lambda e: e.iota(part_i[:, :], [[1, 1]], base=0, channel_multiplier=1))
        p2 = g.step("pool", [p1], lambda e: e.memset(ones_b[:, :], 1.0))
        tri_on = g.step("pool", [p2], lambda e: e.affine_select(out=tri[:, :], in_=ones_b[:, :], compare_op=ALU.is_gt, fill=0.0,
                                                               base=0, pattern=[[1, P]], channel_multiplier=-1))
        p3 = g.step("pool", [tri_on], lambda e: e.memset(keep[:, :, :], 1.0))
        p4 = g.step("pool", [p3], lambda e: e.memset(keep[:, :, 0:1], 0.0))
        p5 = g.step("pool", [p4], lambda e: e.memset(ones_e[:, :], 1.0))
        f0 = V([p0], lambda e: e.tensor_copy(iota_f[:, :], iota_i[:, :]))
        f1 = V([p1], lambda e: e.tensor_copy(part_f[:, :], part_i[:, :]))
        f2 = V([f0], lambda e: e.tensor_copy(iota_b[:, :], iota_f[:, :]))
        f3 = V([f0], lambda e: e.tensor_scalar(expert_less[:, :], iota_f[:, 0:E], -float(E), None, ALU.add))

        source, last = L, f3
        for s in range(TOP_K):
            d = V([last], lambda e, s=s, source=source: e.tensor_reduce(best[:, s, :], source, AX.X, ALU.max))
            d = V([d], lambda e, s=s, source=source: e.tensor_tensor(scratch[:, :, :], source, e_of(best[:, s, :]), ALU.is_equal))
            d = V([d], lambda e: e.tensor_tensor(scratch[:, :, :], scratch[:, :, :], t_of(expert_less[:, :]), ALU.mult))
            d = V([d], lambda e: e.tensor_reduce(pick[:, :], scratch[:, :, :], AX.X, ALU.min))
            last = V([d], lambda e, s=s: e.tensor_tensor(hot[s][:, :, :], t_of(expert_less[:, :]), e_of(pick[:, :]), ALU.is_equal))
            if s == 0:
                last = V([last], lambda e: e.scalar_tensor_tensor(out=masked[:, :, :], in0=hot[0][:, :, :], scalar=-1e30, in1=L,
                                                                  op0=ALU.mult, op1=ALU.add))
                source = masked[:, :, :]
        hots_on = V([last], lambda e: e.tensor_tensor(hots[:, :, :], hot[0][:, :, :], hot[1][:, :, :], ALU.add))

        d = V([last], lambda e: e.tensor_tensor(expo[:, :, :], L, e_of(best[:, 0, :]), ALU.subtract))
        d2 = V([last], lambda e: e.tensor_tensor(expo2[:, :], best[:, 1, :], best[:, 0, :], ALU.subtract))
        a1 = g.step("act", [d], lambda e: e.activation(expo[:, :, :], expo[:, :, :], ACT.Exp))
        a2 = g.step("act", [d2], lambda e: e.activation(expo2[:, :], expo2[:, :], ACT.Exp))
        d = V([a1], lambda e: e.tensor_reduce(inv_sum[:, :], expo[:, :, :], AX.X, ALU.add))
        d = V([d], lambda e: e.reciprocal(w12[:, 0, :], inv_sum[:, :]))
        V([d, a2], lambda e: e.tensor_tensor(w12[:, 1, :], expo2[:, :], w12[:, 0, :], ALU.mult))

        flat = hots[:, :, :].rearrange("p t e -> p (t e)")
        c1 = g.step("pe", [hots_on, tri_on], lambda e: e.matmul(count_ps[:, 0, :], tri[:, :], flat, start=True, stop=True))
        c2 = g.step("pe", [], lambda e: e.matmul(count_ps[:, 1, :], ones_b[:, :], flat, start=True, stop=True))
        d = V([c2], lambda e: e.tensor_copy(tile_count[:, :, :], count_ps[:, 1, :].rearrange("p (t e) -> p e t", e=E)))
        d = V([d, p4], lambda e: e.tensor_tensor_scan(running[:, :, :].rearrange("p e t -> p (e t)"),
                                                      keep[:, :, :].rearrange("p e t -> p (e t)"),
                                                      tile_count[:, :, :].rearrange("p e t -> p (e t)"), 0.0, ALU.mult, ALU.add))
        d_run = V([d], lambda e: e.tensor_tensor(before[:, :, :], running[:, :, :], tile_count[:, :, :], ALU.subtract))
        d = V([d], lambda e: e.tensor_scalar(padded[:, :], running[:, :, NT - 1], float(FTOK - 1), None, ALU.add))
        d = V([d], lambda e: e.tensor_copy(padded_i[:, :], padded[:, :]))
        d = V([d], lambda e: e.tensor_scalar(padded_i[:, :], padded_i[:, :], TILE_SHIFT, None, ALU.arith_shift_right))
        d = V([d], lambda e: e.tensor_copy(tiles_of[:, :], padded_i[:, :]))
        d_end = V([d, p5], lambda e: e.tensor_tensor_scan(tile_end[:, :], ones_e[:, :], tiles_of[:, :], 0.0, ALU.mult, ALU.add))
        d = V([d_end], lambda e: e.tensor_tensor(start[:, :], tile_end[:, :], tiles_of[:, :], ALU.subtract))
        d = V([d], lambda e: e.tensor_scalar(start[:, :], start[:, :], float(FTOK), None, ALU.mult))
        d = V([c1, d_run], lambda e: e.tensor_tensor(place[:, :, :], count_ps[:, 0, :].rearrange("p (t e) -> p t e", e=E),
                                                     before[:, :, :].rearrange("p e t -> p t e"), ALU.add))
        d_place = V([d], lambda e: e.tensor_tensor(place[:, :, :], place[:, :, :], t_of(start[:, :]), ALU.add))
        for s in range(TOP_K):
            d = V([d_place], lambda e, s=s: e.tensor_tensor(hot[s][:, :, :], hot[s][:, :, :], place[:, :, :], ALU.mult))
            d = V([d], lambda e, s=s: e.tensor_reduce(pos_f[:, s, :], hot[s][:, :, :], AX.X, ALU.add))
        d_pos = V([d], lambda e: e.tensor_copy(pos[:, :, :], pos_f[:, :, :]))

        d = V([d_end], lambda e: e.tensor_tensor(ended[:, :, :], iota_f[:, 0:n_tiles].unsqueeze(2).to_broadcast([P, n_tiles, E]),
                                                 tile_end[:, :].unsqueeze(1).to_broadcast([P, n_tiles, E]), ALU.is_ge))
        d = V([d], lambda e: e.tensor_reduce(expert_f[:, :], ended[:, :, :], AX.X, ALU.add))
        d_exp = V([d], lambda e: e.tensor_scalar(expert_f[:, :], expert_f[:, :], float(E - 1), None, ALU.min))
        V([d_exp], lambda e: e.tensor_copy(tile_expert[0:1, :], expert_f[0:1, :]))
        d = V([], lambda e: e.memset(changed_f[:, 0:2], 1.0))
        d = V([d, d_exp], lambda e: e.tensor_tensor(changed_f[:, 2:], expert_f[:, 2:], expert_f[:, :-2], ALU.not_equal))
        V([d], lambda e: e.tensor_copy(tile_changed[0:1, :], changed_f[0:1, :]))

        flat_pos = pos[:, :, :].rearrange("p s t -> p (s t)")
        d = V([d_pos], lambda e: e.tensor_scalar(col_i[:, :], flat_pos, SHIFT, None, ALU.arith_shift_right))
        d2 = V([d_pos], lambda e: e.tensor_scalar(row_i[:, :], flat_pos, P - 1, None, ALU.bitwise_and))
        d = V([d], lambda e: e.tensor_copy(col_b[:, :], col_i[:, :]))
        d2 = V([d2], lambda e: e.tensor_copy(row_b[:, :], row_i[:, :]))
        d_row = V([d2, f2], lambda e: e.tensor_tensor(row_hot[:, :, :], iota_b[:, :].unsqueeze(1).to_broadcast([P, KT, P]),
                                                      row_b[:, :].unsqueeze(2).to_broadcast([P, KT, P]), ALU.is_equal))
        d = V([d], lambda e: e.tensor_tensor(col_hot[:, :, 1, :], iota_b[:, 0:SLOTS].unsqueeze(1).to_broadcast([P, KT, SLOTS]),
                                             col_b[:, :].unsqueeze(2).to_broadcast([P, KT, SLOTS]), ALU.is_equal))
        for s in range(TOP_K):
            cols = slice(s * NT, (s + 1) * NT)
            d3 = V([d, f2], lambda e, cols=cols: e.tensor_tensor(
                col_hot[:, cols, 0, :], col_hot[:, cols, 1, :],
                iota_b[:, 0:NT].unsqueeze(2).to_broadcast([P, NT, SLOTS]), ALU.mult))
        d4 = V([d3, f1], lambda e: e.tensor_scalar(col_hot[:, :, 1, :], col_hot[:, :, 1, :], part_f[:, 0:1], None, ALU.mult))
        for n in range(KT):
            c = g.step("pe", [d_row, d4] if n == 0 else [], lambda e, n=n: e.matmul(
                list_ps[:, :], row_hot[:, n, :], col_hot[:, n, :, :].rearrange("p a c -> p (a c)"), start=(n == 0), stop=(n == KT - 1)))
        d = V([c], lambda e: e.tensor_scalar(low[:, :], list_ps[:, SLOTS:], float(skip * P), None, ALU.add))
        V([d], lambda e: e.scalar_tensor_tensor(out=token_of[:, :], in0=list_ps[:, 0:SLOTS], scalar=float(P), in1=low[:, :],
                                                op0=ALU.mult, op1=ALU.add))

        with nc.Block() as block:
            for name in ("pool", "dve", "act", "pe"):
                deco = {"pool": block.gpsimd, "dve": block.vector, "act": block.scalar, "pe": block.tensor}[name]

                @deco
                def _(e, name=name):
                    g.count[name].open(e)
                    g.run(name, e, 0)


def expert_stage(nc, xln_dram, y_dram, w_gate_up, w_down, b_gate_up, b_down, tile_expert, tile_changed, token_of, ident, n_tiles, s_go):
    E, D, F2 = w_gate_up.shape
    F = F2 // 2
    KD, KF = D // P, F // P
    SUB = FTOK // P
    rows = xln_dram.rearrange("b s d -> (b s) d")

    with ExitStack() as ctx:
        sb = lambda name, shape, dt=F32: ctx.enter_context(nc.sbuf_tensor(name, shape, dt))
        psum = lambda name, shape: ctx.enter_context(nc.psum_tensor(name, shape, F32))
        sem = lambda name: ctx.enter_context(nc.semaphore(name))
        g = Turn(sem, "ffn")
        head = Turn(sem, "ffn_head")
        pe, act, dve, pool, marks = g.pe, g.act, g.dve, g.pool, g.marks
        raw_load = [Count(sem(f"s_raw{s}"), 16) for s in range(2)]
        bias_load = [Count(sem(f"s_bias{s}"), 16) for s in range(2)]
        w_hi = [Count(sem(f"s_whi{s}")) for s in range(2)]
        w_lo = [Count(sem(f"s_wlo{s}")) for s in range(2)]
        s_head = sem("s_ffn_head_raw")
        gather = [Count(sem(f"s_gather{s}"), 16, ahead=0) for s in range(2)]
        head_gather = Count(sem("s_gather_head"), 16, ahead=0)
        store = [Count(sem(f"s_y{s}"), 16) for s in range(2)]

        raw_g = [sb(f"raw_g{s}", [P, KD, F2]) for s in range(2)]
        raw_d = [sb(f"raw_d{s}", [P, KF, D]) for s in range(2)]
        pair = lambda name, shape, s: [sb(f"{name}_{part}{s}", shape, F32R) for part in ("hi", "lo")]
        wg = [pair("wg", [P, KD, F2], s) for s in range(2)]
        wd = [pair("wd", [P, KF, D], s) for s in range(2)]
        PASSES = ((0, 0), (0, 1), (1, 0))
        bg = [sb(f"bg{s}", [P, F2 // P]) for s in range(2)]
        bd = [sb(f"bd{s}", [P, D]) for s in range(2)]
        bu1 = [sb(f"bu1{s}", [P, KF]) for s in range(2)]
        idx = [sb(f"idx{s}", [P, SUB], I32) for s in range(2)]
        xg = [sb(f"xg{s}", [P, SUB, D]) for s in range(2)]
        xgT = [pair("xgT", [P, KD, FTOK], s) for s in range(2)]
        gate = [sb(f"gate{i}", [P, FTOK]) for i in range(2)]
        sig = [sb(f"sig{i}", [P, FTOK]) for i in range(2)]
        up = [sb(f"up{i}", [P, FTOK]) for i in range(2)]
        hid_f = [sb(f"hid_f{i}", [P, FTOK]) for i in range(2)]
        hid = pair("hid", [P, KF, FTOK], "")
        y = [sb(f"y{s}", [P, SUB, D]) for s in range(2)]
        t_ps = [psum(f"t_ps{i}", [P, 2, FTOK]) for i in range(KD // 2)]
        gu_ps = [psum(f"gu_ps{i}", [P, 2, FTOK]) for i in range(2)]
        d_ps = [psum(f"d_ps{i}", [P, D]) for i in range(2)]

        def fetch(g, gather, s, tile, first_wait):
            def copy(e, b):
                first_wait(e, b)
                e.tensor_copy(idx[s][:, :], token_of[:, bass.ds(b * (2 * SUB) + tile * SUB, SUB)]).then_inc(g.pool.sem, 1)
            g.q["pool"].append(copy)
            m = g.pool.did()
            def rows_in(e, b):
                g.pool.wait(e, b, m, s_go)
                for i in range(SUB):
                    e.indirect_dma_start(out=xg[s][:, i, :], out_offset=None, in_=rows,
                                         in_offset=bass.IndirectOffsetOnAxis(ap=idx[s][:, i:i + 1].bitcast(U32), axis=0)).then_inc(gather.sem, 16)
            g.q["pool"].append(rows_in)
            for _ in range(SUB):
                g.marks["gather", s] = gather.did()

        def raw_copies(s, expert):
            return ((raw_g[s][:, :, :], w_gate_up[bass.ds(expert, 1), :, :].rearrange("a (k p) f -> p (a k) f", p=P)),
                    (raw_d[s][:, :, :], w_down[bass.ds(expert, 1), :, :].rearrange("a (k p) f -> p (a k) f", p=P)))

        def bias_copies(s, expert):
            return ((bg[s][:, :], b_gate_up[bass.ds(expert, 1), :, :].rearrange("a p c -> p (a c)")),
                    (bd[s][:, :], b_down[bass.ds(expert, 1), :].to_broadcast([P, D])))

        def issue(e, copies, s, tile, semaphore):
            expert = e.value_load(tile_expert[0:1, tile], min_val=0, max_val=E - 1)
            changed = e.value_load(tile_changed[0:1, tile], min_val=0, max_val=1)
            for dst, src in copies(s, expert):
                e.dma_start(dst, src, cond=changed).then_inc(semaphore, 16)

        def load_raw(s, tile):
            def f(e, b):
                (w_lo[s].wait if s else w_lo[s].wait_before)(e, b, marks["w_lo", s], s_go)
                (w_hi[s].wait if s else w_hi[s].wait_before)(e, b, marks["w_hi", s], s_go)
                issue(e, raw_copies, s, bass.ds(b * 2 + tile, 1), raw_load[s].sem)
            g.q["sp"].append(f)
            for _ in range(2):
                marks["raw", s] = raw_load[s].did()

        def load_bias(s, tile):
            def f(e, b):
                (dve.wait_before if s else dve.wait)(e, b, marks["y", s], s_go)
                issue(e, bias_copies, s, bass.ds(b * 2 + tile, 1), bias_load[s].sem)
            g.q["sp"].append(f)
            for _ in range(2):
                marks["bias", s] = bias_load[s].did()

        def split_hi(e, s, k, sem):
            e.activation(wg[s][0][:, k, :], raw_g[s][:, k, :], ACT.Identity).then_inc(sem, 1)
            e.activation(wd[s][0][:, k, :], raw_d[s][:, k, :], ACT.Identity).then_inc(sem, 1)

        def split_lo(e, s, k, sem, down):
            w, raw = (wd[s], raw_d[s]) if down else (wg[s], raw_g[s])
            e.tensor_tensor(w[1][:, k, :], raw[:, k, :], w[0][:, k, :].bitcast(F32), ALU.subtract).then_inc(sem, 1)

        changed_of = {}

        def guarded(e, b, name, s, tile, split, sem, amount, first):
            if first:
                changed_of[name, s] = e.to_reg(e.value_load(tile_changed[0:1, bass.ds(b * 2 + tile, 1)], min_val=0, max_val=1))
            with e.If_ne(changed_of[name, s], 0):
                split()
            with e.Else():
                e.sem_inc(sem, amount)

        def weights_free_and_in(e, b, s):
            (pe.wait_before if s else pe.wait)(e, b, marks["down", s], s_go)
            (raw_load[s].wait_before if s else raw_load[s].wait)(e, b, marks["raw", s], s_go)

        def make_hi(s, k, tile):
            def on_act(e, b):
                if k == 0:
                    weights_free_and_in(e, b, s)
                guarded(e, b, "act", s, tile, lambda: split_hi(e, s, k, w_hi[s].sem), w_hi[s].sem, 2, k == 0)
            g.q["act"].append(on_act)
            for _ in range(2):
                marks["w_hi", s, k] = w_hi[s].did()
            marks["w_hi", s] = marks["w_hi", s, k]

        def make_lo(s, tile):
            for down in (0, 1):
                for k in range(KD):
                    def on_pool(e, b, k=k, down=down):
                        if k == 0 and not down:
                            weights_free_and_in(e, b, s)
                        w_hi[s].wait(e, b, marks["w_hi", s, k], s_go)
                        guarded(e, b, "pool", s, tile, lambda: split_lo(e, s, k, w_lo[s].sem, down), w_lo[s].sem, 1,
                                k == 0 and not down)
                    g.q["pool"].append(on_pool)
                    marks["w_lo", s, down] = marks["w_lo", s] = w_lo[s].did()

        def turn_rows(g, gather, s, bank_free):
            for half in range(KD // 2):
                def f(e, b, half=half):
                    gather.wait(e, b, g.marks["gather", s])
                    bank_free(e, b, half)
                    for k in range(2):
                        for i in range(SUB):
                            c = 2 * half + k
                            ins = e.transpose(t_ps[half][:, k, i * P:(i + 1) * P], xg[s][:, i, c * P:(c + 1) * P], ident[:, :])
                    ins.then_inc(g.pe.sem, 1)
                g.q["pe"].append(f)
                done = g.marks["turned", s] = g.pe.did()
                def a(e, b, half=half, done=done):
                    g.pe.wait(e, b, done)
                    e.activation(xgT[s][0][:, 2 * half:2 * half + 2, :], t_ps[half][:, :, :], ACT.Identity).then_inc(g.act.sem, 1)
                g.q["act"].append(a)
                hi_made = g.act.did()
                def d(e, b, half=half, hi_made=hi_made):
                    g.act.wait(e, b, hi_made)
                    chunks = slice(2 * half, 2 * half + 2)
                    e.tensor_tensor(xgT[s][1][:, chunks, :], t_ps[half][:, :, :], xgT[s][0][:, chunks, :].bitcast(F32),
                                    ALU.subtract).then_inc(g.dve.sem, 1)
                g.q["dve"].append(d)
                g.marks["xgT", s, half] = g.dve.did()

        def gate_up(s, split_next):
            def plus_one(e, b):
                (bias_load[s].wait if s else bias_load[s].wait_before)(e, b, marks["bias", s])
                e.tensor_scalar(bu1[s][:, :], bg[s][:, KF:], 1.0, None, ALU.add).then_inc(dve.sem, 1)
            g.q["dve"].append(plus_one)
            bu1_on = dve.did()
            split_next(0)
            parts = []
            for f in range(KF):
                i = f % 2
                n = s * KF + f
                def p(e, b, f=f, i=i, n=n):
                    if f == 0:
                        (w_hi[s].wait if s else w_hi[s].wait_before)(e, b, marks["w_hi", s])
                        (w_lo[s].wait if s else w_lo[s].wait_before)(e, b, marks["w_lo", s, 0])
                        (dve.wait if s else dve.wait_before)(e, b, marks["xgT", s, KD // 2 - 1])
                    if n >= 2:
                        dve.wait(e, b, marks["up", n - 2])
                    else:
                        dve.wait_before(e, b, marks["up", n - 2 + 2 * KF])
                    for part in range(2):
                        cols = slice(part * F + f * P, part * F + (f + 1) * P)
                        for k in range(KD):
                            for n_pass, (pw, px) in enumerate(PASSES):
                                ins = e.matmul(gu_ps[i][:, part, :], wg[s][pw][:, k, cols], xgT[s][px][:, k, :],
                                               start=(k == 0 and n_pass == 0), stop=(k == KD - 1 and n_pass == len(PASSES) - 1))
                    ins.then_inc(pe.sem, 1)
                g.q["pe"].append(p)
                made = (pe, pe.did())
                def clip_gate(e, b, i=i, f=f, n=n, made=made):
                    made[0].wait(e, b, made[1])
                    if n >= 2:
                        dve.wait(e, b, marks["hid_f", n - 2])
                    else:
                        dve.wait_before(e, b, marks["hid_f", n - 2 + 2 * KF])
                    e.tensor_scalar(gate[i][:, :], gu_ps[i][:, 0, :], bg[s][:, f:f + 1], LIMIT, ALU.add, ALU.min).then_inc(dve.sem, 1)
                g.q["dve"].append(clip_gate)
                g1 = (dve, dve.did())
                s1 = g.step("act", [g1], lambda e, i=i: e.activation(sig[i][:, :], gate[i][:, :], ACT.Sigmoid, scale=ALPHA))
                u1 = g.step("dve", [made, (dve, bu1_on)], lambda e, i=i, f=f: e.tensor_scalar(
                    up[i][:, :], gu_ps[i][:, 1, :], bu1[s][:, f:f + 1], LIMIT + 1.0, ALU.add, ALU.min))
                marks["up", n] = u1[1]
                if f:
                    glu(s, f - 1, *pending, parts)
                if f > 1:
                    parts.pop(0)()
                pending = (s1, u1)
                if f + 1 < KF:
                    split_next(f + 1)
            glu(s, KF - 1, *pending, parts)
            for lo_part in parts:
                lo_part()

        def glu(s, f, s1, u1, parts):
            i = f % 2
            g2 = g.step("dve", [s1], lambda e: e.tensor_tensor(gate[i][:, :], gate[i][:, :], sig[i][:, :], ALU.mult))
            n = s * KF + f
            def h(e, b):
                if n >= 2:
                    dve.wait(e, b, marks["hid_of", n - 2])
                else:
                    dve.wait_before(e, b, marks["hid_of", n - 2 + 2 * KF])
                dve.wait(e, b, g2[1])
                e.scalar_tensor_tensor(out=hid_f[i][:, :], in0=up[i][:, :], scalar=1.0 - LIMIT, in1=gate[i][:, :],
                                       op0=ALU.max, op1=ALU.mult).then_inc(dve.sem, 1)
            g.q["dve"].append(h)
            made = marks["hid_f", n] = dve.did()
            def to_hi(e, b):
                (pe.wait if s else pe.wait_before)(e, b, marks["down", 1 - s])
                dve.wait(e, b, made)
                e.activation(hid[0][:, f, :], hid_f[i][:, :], ACT.Identity).then_inc(act.sem, 1)
            g.q["act"].append(to_hi)
            hi_made = (act, act.did())
            def lo_part():
                marks["hid_of", n] = g.step("dve", [hi_made], lambda e: e.tensor_tensor(
                    hid[1][:, f, :], hid_f[i][:, :], hid[0][:, f, :].bitcast(F32), ALU.subtract))[1]
            parts.append(lo_part)

        def down(s):
            for k in range(KF):
                for i in range(SUB):
                    def p(e, b, i=i, k=k):
                        if k == 0 and i == 0:
                            (w_lo[s].wait if s else w_lo[s].wait_before)(e, b, marks["w_lo", s, 1])
                        if k == 0 and s:
                            dve.wait(e, b, marks["y", 0, i])
                        elif k == 0:
                            dve.wait_before(e, b, marks["y", 1, i])
                        if i == 0:
                            dve.wait(e, b, marks["hid_of", s * KF + k])
                        for n_pass, (pw, px) in enumerate(PASSES):
                            ins = e.matmul(d_ps[i][:, :], hid[px][:, k, i * P:(i + 1) * P], wd[s][pw][:, k, :],
                                           start=(k == 0 and n_pass == 0), stop=(k == KF - 1 and n_pass == len(PASSES) - 1))
                        if k == KF - 1:
                            ins.then_inc(pe.sem, 1)
                    g.q["pe"].append(p)
                    if k == KF - 1:
                        done = marks["down", s] = pe.did()
                        rows_out(s, i, done)

        def rows_out(s, i, done):
            def d(e, b):
                pe.wait(e, b, done)
                store[s].wait_before(e, b, marks["store", s])
                e.tensor_tensor(y[s][:, i, :], d_ps[i][:, :], bd[s][:, :], ALU.add).then_inc(dve.sem, 1)
            g.q["dve"].append(d)
            marks["y", s, i] = marks["y", s] = dve.did()

        def store_rows(s):
            def f(e, b):
                dve.wait(e, b, marks["y", s], s_go)
                e.dma_start(y_dram[bass.ds(b * 2 + s, 1), :, :].rearrange("a (i p) n -> p (a i) n", p=P), y[s][:, :, :]).then_inc(store[s].sem, 16)
            g.q["act" if s else "sp"].append(f)
            marks["store", s] = store[s].did()

        fetch(head, head_gather, 0, 0, lambda e, b: None)
        turn_rows(head, head_gather, 0, lambda e, b, half: None)

        fetch(g, gather[1], 1, 1, lambda e, b: pe.wait_before(e, b, marks["turned", 1]))
        ahead = len(g.q["pool"])
        fetch(g, gather[0], 0, 2, lambda e, b: pe.wait_before(e, b, marks["turned", 0]))
        ahead = range(ahead, len(g.q["pool"]))
        load_bias(1, 1)
        load_raw(0, 2)
        make_lo(1, 1)
        gate_up(0, lambda k: make_hi(1, k, 1))
        turn_rows(g, gather[1], 1, lambda e, b, half: dve.wait_before(e, b, marks["xgT", 0, half]))
        down(0)
        sp_store = len(g.q["sp"])
        store_rows(0)
        first_tile = {n: len(g.q[n]) for n in g.q}
        load_bias(0, 2)
        load_raw(1, 3)
        make_lo(0, 2)
        gate_up(1, lambda k: make_hi(0, k, 2))
        turn_rows(g, gather[0], 0, lambda e, b, half: dve.wait(e, b, marks["xgT", 1, half]))
        down(1)
        store_rows(1)
        pairs = n_tiles // 2
        odd = n_tiles % 2
        assert odd

        with nc.Block() as block:
            @block.sync
            def _(e):
                issue(e, raw_copies, 0, slice(0, 1), s_head)
                issue(e, bias_copies, 0, slice(0, 1), bias_load[0].sem)
                issue(e, raw_copies, 1, slice(1, 2), raw_load[1].sem)
                e.wait_ge(s_head, 32)

            @block.gpsimd
            def _(e):
                head.pool.open(e)
                head.run("pool", e, 0)

            @block.tensor
            def _(e):
                head.pe.open(e)
                head.run("pe", e, 0)

            @block.scalar
            def _(e):
                head.act.open(e)
                head.run("act", e, 0)

            @block.vector
            def _(e):
                head.dve.open(e)
                head.run("dve", e, 0)

        with nc.Block() as block:
            @block.scalar
            def _(e):
                for k in range(KD):
                    split_hi(e, 0, k, w_hi[0].sem)

            @block.gpsimd
            def _(e):
                for down in (0, 1):
                    for k in range(KD):
                        e.wait_ge(w_hi[0].sem, 2 * (k + 1))
                        split_lo(e, 0, k, w_lo[0].sem, down)

        with nc.Block() as block:
            @block.sync
            def _(e):
                for c in (raw_load[0], bias_load[1], w_hi[1], w_lo[1], *store):
                    c.open(e)
                with e.Fori(0, pairs) as b:
                    g.run("sp", e, b)
                g.q["sp"][sp_store](e, pairs)
                store[0].wait(e, pairs, marks["store", 0])
                store[1].wait(e, pairs - 1, marks["store", 1])

            for name in ("pool", "dve", "act", "pe"):
                deco = {"pool": block.gpsimd, "dve": block.vector, "act": block.scalar, "pe": block.tensor}[name]

                @deco
                def _(e, name=name):
                    g.count[name].open(e)
                    with e.Fori(0, pairs) as b:
                        g.run(name, e, b)
                    for n, f in enumerate(g.q[name][:first_tile[name]]):
                        if name != "pool" or n not in ahead:
                            f(e, pairs)


def combine_stage(nc, x2_dram, y_dram, out, w12, pos, s_go):
    _, S, D = x2_dram.shape
    B = out.shape[0]
    T = S // P
    y_rows = y_dram.rearrange("a b d -> (a b) d")
    TT = 2 * T

    with ExitStack() as ctx:
        sb = lambda name, shape, dt=F32: ctx.enter_context(nc.sbuf_tensor(name, shape, dt))
        sem = lambda name: ctx.enter_context(nc.semaphore(name))
        g = Turn(sem, "mix")
        dve, pool, marks = g.dve, g.pool, g.marks
        res = [sb(f"res{i}", [P, T, D]) for i in range(2)]
        ya = sb("ya", [P, TOP_K, TT, D])
        idx = sb("idx", [P, TOP_K, TT], I32)
        w = sb("w", [P, TOP_K, TT])
        load = [Count(sem(f"s_res{i}"), 16) for i in range(2)]
        store = [Count(sem(f"s_out{i}"), 16) for i in range(2)]
        gathered = [Count(sem(f"s_ya{t}"), 16, ahead=0) for t in range(TT)]

        def copies():
            def f(e, b):
                dve.wait_before(e, b, marks["mixed", TT - 1])
                e.tensor_copy(w[:, :, :], w12[:, :, bass.ds(b * TT, TT)]).then_inc(pool.sem, 1)
                e.tensor_copy(idx[:, :, :], pos[:, :, bass.ds(b * TT, TT)]).then_inc(pool.sem, 1)
            g.q["pool"].append(f)
            marks["w"] = pool.did()
            marks["idx"] = pool.did()

        def gather(t):
            def f(e, b):
                if t == 0:
                    pool.wait(e, b, marks["idx"])
                dve.wait_before(e, b, marks["mixed", t], s_go)
                for s in range(TOP_K):
                    e.indirect_dma_start(out=ya[:, s, t, :], out_offset=None, in_=y_rows,
                                         in_offset=bass.IndirectOffsetOnAxis(ap=idx[:, s, t:t + 1].bitcast(U32), axis=0)).then_inc(gathered[t].sem, 16)
            g.q["pool"].append(f)
            for _ in range(TOP_K):
                marks["ya", t] = gathered[t].did()

        def load_residual(i):
            def f(e, b):
                store[i].wait_before(e, b, marks["store", i], s_go)
                e.dma_start(res[i][:, :, :], x2_dram[bass.ds(b * 2 + (i + 1), 1), :, :].rearrange("a (t p) n -> p (a t) n", p=P)).then_inc(load[i].sem, 16)
            g.q["sp"].append(f)
            marks["load", i] = load[i].did()

        def mix(t):
            i = t // T
            def f(e, b):
                load[i].wait(e, b, marks["load", i])
                gathered[t].wait(e, b, marks["ya", t])
                pool.wait(e, b, marks["w"])
                e.scalar_tensor_tensor(out=res[i][:, t % T, :], in0=ya[:, 0, t, :], scalar=w[:, 0, t:t + 1],
                                       in1=res[i][:, t % T, :], op0=ALU.mult, op1=ALU.add).then_inc(dve.sem, 1)
            g.q["dve"].append(f)
            m = (dve, dve.did())
            marks["mixed", t] = g.step("dve", [m], lambda e: e.scalar_tensor_tensor(
                out=res[i][:, t % T, :], in0=ya[:, 1, t, :], scalar=w[:, 1, t:t + 1],
                in1=res[i][:, t % T, :], op0=ALU.mult, op1=ALU.add))[1]

        def store_out(i):
            def f(e, b):
                dve.wait(e, b, marks["mixed", (i + 1) * T - 1], s_go)
                e.dma_start(out[bass.ds(b * 2 + i, 1), :, :].rearrange("a (t p) n -> p (a t) n", p=P), res[i][:, :, :]).then_inc(store[i].sem, 16)
            g.q["sp"].append(f)
            marks["store", i] = store[i].did()

        copies()
        load_residual(0)
        load_residual(1)
        for t in range(TT):
            gather(t)
            mix(t)
        store_out(0)
        store_out(1)

        with nc.Block() as block:
            @block.sync
            def _(e):
                for c in (*load, *store):
                    c.open(e)
                with e.Fori(0, B // 2) as b:
                    g.run("sp", e, b)
                for i in range(2):
                    store[i].wait(e, B // 2 - 1, marks["store", i])

            @block.gpsimd
            def _(e):
                pool.open(e)
                with e.Fori(0, B // 2) as b:
                    g.run("pool", e, b)

            @block.vector
            def _(e):
                dve.open(e)
                with e.Fori(0, B // 2) as b:
                    g.run("dve", e, b)


def build(nc, x, ctx_t, wq_t, bq, wk_t, bk, wv_t, bv, wo_t, bo, router_w, router_b, w_gate_up, b_gate_up, w_down, b_down, out):
    B, S, D = x.shape
    E = router_w.shape[0]
    T = S // P
    NT = B * T
    n_tiles = (TOP_K * B * S - E) // FTOK + E
    whole_turns = n_tiles + n_tiles % 2
    slots = whole_turns * (FTOK // P)
    x2_dram = nc.dram_tensor("x2_dram", (B + 1, S, D), F32, kind="Internal").ap()
    xln_dram = nc.dram_tensor("xln_dram", (B + 1, S, D), F32, kind="Internal").ap()
    y_dram = nc.dram_tensor("y_dram", (n_tiles, FTOK, D), F32, kind="Internal").ap()

    with ExitStack() as ctx:
        sb = lambda name, shape, dt=F32: ctx.enter_context(nc.sbuf_tensor(name, shape, dt))
        logits = sb("logits", [P, NT + T, E])
        ident = sb("ident", [P, P])
        w12 = sb("w12", [P, TOP_K, NT])
        pos = sb("pos", [P, TOP_K, NT], I32)
        tile_expert = sb("tile_expert", [1, whole_turns], I32)
        tile_changed = sb("tile_changed", [1, whole_turns], I32)
        token_of = sb("token_of", [P, slots], I32)
        s_ident = ctx.enter_context(nc.semaphore("s_ident"))
        s_go = ctx.enter_context(nc.semaphore("s_go"))

        with nc.Block() as block:
            @block.gpsimd
            def _(e):
                e.memset(ident[:, :], 0.0).then_inc(s_ident, 1)
                e.wait_ge(s_ident, 1)
                e.affine_select(out=ident[:, :], in_=ident[:, :], compare_op=ALU.not_equal, fill=1.0,
                                base=0, pattern=[[-1, P]], channel_multiplier=1).then_inc(s_ident, 1)
                e.wait_ge(s_ident, 2)
                e.sem_inc(s_go, 1)

        attention_stage(nc, x, ctx_t, (wq_t, wk_t, wv_t, wo_t), bq, bk, bv, bo, router_w, router_b, x2_dram, xln_dram, logits, ident, s_go)
        routing_stage(nc, logits, T, w12, pos, tile_expert, tile_changed, token_of, whole_turns)
        expert_stage(nc, xln_dram, y_dram, w_gate_up, w_down, b_gate_up, b_down, tile_expert, tile_changed, token_of, ident, n_tiles, s_go)
        combine_stage(nc, x2_dram, y_dram, out, w12, pos, s_go)


_INS = ["x", "ctx_t", "wq_t", "bq", "wk_t", "bk", "wv_t", "bv", "wo_t", "bo", "router_w", "router_b",
        "w_gate_up", "b_gate_up", "w_down", "b_down"]


def kernel(**i):
    import numpy as np
    import concourse.bacc as bacc
    from concourse.bass_utils import run_bass_kernel_spmd

    lay = np.ascontiguousarray
    a = {k: np.asarray(v) for k, v in i.items()}
    column = lambda v: lay(v.reshape(-1, P).T)
    gub = a["L0_ffn_gate_up_bias"]
    arrays = {
        "x": lay(a["x"]),
        "ctx_t": lay(a["ctx_1024"].transpose(0, 2, 1)),
        "wq_t": lay(a["L0_xattn_Wq"].T), "wk_t": lay(a["L0_xattn_Wk"].T),
        "wv_t": lay(a["L0_xattn_Wv"].T), "wo_t": lay(a["L0_xattn_Wo"].T),
        "bq": column(a["L0_xattn_bq"]), "bk": column(a["L0_xattn_bk"]),
        "bv": lay(a["L0_xattn_bv"]), "bo": lay(a["L0_xattn_bo"]),
        "router_w": lay(a["L0_ffn_router_weight"]), "router_b": lay(a["L0_ffn_router_bias"]),
        "w_gate_up": lay(a["L0_ffn_gate_up_proj"]),
        "b_gate_up": lay(gub.reshape(gub.shape[0], -1, P).transpose(0, 2, 1)),
        "w_down": lay(a["L0_ffn_down_proj"]), "b_down": lay(a["L0_ffn_down_bias"]),
    }
    nc = bacc.Bacc("TRN2", target_bir_lowering=False, num_devices=1)
    args = [nc.dram_tensor(n, arrays[n].shape, mybir.dt.from_np(arrays[n].dtype), kind="ExternalInput").ap() for n in _INS]
    out = nc.dram_tensor("out", arrays["x"].shape, F32, kind="ExternalOutput").ap()
    build(nc, *args, out)
    r = run_bass_kernel_spmd(nc, [arrays], core_ids=[0])
    return r.results[0]["out"]
```

```python
from contextlib import ExitStack

import concourse.bass as bass
from concourse import mybir

ALU = mybir.AluOpType
ACT = mybir.ActivationFunctionType
AX = mybir.AxisListType
F32 = mybir.dt.float32
F32R = mybir.dt.float32r
BF16 = mybir.dt.bfloat16
I32 = mybir.dt.int32
U32 = mybir.dt.uint32

P = 128
LN_EPS = 1e-5
HEADS = 16
GROUP = 4
HD = 32
TOP_K = 2
ALPHA = 1.702
LIMIT = 7.0
FTOK = 256


class Count:

    def __init__(self, sem, step=1, ahead=1):
        self.sem, self.step, self.per_turn, self.ahead = sem, step, 0, ahead

    def did(self):
        self.per_turn += self.step
        return self.per_turn

    def open(self, eng, first_turn=0):
        eng.sem_inc(self.sem, (first_turn + 1) * self.per_turn)

    def wait(self, eng, turn, mark, go=None):
        self._wait(eng, turn * self.per_turn + (self.ahead * self.per_turn + mark), go)

    def wait_before(self, eng, turn, mark, go=None):
        self._wait(eng, turn * self.per_turn + mark, go)

    def _wait(self, eng, value, go):
        if go is not None:
            value = value if isinstance(value, int) else eng.to_reg(value)
            eng.wait_ge(go, 1)
        eng.wait_ge(self.sem, value)


class Turn:

    def __init__(self, sem, tag):
        self.q = {n: [] for n in ("sp", "act", "dve", "pe", "pool")}
        self.count = {n: Count(sem(f"{tag}_{n}")) for n in ("act", "dve", "pe", "pool")}
        self.act, self.dve, self.pe, self.pool = self.count.values()
        self.marks = {}

    def step(self, engine, waits, emit, go=None):
        count = self.count[engine]

        def f(e, turn):
            for c, m in waits:
                c.wait(e, turn, m, go)
            emit(e).then_inc(count.sem, 1)
        self.q[engine].append(f)
        return count, count.did()

    def run(self, engine, eng, turn):
        for f in self.q[engine]:
            f(eng, turn)


def attention_stage(nc, x, ctx_t, w_t, bq, bk, bv, bo, router_wt, router_b, x2_dram, xln_dram, logits, ident, s_go):
    B, S, D = x.shape
    C = D // P
    T = S // P
    E = router_wt.shape[1]
    scale = 1.0 / float(HD) ** 0.5

    with ExitStack() as ctx:
        sb = lambda name, shape, dt=F32: ctx.enter_context(nc.sbuf_tensor(name, shape, dt))
        psum = lambda name, shape: ctx.enter_context(nc.psum_tensor(name, shape, F32))
        sem = lambda name: ctx.enter_context(nc.semaphore(name))

        wk, wv = sb("wk", [P, C, D]), sb("wv", [P, C, D])
        wq, wo = ([sb(f"{n}_{part}", [P, C, D], F32R) for part in ("hi", "lo")] for n in ("wq", "wo"))
        PASSES = ((0, 0), (0, 1), (1, 0))
        rw_cols = sb("rw_cols", [P, C, HD])
        select = sb("select", [P, E])
        rb_rows = sb("rb_rows", [P, E])
        bv_rows = sb("bv_rows", [P, D])
        bo_rows = sb("bo_rows", [P, D])
        bq_col = sb("bq_col", [P, C])
        bk_col = sb("bk_col", [P, C])
        x_in = sb("x_in", [P, T, D])
        x2 = sb("x2", [P, T, D])
        ctxT = sb("ctxT", [P, C, S])
        hi = {n: [sb(f"{n}_hi{i}", [P, S], F32R) for i in range(2)] for n in "qk"}
        lo = {n: [sb(f"{n}_lo{i}", [P, S], F32R) for i in range(2)] for n in "qk"}
        qs = [sb(f"qs{c}", [P, GROUP, S], F32R) for c in range(C)]
        ks = [sb(f"ks{c}", [P, GROUP, S], F32R) for c in range(C)]
        v = sb("v", [P, T, D])
        pt = [sb("pt0", [P, GROUP, S])]
        pt1_at = nc.sbuf_base
        pt.append(sb("pt1", [P, GROUP, S]))
        oT_at = nc.sbuf_base
        oT_hi = sb("oT_hi", [P, C, S], F32R)
        xT_hi = sb("xT_hi", [P, C, S], F32R)
        xT = [xT_hi, nc.alloc_sbuf_tensor_at("xT_lo", [P, C, S], F32R, offset=pt1_at)]
        oT = [oT_hi, xT_hi]
        xln = nc.alloc_sbuf_tensor_at("xln", [P, T, D], F32, offset=oT_at)
        o_sum = sb("o_sum", [P, 2, S])
        parts = sb("parts", [P, S])
        ones = sb("ones", [P, HD])
        negmax = sb("negmax", [P, C, GROUP * T])
        m_hi = sb("m_hi", [GROUP * T, P], F32R)
        m_lo = sb("m_lo", [GROUP * T, P], F32R)
        stats = sb("stats", [P, 2, T, 6])
        mv = sb("mv", [P, 2, T, 2])
        var_eps = sb("var_eps", [P, 2, T])
        rstd = sb("rstd", [P, 2, T])
        minus_half = sb("minus_half", [P, T])
        eps_col = sb("eps_col", [P, T])

        work = [psum(f"work{i}", [P, S]) for i in range(2)]
        st = [psum(f"st{i}", [P, 2, S]) for i in range(2)]
        o_ps = psum("o_ps", [P, S])
        sum_ps = psum("sum_ps", [P, S])

        s_const = sem("s_const")
        s_init = sem("s_init")
        s_first_x, s_raw_w = sem("s_first_x"), sem("s_raw_w")
        s_split, s_split_lo = sem("s_split"), sem("s_split_lo")
        g = Turn(sem, "att")
        pe, act, dve, pool = g.pe, g.act, g.dve, g.pool
        x_load, ctx_load, res_load = (Count(sem(n), 16) for n in ("s_x", "s_ctx", "s_res"))
        stack = [Count(sem(f"s_stack{c}"), 16) for c in range(C)]
        stack_lo = [Count(sem(f"s_stack_lo{c}"), 16, ahead=0) for c in range(C)]
        mrow = [Count(sem(f"s_mrow{c}"), 16, ahead=0) for c in range(C)]
        x2_store, xln_store = Count(sem("s_x2"), 16), Count(sem("s_xln"), 16)

        marks = g.marks
        last_used = {"work": 1, "st": 1}
        last_reader = {}

        def take(ring, i=None):
            i = 1 - last_used[ring] if i is None else i
            last_used[ring] = i
            key = (ring, i)
            if key in last_reader:
                g.q["pe"].append(lambda e, b, f=last_reader[key]: f[0].wait(e, b, f[1]))
            else:
                g.q["pe"].append(lambda e, b: last_reader[key][0].wait_before(e, b, last_reader[key][1]))
            return i

        def take_bank():
            return take("work")

        def free_bank(i, count, mark):
            last_reader["work", i] = (count, mark)

        light = []

        def gap(n=1):
            for _ in range(n):
                if light:
                    step, *args = light.pop(0)
                    step(*args)

        def norm_stats(g, src, slot, t, first_wait=None):
            def f(e, b):
                if first_wait:
                    first_wait(e, b)
                e.bn_stats(stats[:, slot, t, :], src[:, t, :]).then_inc(g.dve.sem, 1)
            g.q["dve"].append(f)
            g.marks["bn", slot, t] = g.dve.did()

        def norm_rstd(g, slot):
            for t in range(T):
                g.marks["mv", slot] = g.step("dve", [(g.dve, g.marks["bn", slot, t])],
                                             lambda e, t=t: e.bn_aggr(mv[:, slot, t, :], stats[:, slot, t, :]), s_go)
            r = g.step("pool", [g.marks["mv", slot]],
                       lambda e: e.tensor_tensor(var_eps[:, slot, :], mv[:, slot, :, 1], eps_col[:, :], ALU.add))
            g.marks["rstd", slot] = g.step("pool", [r], lambda e: e.tensor_tensor(rstd[:, slot, :], var_eps[:, slot, :],
                                                                                 minus_half[:, :], ALU.pow))

        def norm_apply(g, dst, src, slot, t, first_wait):
            def f(e, b):
                first_wait(e, b)
                e.tensor_scalar(dst[:, t, :], src[:, t, :], mv[:, slot, t, 0:1], rstd[:, slot, t:t + 1],
                                ALU.subtract, ALU.mult).then_inc(g.dve.sem, 1)
            g.q["dve"].append(f)
            return g.dve.did()

        def transpose_x():
            for half in range(C // 2):
                take("st", half)
                def f(e, b, half=half):
                    dve.wait_before(e, b, marks["ln1"])
                    for j in range(2):
                        c = 2 * half + j
                        for t in range(T):
                            ins = e.transpose(st[half][:, j, t * P:(t + 1) * P], x_in[:, t, c * P:(c + 1) * P], ident[:, :])
                    ins.then_inc(pe.sem, 1)
                g.q["pe"].append(f)
                done = pe.did()
                chunks = slice(2 * half, 2 * half + 2)
                hi_made = g.step("act", [(pe, done)], lambda e, half=half, chunks=chunks: e.activation(
                    xT[0][:, chunks, :], st[half][:, :, :], ACT.Identity))
                last_reader["st", half] = g.step("dve", [hi_made], lambda e, half=half, chunks=chunks: e.tensor_tensor(
                    xT[1][:, chunks, :], st[half][:, :, :], xT[0][:, chunks, :].bitcast(F32), ALU.subtract))
            marks["x_turned"] = done
            marks["xT"] = dve.per_turn

        def project_qk(name, c):
            bias = bq_col if name == "q" else bk_col
            i = take_bank()
            for k in range(C):
                def f(e, b, k=k):
                    if k == 0 and name == "q":
                        dve.wait(e, b, marks["xT"])
                    elif k == 0:
                        ctx_load.wait_before(e, b, marks["ctx_next"])
                    products = [(wk[:, k, :], ctxT)] if name == "k" else [(wq[pw][:, k, :], xT[px]) for pw, px in PASSES]
                    for n, (w, src) in enumerate(products):
                        ins = e.matmul(work[i][:, :], w[:, c * P:(c + 1) * P], src[:, k, :],
                                       start=(k == 0 and n == 0), stop=(k == C - 1 and n == len(products) - 1))
                    if k == C - 1:
                        ins.then_inc(pe.sem, 1)
                g.q["pe"].append(f)
                if k < C - 1:
                    gap()
            done = pe.did()
            h, l = hi[name][c % 2], lo[name][c % 2]
            def on_act(e, b):
                pe.wait(e, b, done)
                if c >= 2:
                    stack[c - 2].wait(e, b, marks["stack", c - 2])
                else:
                    pe.wait_before(e, b, marks["c_end", c + 2])
                e.activation(h[:, :], work[i][:, :], ACT.Identity, bias=bias[:, c:c + 1]).then_inc(act.sem, 1)
            g.q["act"].append(on_act)
            h_done = act.did()
            def d(e, b):
                act.wait(e, b, h_done)
                if c >= 2:
                    stack_lo[c - 2].wait(e, b, marks["stack_lo", c - 2])
                e.scalar_tensor_tensor(out=l[:, :], in0=work[i][:, :], scalar=bias[:, c:c + 1], in1=h[:, :].bitcast(F32),
                                       op0=ALU.add, op1=ALU.subtract).then_inc(dve.sem, 1)
            g.q["dve"].append(d)
            l_done = dve.did()
            free_bank(i, dve, l_done)
            dst = qs[c] if name == "q" else ks[c]
            hi_parts, lo_part = ((0, 1), 2) if name == "q" else ((0, 2), 1)
            def rows_to(e, part, src, semaphore):
                for r in range(GROUP):
                    e.dma_start(dst[HD * part:HD * (part + 1), r, :].bitcast(F32),
                                src[HD * r:HD * (r + 1), :].bitcast(F32)).then_inc(semaphore, 16)
            def s(e, b):
                act.wait(e, b, h_done, s_go)
                pe.wait_before(e, b, marks["c_end", c], s_go)
                for part in hi_parts:
                    rows_to(e, part, h, stack[c].sem)
            g.q["sp"].append(s)
            for _ in range(2 * GROUP):
                marks["stack", c] = stack[c].did()
            def on_pool(e, b):
                dve.wait(e, b, l_done, s_go)
                pe.wait_before(e, b, marks["c_end", c], s_go)
                rows_to(e, lo_part, l, stack_lo[c].sem)
            g.q["pool"].append(on_pool)
            for _ in range(GROUP):
                marks["stack_lo", c] = stack_lo[c].did()
            gap()

        def project_v(c):
            i = take_bank()
            for t in range(T):
                def f(e, b, t=t):
                    if t == 0:
                        ctx_load.wait_before(e, b, marks["ctx_next"])
                    for k in range(C):
                        ins = e.matmul(work[i][:, t * P:(t + 1) * P], ctxT[:, k, t * P:(t + 1) * P],
                                       wv[:, k, c * P:(c + 1) * P], start=(k == 0), stop=(k == C - 1))
                    if t == T - 1:
                        ins.then_inc(pe.sem, 1)
                g.q["pe"].append(f)
                if t < T - 1:
                    gap()
            done = pe.did()
            def d(e, b):
                pe.wait(e, b, done)
                e.tensor_tensor(v[:, :, c * P:(c + 1) * P], work[i][:, :].rearrange("p (t n) -> p t n", t=T),
                                bv_rows[:, c * P:(c + 1) * P].unsqueeze(1).to_broadcast([P, T, P]), ALU.add).then_inc(dve.sem, 1)
            g.q["dve"].append(d)
            marks["v", c] = dve.did()
            free_bank(i, dve, marks["v", c])
            gap()

        def row_max(c, h, t, n=1):
            i = take("st") if n == 2 else take("work")
            bank = st[i] if n == 2 else work[i][:, :].unsqueeze(1)
            def f(e, b):
                stack[c].wait(e, b, marks["stack", c])
                stack_lo[c].wait(e, b, marks["stack_lo", c])
                for j in range(n):
                    ins = e.matmul(bank[:, j, :], qs[c][0:3 * HD, h, (t + j) * P:(t + j + 1) * P], ks[c][0:3 * HD, h, :],
                                   start=True, stop=True)
                ins.then_inc(pe.sem, 1)
            g.q["pe"].append(f)
            done = pe.did()
            def d(e, b):
                pe.wait(e, b, done)
                e.tensor_reduce(negmax[:, c, h * T + t:h * T + t + n], bank[:, 0:n, :], AX.X, ALU.max,
                                negate=True).then_inc(dve.sem, 1)
            g.q["dve"].append(d)
            marks["max", c] = dve.did()
            last_reader["st" if n == 2 else "work", i] = (dve, marks["max", c])

        def turn_max(c, ring="work"):
            i = take(ring)
            bank = st[i][:, 0, :] if ring == "st" else work[i]
            R = GROUP * T
            def f(e, b):
                dve.wait(e, b, marks["max", c])
                e.transpose(bank[0:R, 0:P], negmax[:, c, :], ident[:, :]).then_inc(pe.sem, 1)
            g.q["pe"].append(f)
            done = pe.did()
            def on_act(e, b):
                pe.wait(e, b, done)
                if c:
                    mrow[c - 1].wait(e, b, marks["mrow", c - 1])
                else:
                    pe.wait_before(e, b, marks["c_end", C - 1])
                e.activation(m_hi[:, :], bank[0:R, 0:P], ACT.Identity).then_inc(act.sem, 1)
            g.q["act"].append(on_act)
            h_done = act.did()
            def d(e, b):
                act.wait(e, b, h_done)
                e.tensor_tensor(m_lo[:, :], bank[0:R, 0:P], m_hi[:, :].bitcast(F32), ALU.subtract).then_inc(dve.sem, 1)
            g.q["dve"].append(d)
            l_done = dve.did()
            last_reader[ring, i] = (dve, l_done)
            def send_rows(e, b):
                dve.wait(e, b, l_done, s_go)
                pe.wait_before(e, b, marks["c_end", c], s_go)
                for row, src in ((3 * HD, m_hi), (3 * HD + 1, m_lo)):
                    e.dma_start(qs[c][row:row + 1, :, :].rearrange("a h n -> a (h n)").bitcast(F32),
                                src[:, :].bitcast(F32)).then_inc(mrow[c].sem, 16)
            g.q["sp" if c >= 2 else "pool"].append(send_rows)
            mrow[c].did()
            marks["mrow", c] = mrow[c].did()

        exp_marks = []
        pv_marks = []

        def exp_scores(c, k):
            n = c * T + k
            for p in range(2):
                take("st", p)
                def f(e, b, p=p):
                    if p == 0 and k == 0:
                        mrow[c].wait(e, b, marks["mrow", c])
                    for j in range(2):
                        h = 2 * p + j
                        ins = e.matmul(st[p][:, j, :], ks[c][0:3 * HD + 2, h, k * P:(k + 1) * P],
                                       qs[c][0:3 * HD + 2, h, :], start=True, stop=True)
                    ins.then_inc(pe.sem, 1)
                g.q["pe"].append(f)
                done = pe.did()
                def on_act(e, b, p=p, done=done):
                    pe.wait(e, b, done)
                    if n >= 2:
                        pe.wait(e, b, pv_marks[n - 2])
                    else:
                        pe.wait_before(e, b, pv_marks[n - 2 + C * T])
                    e.activation(pt[k % 2][:, 2 * p:2 * p + 2, :], st[p][:, :, :], ACT.Exp, scale=scale).then_inc(act.sem, 1)
                g.q["act"].append(on_act)
                exp_marks.append(act.did())
                last_reader["st", p] = (act, exp_marks[-1])
                gap()

        def weigh_values(c, k):
            n = c * T + k
            def values(e, b):
                if k == 0:
                    dve.wait(e, b, marks["v", c])
                    if c:
                        act.wait(e, b, marks["copied", c - 1, 0])
                    else:
                        act.wait_before(e, b, marks["copied", C - 1, 0])
                act.wait(e, b, exp_marks[2 * n + 1])
                for h in range(GROUP):
                    rows = slice(HD * h, HD * (h + 1))
                    e.matmul(o_ps[rows, :], v[:, k, c * P + HD * h:c * P + HD * (h + 1)], pt[k % 2][:, h, :],
                             start=(k == 0), stop=(k == T - 1))
            g.q["pe"].append(values)
            gap()
            def sums(e, b):
                for h in range(GROUP):
                    rows = slice(HD * h, HD * (h + 1))
                    ins = e.matmul(sum_ps[rows, :], ones[:, :], pt[k % 2][:, h, :], start=(k == 0), stop=(k == T - 1))
                ins.then_inc(pe.sem, 1)
            g.q["pe"].append(sums)
            pv_marks.append(pe.did())

        pieces = []

        def piece(n=1):
            for _ in range(n):
                if pieces:
                    pieces.pop(0)()

        def normalise(c):
            done = marks["c_end", c] = pv_marks[c * T + T - 1]
            for i, src in ((1, sum_ps), (0, o_ps)):
                def on_act(e, b, i=i, src=src):
                    pe.wait(e, b, done)
                    if c:
                        dve.wait(e, b, marks["norm", c - 1, T - 1])
                    else:
                        dve.wait_before(e, b, marks["norm", C - 1, T - 1])
                    e.activation(o_sum[:, i, :], src[:, :], ACT.Identity).then_inc(act.sem, 1)
                g.q["act"].append(on_act)
                marks["copied", c, i] = act.did()
            def divide(t):
                cols = slice(t * P, (t + 1) * P)
                r = g.step("dve", [(act, marks["copied", c, 1])],
                           lambda e: e.reciprocal(o_sum[:, 1, cols], o_sum[:, 1, cols]))
                marks["divided", c, t] = g.step("dve", [(act, marks["copied", c, 0]), r], lambda e: e.tensor_tensor(
                    o_sum[:, 0, cols], o_sum[:, 0, cols], o_sum[:, 1, cols], ALU.mult))

            def split(t):
                cols = slice(t * P, (t + 1) * P)
                def to_hi(e, b):
                    dve.wait(e, b, marks["divided", c, t][1])
                    if c == 0:
                        xln_store.wait(e, b, marks["xln_store"])
                    e.activation(oT[0][:, c, cols], o_sum[:, 0, cols], ACT.Identity).then_inc(act.sem, 1)
                g.q["act"].append(to_hi)
                hi_made = (act, act.did())
                marks["norm", c, t] = g.step("dve", [hi_made], lambda e: e.tensor_tensor(
                    oT[1][:, c, cols], o_sum[:, 0, cols], oT[0][:, c, cols].bitcast(F32), ALU.subtract))[1]

            late = 0 if c == C - 1 else 1
            for t in range(T + late):
                def both(t=t):
                    if t < T:
                        divide(t)
                    if t >= late:
                        split(t - late)
                pieces.append(both)

        def project_out():
            banks = []
            for t in range(T):
                ring = "work" if t < 2 else "st"
                i = take(ring)
                banks.append(((ring, i), st[i][:, 0, :] if ring == "st" else work[i][:, :]))
            for chunks in (range(C - 1), range(C - 1, C)):
                for t in range(T):
                    def f(e, b, t=t, chunks=chunks):
                        for c in chunks:
                            if c == C - 1:
                                dve.wait(e, b, marks["norm", c, t])
                            elif t == 0:
                                dve.wait(e, b, marks["norm", c, T - 1])
                            for n, (po, pw) in enumerate(PASSES):
                                ins = e.matmul(banks[t][1], oT[po][:, c, t * P:(t + 1) * P], wo[pw][:, c, :],
                                               start=(c == 0 and n == 0), stop=(c == C - 1 and n == len(PASSES) - 1))
                        if chunks[-1] == C - 1:
                            ins.then_inc(pe.sem, 1)
                    g.q["pe"].append(f)
                    if chunks[-1] == C - 1:
                        add_residual(t, *banks[t])
            for t in range(T):
                norm_stats(g, x2, 1, t, lambda e, b, t=t: dve.wait(e, b, marks["x2", t]))

        def add_residual(t, key, bank):
            done = pe.did()
            def d(e, b):
                pe.wait(e, b, done)
                pool.wait(e, b, marks["x_bo"])
                e.tensor_tensor(x2[:, t, :], bank, x2[:, t, :], ALU.add).then_inc(dve.sem, 1)
            g.q["dve"].append(d)
            marks["x2", t] = dve.did()
            marks["out_pe"] = done
            last_reader[key] = (dve, marks["x2", t])

        def post_apply(g, t, first_wait=None):
            g.marks["ln2", t] = norm_apply(g, xln, x2, 1, t, first_wait)

        def post_turn(g, half, taken=lambda *ring: None):
            taken("st", half)
            def f(e, b):
                for j in range(2):
                    c = 2 * half + j
                    for t in range(T):
                        if j == 0:
                            g.dve.wait(e, b, g.marks["ln2", t])
                        ins = e.transpose(st[half][:, j, t * P:(t + 1) * P], xln[:, t, c * P:(c + 1) * P], ident[:, :])
                ins.then_inc(g.pe.sem, 1)
            g.q["pe"].append(f)
            turned = (g.pe, g.pe.did())
            g.marks["turned", half] = g.step("act", [turned], lambda e: e.activation(
                pt[0][:, 2 * half:2 * half + 2, :], st[half][:, :, :], ACT.Identity))

        def post_logits(g, bank):
            def f(e, b):
                g.act.wait(e, b, g.marks["turned", 1][1])
                for c in range(C):
                    ins = e.matmul(st[bank][HD * c:HD * (c + 1), 0, :], rw_cols[:, c, :], pt[0][:, c, :], start=True, stop=True)
                ins.then_inc(g.pe.sem, 1)
            g.q["pe"].append(f)
            made = (g.pe, g.pe.did())
            g.marks["parts"] = g.step("act", [made], lambda e: e.activation(parts[:, :], st[bank][:, 0, :], ACT.Identity))
            return g.marks["parts"]

        def post_sum(g, bank):
            def f(e, b):
                g.act.wait(e, b, g.marks["parts"][1])
                for t in range(T):
                    ins = e.matmul(st[bank][:, 0, t * E:(t + 1) * E], parts[:, t * P:(t + 1) * P], select[:, :], start=True, stop=True)
                ins.then_inc(g.pe.sem, 1)
            g.q["pe"].append(f)
            done = g.pe.did()
            def d(e, b):
                g.pe.wait(e, b, done)
                e.tensor_tensor(logits[:, bass.ds(b * T, T), :], st[bank][:, 0, 0:T * E].rearrange("p (t n) -> p t n", t=T),
                                rb_rows[:, :].unsqueeze(1).to_broadcast([P, T, E]), ALU.add).then_inc(g.dve.sem, 1)
            g.q["dve"].append(d)
            return g.dve, g.dve.did()

        def post_store(g, xln_store, x2_store):
            def s(e, b):
                g.dve.wait(e, b, g.marks["ln2", T - 1], s_go)
                e.dma_start(xln_dram[bass.ds(b, 1), :, :].rearrange("a (t p) n -> p (a t) n", p=P), xln[:, :, :]).then_inc(xln_store.sem, 16)
                e.dma_start(x2_dram[bass.ds(b, 1), :, :].rearrange("a (t p) n -> p (a t) n", p=P), x2[:, :, :]).then_inc(x2_store.sem, 16)
            g.q["sp"].append(s)
            g.marks["xln_store"] = xln_store.did()
            g.marks["x2_store"] = x2_store.did()

        def load_ctx():
            def s(e, b):
                pe.wait(e, b, marks["proj_end"], s_go)
                e.dma_start(ctxT[:, :, :], ctx_t[bass.ds((b + 1) % B, 1), :, :].rearrange("a (c p) n -> p (a c) n", p=P)).then_inc(ctx_load.sem, 16)
            g.q["sp"].append(s)

        def load_x():
            def s(e, b):
                pe.wait(e, b, marks["x_turned"], s_go)
                e.dma_start(x_in[:, :, :], x[bass.ds((b + 1) % B, 1), :, :].rearrange("a (t p) n -> p (a t) n", p=P)).then_inc(x_load.sem, 16)
            g.q["sp"].append(s)
            marks["x_load"] = x_load.did()

        def load_residual():
            def s(e, b):
                x2_store.wait(e, b, marks["x2_store"], s_go)
                dve.wait(e, b, marks["ln2", T - 1], s_go)
                e.dma_start(x2[:, :, :], x[bass.ds(b, 1), :, :].rearrange("a (t p) n -> p (a t) n", p=P)).then_inc(res_load.sem, 16)
            g.q["sp"].append(s)
            marks["res_load"] = res_load.did()

        def add_bias():
            def on_pool(e, b):
                res_load.wait(e, b, marks["res_load"])
                e.tensor_tensor(x2[:, :, :], x2[:, :, :], bo_rows[:, :].unsqueeze(1).to_broadcast([P, T, D]), ALU.add).then_inc(pool.sem, 1)
            g.q["pool"].append(on_pool)
            marks["x_bo"] = pool.did()

        transpose_x()
        load_x()

        def ln2_ready(e, b):
            pool.wait_before(e, b, marks["rstd", 1][1])
            pe.wait_before(e, b, marks["out_pe"])

        def with_bank(step):
            i = take("st")
            last_reader["st", i] = step(g, i)

        def post_turn_half(half):
            post_turn(g, half, take)
            last_reader["st", half] = marks["turned", half]

        for t in range(T):
            post_apply(g, t, ln2_ready)
        wait, rest = (lambda: None,), (piece,)
        row_pairs = lambda c: [(row_max, c, h, t, 2) for h in range(GROUP) for t in range(0, T, 2)]
        row_tiles = lambda c: [(row_max, c, h, t) for h in range(GROUP) for t in range(T)]
        light += [wait] * 7 + [(post_turn_half, 0), wait, (post_turn_half, 1), wait, wait, (with_bank, post_logits)]
        light += [wait] * 3 + [(with_bank, post_sum)]
        for c in range(C):
            if c == 2:
                assert not light
                light += [wait] + row_pairs(0) + [wait] * 3
            elif c == 3:
                light += [(turn_max, 0, "st")] + [wait] + row_pairs(1)
            for step in ("kvq" if c == 0 else "qkv"):
                if step == "v":
                    project_v(c)
                else:
                    project_qk(step, c)
            if c == 1:
                post_store(g, xln_store, x2_store)
        gap(len(light))
        marks["proj_end"] = pe.per_turn
        load_ctx()
        load_residual()
        r2, r3 = row_tiles(2), row_tiles(3)
        light += [(turn_max, 1)] + r2 + [(turn_max, 2)]
        for n in range(T + 1):
            light += [r3.pop(0), rest] + ([r3.pop(0)] if n < T else [])
        light += r3 + [(turn_max, 3)] + [rest] * (T + 1) + [wait] * 3 + [rest] * (T + 1)
        tiles = [(c, k) for c in range(C) for k in range(T)]
        exp_scores(*tiles[0])
        for n, (c, k) in enumerate(tiles):
            if n + 1 < len(tiles):
                exp_scores(*tiles[n + 1])
            weigh_values(c, k)
            if k == T - 1:
                piece(len(pieces))
                normalise(c)
            gap()
            if c == C - 1 and k == 1:
                for t in range(T):
                    norm_stats(g, x_in, 0, t, lambda e, b: x_load.wait(e, b, marks["x_load"]))
                norm_rstd(g, 0)
            if c == C - 1 and k == 2:
                for t in range(T):
                    marks["ln1"] = norm_apply(g, x_in, x_in, 0, t, lambda e, b: pool.wait(e, b, marks["rstd", 0][1]))
        gap(len(light))
        add_bias()
        piece(len(pieces))
        project_out()
        norm_rstd(g, 1)
        marks["ctx_next"] = ctx_load.did()

        head = Turn(sem, "head")
        for t in range(T):
            norm_stats(head, x_in, 0, t, lambda e, b: e.wait_ge(s_first_x, 16))
        norm_rstd(head, 0)
        for t in range(T):
            norm_apply(head, x_in, x_in, 0, t, lambda e, b: head.pool.wait(e, b, head.marks["rstd", 0][1]))
        tail = Turn(sem, "tail")
        tail_xln, tail_x2 = Count(sem("tail_xln"), 16), Count(sem("tail_x2"), 16)
        for t in range(T):
            post_apply(tail, t, lambda e, b: None)
        post_turn(tail, 0)
        post_turn(tail, 1)
        post_logits(tail, 0)
        post_sum(tail, 1)
        post_store(tail, tail_xln, tail_x2)

        first = [(x_in[:], x[0].rearrange("(t p) n -> p t n", p=P), s_first_x)]
        first += [(raw[:], w_t[i].rearrange("(c p) n -> p c n", p=P), s_raw_w) for i, raw in ((0, pt[0]), (3, pt[1]))]
        consts = [(dst[:], src.rearrange("(c p) n -> p c n", p=P)) for dst, src in ((wk, w_t[1]), (wv, w_t[2]), (ctxT, ctx_t[0]))]
        consts += [(bq_col[:], bq), (bk_col[:], bk)]
        rows = [(bv_rows[:, :], bv), (bo_rows[:, :], bo), (rb_rows[:, :], router_b)]
        N_ROUTER = 1
        N_CONST = 16 * (len(consts) + len(rows) + 1)

        with nc.Block() as block:
            @block.sync
            def _(e):
                for dst, src, semaphore in first:
                    e.dma_start(dst, src).then_inc(semaphore, 16)
                for dst, src in consts:
                    e.dma_start(dst, src).then_inc(s_const, 16)
                e.wait_ge(s_init, N_ROUTER)
                e.dma_start(rw_cols[:, :, 0:E], router_wt.rearrange("(c p) e -> p c e", p=P)).then_inc(s_const, 16)
                for dst, src in rows:
                    e.dma_start(dst, src.partition_broadcast(P)).then_inc(s_const, 16)
                e.wait_ge(s_const, N_CONST)

            @block.gpsimd
            def _(e):
                head.pool.open(e)
                fills = [(rw_cols[:, :, :], 0.0), (select[:, :], 0.0), (minus_half[:, :], -0.5), (eps_col[:, :], LN_EPS), (ones[:, :], 1.0), (x2[:, :, :], 0.0)]
                fills += [(mv[:, 1, :, :], 0.0), (rstd[:, 1, :], 0.0)]
                fills += [(ks[c][3 * HD:P, :, :].bitcast(F32), 1.0) for c in range(C)]
                for n, (dst, value) in enumerate(fills):
                    e.memset(dst, value).then_inc(s_init, 1)
                    e.wait_ge(s_init, n + 1)
                for c in range(C):
                    e.affine_select(out=select[:, :], in_=select[:, :], compare_op=ALU.not_equal, fill=1.0,
                                    base=-HD * c, pattern=[[-1, E]], channel_multiplier=1).then_inc(s_init, 1)
                    e.wait_ge(s_init, len(fills) + c + 1)
                head.run("pool", e, 0)

            @block.scalar
            def _(e):
                e.wait_ge(s_raw_w, 32)
                for w, raw in ((wq, pt[0]), (wo, pt[1])):
                    e.activation(w[0][:, :, :], raw[:, :, :], ACT.Identity).then_inc(s_split, 1)

            @block.vector
            def _(e):
                head.dve.open(e)
                head.run("dve", e, 0)
                for n, (w, raw) in enumerate(((wq, pt[0]), (wo, pt[1]))):
                    e.wait_ge(s_split, n + 1)
                    e.tensor_tensor(w[1][:, :, :], raw[:, :, :], w[0][:, :, :].bitcast(F32), ALU.subtract).then_inc(s_split_lo, 1)
                e.wait_ge(s_split_lo, 2)

        with nc.Block() as block:
            @block.sync
            def _(e):
                for c in (x_load, ctx_load, res_load, x2_store, xln_store, *stack):
                    c.open(e)
                with e.Fori(0, B) as b:
                    g.run("sp", e, b)
                ctx_load.wait(e, B - 1, marks["ctx_next"])
                xln_store.wait(e, B - 1, marks["xln_store"])
                x2_store.wait(e, B - 1, marks["x2_store"])

            for name, run in (("gpsimd", "pool"), ("vector", "dve"), ("scalar", "act"), ("tensor", "pe")):
                deco = {"gpsimd": block.gpsimd, "vector": block.vector, "scalar": block.scalar, "tensor": block.tensor}[name]

                @deco
                def _(e, run=run):
                    {"pool": pool, "dve": dve, "act": act, "pe": pe}[run].open(e)
                    with e.Fori(0, B) as b:
                        g.run(run, e, b)

        with nc.Block() as block:
            @block.sync
            def _(e):
                tail_xln.open(e, B)
                tail_x2.open(e, B)
                tail.run("sp", e, B)
                tail_xln.wait(e, B, tail.marks["xln_store"])
                tail_x2.wait(e, B, tail.marks["x2_store"])

            @block.vector
            def _(e):
                tail.dve.open(e, B)
                tail.run("dve", e, B)

            @block.scalar
            def _(e):
                tail.act.open(e, B)
                tail.run("act", e, B)

            @block.tensor
            def _(e):
                tail.pe.open(e, B)
                tail.run("pe", e, B)


def routing_stage(nc, logits, skip, w12, pos, tile_expert, tile_changed, token_of, n_tiles, first_loads):
    NT, E = logits.shape[1] - skip, logits.shape[2]
    KT = TOP_K * NT
    SLOTS = token_of.shape[1]
    SHIFT = P.bit_length() - 1
    TILE_SHIFT = FTOK.bit_length() - 1

    with ExitStack() as ctx:
        sb = lambda name, shape, dt=F32: ctx.enter_context(nc.sbuf_tensor(name, shape, dt))
        psum = lambda name, shape: ctx.enter_context(nc.psum_tensor(name, shape, F32))
        sem = lambda name: ctx.enter_context(nc.semaphore(name))
        g = Turn(sem, "route")

        iota_i = sb("iota_i", [P, P], I32)
        part_i = sb("part_i", [P, 1], I32)
        iota_f = sb("iota_f", [P, P])
        iota_b = sb("iota_b", [P, P], BF16)
        part_f = sb("part_f", [P, 1])
        expert_less = sb("expert_less", [P, E])
        tri = sb("tri", [P, P], BF16)
        ones_b = sb("ones_b", [P, P], BF16)
        keep = sb("keep", [P, E, NT])
        ones_e = sb("ones_e", [P, E])
        best = sb("best", [P, TOP_K, NT])
        pick = sb("pick", [P, NT])
        scratch = sb("scratch", [P, NT, E])
        masked = sb("masked", [P, NT, E])
        hot = [sb(f"hot{i}", [P, NT, E]) for i in range(TOP_K)]
        hots = sb("hots", [P, NT, E], BF16)
        expo = sb("expo", [P, NT, E])
        expo2 = sb("expo2", [P, NT])
        inv_sum = sb("inv_sum", [P, NT])
        tile_count = sb("tile_count", [P, E, NT])
        running = sb("running", [P, E, NT])
        before = sb("before", [P, E, NT])
        padded = sb("padded", [P, E])
        padded_i = sb("padded_i", [P, E], I32)
        tiles_of = sb("tiles_of", [P, E])
        tile_end = sb("tile_end", [P, E])
        start = sb("start", [P, E])
        place = sb("place", [P, NT, E])
        pos_f = sb("pos_f", [P, TOP_K, NT])
        col_i = sb("col_i", [P, KT], I32)
        row_i = sb("row_i", [P, KT], I32)
        col_b = sb("col_b", [P, KT], BF16)
        row_b = sb("row_b", [P, KT], BF16)
        col_hot = sb("col_hot", [P, KT, 2, SLOTS], BF16)
        row_hot = sb("row_hot", [P, KT, P], BF16)
        low = sb("low", [P, SLOTS])
        ended = sb("ended", [P, n_tiles, E])
        expert_f = sb("expert_f", [P, n_tiles])
        changed_f = sb("changed_f", [P, n_tiles])
        count_ps = psum("count_ps", [P, 2, NT * E])
        list_ps = psum("list_ps", [P, 2 * SLOTS])

        L = logits[:, skip:, :]
        e_of = lambda a: a.unsqueeze(2).to_broadcast([P, NT, E])
        t_of = lambda a: a.unsqueeze(1).to_broadcast([P, NT, E])
        V = lambda waits, emit: g.step("dve", waits, emit)

        p0 = g.step("pool", [], lambda e: e.iota(iota_i[:, :], [[1, P]], base=0, channel_multiplier=0))
        p1 = g.step("pool", [p0], lambda e: e.iota(part_i[:, :], [[1, 1]], base=0, channel_multiplier=1))
        p2 = g.step("pool", [p1], lambda e: e.memset(ones_b[:, :], 1.0))
        tri_on = g.step("pool", [p2], lambda e: e.affine_select(out=tri[:, :], in_=ones_b[:, :], compare_op=ALU.is_gt, fill=0.0,
                                                               base=0, pattern=[[1, P]], channel_multiplier=-1))
        p3 = g.step("pool", [tri_on], lambda e: e.memset(keep[:, :, :], 1.0))
        p4 = g.step("pool", [p3], lambda e: e.memset(keep[:, :, 0:1], 0.0))
        p5 = g.step("pool", [p4], lambda e: e.memset(ones_e[:, :], 1.0))
        f0 = V([p0], lambda e: e.tensor_copy(iota_f[:, :], iota_i[:, :]))
        f1 = V([p1], lambda e: e.tensor_copy(part_f[:, :], part_i[:, :]))
        f2 = V([f0], lambda e: e.tensor_copy(iota_b[:, :], iota_f[:, :]))
        f3 = V([f0], lambda e: e.tensor_scalar(expert_less[:, :], iota_f[:, 0:E], -float(E), None, ALU.add))

        source, last = L, f3
        for s in range(TOP_K):
            d = V([last], lambda e, s=s, source=source: e.tensor_reduce(best[:, s, :], source, AX.X, ALU.max))
            d = V([d], lambda e, s=s, source=source: e.tensor_tensor(scratch[:, :, :], source, e_of(best[:, s, :]), ALU.is_equal))
            d = V([d], lambda e: e.tensor_tensor(scratch[:, :, :], scratch[:, :, :], t_of(expert_less[:, :]), ALU.mult))
            d = V([d], lambda e: e.tensor_reduce(pick[:, :], scratch[:, :, :], AX.X, ALU.min))
            last = V([d], lambda e, s=s: e.tensor_tensor(hot[s][:, :, :], t_of(expert_less[:, :]), e_of(pick[:, :]), ALU.is_equal))
            if s == 0:
                last = V([last], lambda e: e.scalar_tensor_tensor(out=masked[:, :, :], in0=hot[0][:, :, :], scalar=-1e30, in1=L,
                                                                  op0=ALU.mult, op1=ALU.add))
                source = masked[:, :, :]
        hots_on = V([last], lambda e: e.tensor_tensor(hots[:, :, :], hot[0][:, :, :], hot[1][:, :, :], ALU.add))

        d = V([last], lambda e: e.tensor_tensor(expo[:, :, :], L, e_of(best[:, 0, :]), ALU.subtract))
        d2 = V([last], lambda e: e.tensor_tensor(expo2[:, :], best[:, 1, :], best[:, 0, :], ALU.subtract))
        a1 = g.step("act", [d], lambda e: e.activation(expo[:, :, :], expo[:, :, :], ACT.Exp))
        a2 = g.step("act", [d2], lambda e: e.activation(expo2[:, :], expo2[:, :], ACT.Exp))
        d = V([a1], lambda e: e.tensor_reduce(inv_sum[:, :], expo[:, :, :], AX.X, ALU.add))
        d = V([d], lambda e: e.reciprocal(w12[:, 0, :], inv_sum[:, :]))
        V([d, a2], lambda e: e.tensor_tensor(w12[:, 1, :], expo2[:, :], w12[:, 0, :], ALU.mult))

        flat = hots[:, :, :].rearrange("p t e -> p (t e)")
        c1 = g.step("pe", [hots_on, tri_on], lambda e: e.matmul(count_ps[:, 0, :], tri[:, :], flat, start=True, stop=True))
        c2 = g.step("pe", [], lambda e: e.matmul(count_ps[:, 1, :], ones_b[:, :], flat, start=True, stop=True))
        d = V([c2], lambda e: e.tensor_copy(tile_count[:, :, :], count_ps[:, 1, :].rearrange("p (t e) -> p e t", e=E)))
        d = V([d, p4], lambda e: e.tensor_tensor_scan(running[:, :, :].rearrange("p e t -> p (e t)"),
                                                      keep[:, :, :].rearrange("p e t -> p (e t)"),
                                                      tile_count[:, :, :].rearrange("p e t -> p (e t)"), 0.0, ALU.mult, ALU.add))
        d_run = V([d], lambda e: e.tensor_tensor(before[:, :, :], running[:, :, :], tile_count[:, :, :], ALU.subtract))
        d = V([d], lambda e: e.tensor_scalar(padded[:, :], running[:, :, NT - 1], float(FTOK - 1), None, ALU.add))
        d = V([d], lambda e: e.tensor_copy(padded_i[:, :], padded[:, :]))
        d = V([d], lambda e: e.tensor_scalar(padded_i[:, :], padded_i[:, :], TILE_SHIFT, None, ALU.arith_shift_right))
        d = V([d], lambda e: e.tensor_copy(tiles_of[:, :], padded_i[:, :]))
        d_end = V([d, p5], lambda e: e.tensor_tensor_scan(tile_end[:, :], ones_e[:, :], tiles_of[:, :], 0.0, ALU.mult, ALU.add))
        d = V([d_end], lambda e: e.tensor_tensor(start[:, :], tile_end[:, :], tiles_of[:, :], ALU.subtract))
        d = V([d], lambda e: e.tensor_scalar(start[:, :], start[:, :], float(FTOK), None, ALU.mult))
        d = V([c1, d_run], lambda e: e.tensor_tensor(place[:, :, :], count_ps[:, 0, :].rearrange("p (t e) -> p t e", e=E),
                                                     before[:, :, :].rearrange("p e t -> p t e"), ALU.add))
        d_place = V([d], lambda e: e.tensor_tensor(place[:, :, :], place[:, :, :], t_of(start[:, :]), ALU.add))
        for s in range(TOP_K):
            d = V([d_place], lambda e, s=s: e.tensor_tensor(hot[s][:, :, :], hot[s][:, :, :], place[:, :, :], ALU.mult))
            d = V([d], lambda e, s=s: e.tensor_reduce(pos_f[:, s, :], hot[s][:, :, :], AX.X, ALU.add))
        d_pos = V([d], lambda e: e.tensor_copy(pos[:, :, :], pos_f[:, :, :]))

        d = V([d_end], lambda e: e.tensor_tensor(ended[:, :, :], iota_f[:, 0:n_tiles].unsqueeze(2).to_broadcast([P, n_tiles, E]),
                                                 tile_end[:, :].unsqueeze(1).to_broadcast([P, n_tiles, E]), ALU.is_ge))
        d = V([d], lambda e: e.tensor_reduce(expert_f[:, :], ended[:, :, :], AX.X, ALU.add))
        d_exp = V([d], lambda e: e.tensor_scalar(expert_f[:, :], expert_f[:, :], float(E - 1), None, ALU.min))
        expert_on = V([d_exp], lambda e: e.tensor_copy(tile_expert[0:1, :], expert_f[0:1, :]))
        d = V([], lambda e: e.memset(changed_f[:, 0:2], 1.0))
        d = V([d, d_exp], lambda e: e.tensor_tensor(changed_f[:, 2:], expert_f[:, 2:], expert_f[:, :-2], ALU.not_equal))
        changed_on = V([d], lambda e: e.tensor_copy(tile_changed[0:1, :], changed_f[0:1, :]))

        def first_weights(e, turn):
            for c, m in (expert_on, changed_on):
                c.wait(e, turn, m)
            first_loads(e)
        g.q["sp"].append(first_weights)

        flat_pos = pos[:, :, :].rearrange("p s t -> p (s t)")
        d = V([d_pos], lambda e: e.tensor_scalar(col_i[:, :], flat_pos, SHIFT, None, ALU.arith_shift_right))
        d2 = V([d_pos], lambda e: e.tensor_scalar(row_i[:, :], flat_pos, P - 1, None, ALU.bitwise_and))
        d = V([d], lambda e: e.tensor_copy(col_b[:, :], col_i[:, :]))
        d2 = V([d2], lambda e: e.tensor_copy(row_b[:, :], row_i[:, :]))
        NQ = 4
        for q in range(NQ):
            some = slice(q * KT // NQ, (q + 1) * KT // NQ)
            n_some = KT // NQ
            tiles = slice(some.start % NT, some.start % NT + n_some)
            d_row = V([d2, f2], lambda e, some=some: e.tensor_tensor(
                row_hot[:, some, :], iota_b[:, :].unsqueeze(1).to_broadcast([P, n_some, P]),
                row_b[:, some].unsqueeze(2).to_broadcast([P, n_some, P]), ALU.is_equal))
            d3 = V([d], lambda e, some=some: e.tensor_tensor(
                col_hot[:, some, 1, :], iota_b[:, 0:SLOTS].unsqueeze(1).to_broadcast([P, n_some, SLOTS]),
                col_b[:, some].unsqueeze(2).to_broadcast([P, n_some, SLOTS]), ALU.is_equal))
            d3 = V([d3], lambda e, some=some, tiles=tiles: e.tensor_tensor(
                col_hot[:, some, 0, :], col_hot[:, some, 1, :],
                iota_b[:, tiles].unsqueeze(2).to_broadcast([P, n_some, SLOTS]), ALU.mult))
            d4 = V([d3, f1], lambda e, some=some: e.tensor_scalar(
                col_hot[:, some, 1, :], col_hot[:, some, 1, :], part_f[:, 0:1], None, ALU.mult))
            for n in range(some.start, some.stop):
                c = g.step("pe", [d_row, d4] if n == some.start else [], lambda e, n=n: e.matmul(
                    list_ps[:, :], row_hot[:, n, :], col_hot[:, n, :, :].rearrange("p a c -> p (a c)"), start=(n == 0), stop=(n == KT - 1)))
        d = V([c], lambda e: e.tensor_scalar(low[:, :], list_ps[:, SLOTS:], float(skip * P), None, ALU.add))
        V([d], lambda e: e.scalar_tensor_tensor(out=token_of[:, :], in0=list_ps[:, 0:SLOTS], scalar=float(P), in1=low[:, :],
                                                op0=ALU.mult, op1=ALU.add))

        with nc.Block() as block:
            @block.sync
            def _(e):
                g.run("sp", e, 0)

            for name in ("pool", "dve", "act", "pe"):
                deco = {"pool": block.gpsimd, "dve": block.vector, "act": block.scalar, "pe": block.tensor}[name]

                @deco
                def _(e, name=name):
                    g.count[name].open(e)
                    g.run(name, e, 0)


def load_if_changed(e, tile_expert, tile_changed, tile, semaphore, experts, copies):
    expert = e.value_load(tile_expert[0:1, tile], min_val=0, max_val=experts - 1)
    changed = e.value_load(tile_changed[0:1, tile], min_val=0, max_val=1)
    for dst, src in copies(expert):
        e.dma_start(dst, src, cond=changed).then_inc(semaphore, 16)


def load_raw_weights(e, raw, w_gate_up, w_down, tile_expert, tile_changed, tile, semaphore):
    gate_up, down = raw
    load_if_changed(e, tile_expert, tile_changed, tile, semaphore, w_gate_up.shape[0], lambda expert: (
        (gate_up[:, :, :], w_gate_up[bass.ds(expert, 1), :, :].rearrange("a (k p) f -> p (a k) f", p=P)),
        (down[:, :, :], w_down[bass.ds(expert, 1), :, :].rearrange("a (k p) f -> p (a k) f", p=P))))


def expert_stage(nc, raw, s_raw, xln_dram, y_dram, w_gate_up, w_down, b_gate_up, b_down, tile_expert, tile_changed, token_of, ident, n_tiles, s_go):
    E, D, F2 = w_gate_up.shape
    F = F2 // 2
    KD, KF = D // P, F // P
    SUB = FTOK // P
    rows = xln_dram.rearrange("b s d -> (b s) d")

    with ExitStack() as ctx:
        sb = lambda name, shape, dt=F32: ctx.enter_context(nc.sbuf_tensor(name, shape, dt))
        psum = lambda name, shape: ctx.enter_context(nc.psum_tensor(name, shape, F32))
        sem = lambda name: ctx.enter_context(nc.semaphore(name))
        g = Turn(sem, "ffn")
        head = Turn(sem, "ffn_head")
        pe, act, dve, pool, marks = g.pe, g.act, g.dve, g.pool, g.marks
        raw_load = [Count(s, 16) for s in s_raw]
        bias_load = [Count(sem(f"s_bias{s}"), 16) for s in range(2)]
        w_hi = [Count(sem(f"s_whi{s}")) for s in range(2)]
        w_lo = [Count(sem(f"s_wlo{s}")) for s in range(2)]
        gather = [Count(sem(f"s_gather{s}"), 16, ahead=0) for s in range(2)]
        head_gather = Count(sem("s_gather_head"), 16, ahead=0)
        store = [Count(sem(f"s_y{s}"), 16) for s in range(2)]

        raw_g, raw_d = zip(*raw)
        pair = lambda name, shape, s: [sb(f"{name}_{part}{s}", shape, F32R) for part in ("hi", "lo")]
        wg = [pair("wg", [P, KD, F2], s) for s in range(2)]
        wd = [pair("wd", [P, KF, D], s) for s in range(2)]
        PASSES = ((0, 0), (0, 1), (1, 0))
        bg = [sb(f"bg{s}", [P, F2 // P]) for s in range(2)]
        bd = [sb(f"bd{s}", [P, D]) for s in range(2)]
        bu1 = [sb(f"bu1{s}", [P, KF]) for s in range(2)]
        idx = [sb(f"idx{s}", [P, SUB], I32) for s in range(2)]
        xg = [sb(f"xg{s}", [P, SUB, D]) for s in range(2)]
        xgT = [pair("xgT", [P, KD, FTOK], s) for s in range(2)]
        gate = [sb(f"gate{i}", [P, FTOK]) for i in range(2)]
        sig = [sb(f"sig{i}", [P, FTOK]) for i in range(2)]
        up = [sb(f"up{i}", [P, FTOK]) for i in range(2)]
        hid_f = [sb(f"hid_f{i}", [P, FTOK]) for i in range(2)]
        hid = pair("hid", [P, KF, FTOK], "")
        y = [sb(f"y{s}", [P, SUB, D]) for s in range(2)]
        t_ps = [psum(f"t_ps{i}", [P, 2, FTOK]) for i in range(KD // 2)]
        gu_ps = [psum(f"gu_ps{i}", [P, 2, FTOK]) for i in range(2)]
        d_ps = [psum(f"d_ps{i}", [P, D]) for i in range(2)]

        def fetch(g, gather, s, tile, first_wait):
            def copy(e, b):
                first_wait(e, b)
                e.tensor_copy(idx[s][:, :], token_of[:, bass.ds(b * (2 * SUB) + tile * SUB, SUB)]).then_inc(g.pool.sem, 1)
            g.q["pool"].append(copy)
            m = g.pool.did()
            def rows_in(e, b):
                g.pool.wait(e, b, m, s_go)
                for i in range(SUB):
                    e.indirect_dma_start(out=xg[s][:, i, :], out_offset=None, in_=rows,
                                         in_offset=bass.IndirectOffsetOnAxis(ap=idx[s][:, i:i + 1].bitcast(U32), axis=0)).then_inc(gather.sem, 16)
            g.q["pool"].append(rows_in)
            for _ in range(SUB):
                g.marks["gather", s] = gather.did()

        def issue_raw(e, s, tile):
            load_raw_weights(e, raw[s], w_gate_up, w_down, tile_expert, tile_changed, tile, raw_load[s].sem)

        def issue_bias(e, s, tile):
            load_if_changed(e, tile_expert, tile_changed, tile, bias_load[s].sem, E, lambda expert: (
                (bg[s][:, :], b_gate_up[bass.ds(expert, 1), :, :].rearrange("a p c -> p (a c)")),
                (bd[s][:, :], b_down[bass.ds(expert, 1), :].to_broadcast([P, D]))))

        def load_raw(s, tile):
            def f(e, b):
                (w_lo[s].wait if s else w_lo[s].wait_before)(e, b, marks["w_lo", s], s_go)
                (w_hi[s].wait if s else w_hi[s].wait_before)(e, b, marks["w_hi", s], s_go)
                issue_raw(e, s, bass.ds(b * 2 + tile, 1))
            g.q["sp"].append(f)
            for _ in range(2):
                marks["raw", s] = raw_load[s].did()

        def load_bias(s, tile):
            def f(e, b):
                (dve.wait_before if s else dve.wait)(e, b, marks["y", s], s_go)
                issue_bias(e, s, bass.ds(b * 2 + tile, 1))
            g.q["sp"].append(f)
            for _ in range(2):
                marks["bias", s] = bias_load[s].did()

        def split_hi(e, s, k, sem):
            e.activation(wg[s][0][:, k, :], raw_g[s][:, k, :], ACT.Identity).then_inc(sem, 1)
            e.activation(wd[s][0][:, k, :], raw_d[s][:, k, :], ACT.Identity).then_inc(sem, 1)

        def split_lo(e, s, k, sem, down):
            w, raw = (wd[s], raw_d[s]) if down else (wg[s], raw_g[s])
            e.tensor_tensor(w[1][:, k, :], raw[:, k, :], w[0][:, k, :].bitcast(F32), ALU.subtract).then_inc(sem, 1)

        changed_of = {}

        def guarded(e, b, name, s, tile, split, sem, amount, first):
            if first:
                changed_of[name, s] = e.to_reg(e.value_load(tile_changed[0:1, bass.ds(b * 2 + tile, 1)], min_val=0, max_val=1))
            with e.If_ne(changed_of[name, s], 0):
                split()
            with e.Else():
                e.sem_inc(sem, amount)

        def weights_free_and_in(e, b, s):
            (pe.wait_before if s else pe.wait)(e, b, marks["down", s], s_go)
            (raw_load[s].wait_before if s else raw_load[s].wait)(e, b, marks["raw", s], s_go)

        def make_hi(s, k, tile):
            def on_act(e, b):
                if k == 0:
                    weights_free_and_in(e, b, s)
                guarded(e, b, "act", s, tile, lambda: split_hi(e, s, k, w_hi[s].sem), w_hi[s].sem, 2, k == 0)
            g.q["act"].append(on_act)
            for _ in range(2):
                marks["w_hi", s, k] = w_hi[s].did()
            marks["w_hi", s] = marks["w_hi", s, k]

        def make_lo(s, tile):
            for down in (0, 1):
                for k in range(KD):
                    def on_pool(e, b, k=k, down=down):
                        if k == 0 and not down:
                            weights_free_and_in(e, b, s)
                        w_hi[s].wait(e, b, marks["w_hi", s, k], s_go)
                        guarded(e, b, "pool", s, tile, lambda: split_lo(e, s, k, w_lo[s].sem, down), w_lo[s].sem, 1,
                                k == 0 and not down)
                    g.q["pool"].append(on_pool)
                    marks["w_lo", s, down] = marks["w_lo", s] = w_lo[s].did()

        def turn_rows(g, gather, s, bank_free):
            for half in range(KD // 2):
                def f(e, b, half=half):
                    gather.wait(e, b, g.marks["gather", s])
                    bank_free(e, b, half)
                    for k in range(2):
                        for i in range(SUB):
                            c = 2 * half + k
                            ins = e.transpose(t_ps[half][:, k, i * P:(i + 1) * P], xg[s][:, i, c * P:(c + 1) * P], ident[:, :])
                    ins.then_inc(g.pe.sem, 1)
                g.q["pe"].append(f)
                done = g.marks["turned", s] = g.pe.did()
                def a(e, b, half=half, done=done):
                    g.pe.wait(e, b, done)
                    e.activation(xgT[s][0][:, 2 * half:2 * half + 2, :], t_ps[half][:, :, :], ACT.Identity).then_inc(g.act.sem, 1)
                g.q["act"].append(a)
                hi_made = g.act.did()
                def d(e, b, half=half, hi_made=hi_made):
                    g.act.wait(e, b, hi_made)
                    chunks = slice(2 * half, 2 * half + 2)
                    e.tensor_tensor(xgT[s][1][:, chunks, :], t_ps[half][:, :, :], xgT[s][0][:, chunks, :].bitcast(F32),
                                    ALU.subtract).then_inc(g.dve.sem, 1)
                g.q["dve"].append(d)
                g.marks["xgT", s, half] = g.dve.did()

        def gate_up(s, split_next):
            def plus_one(e, b):
                (bias_load[s].wait if s else bias_load[s].wait_before)(e, b, marks["bias", s])
                e.tensor_scalar(bu1[s][:, :], bg[s][:, KF:], 1.0, None, ALU.add).then_inc(dve.sem, 1)
            g.q["dve"].append(plus_one)
            bu1_on = dve.did()
            split_next(0)
            parts = []
            for f in range(KF):
                i = f % 2
                n = s * KF + f
                def p(e, b, f=f, i=i, n=n):
                    if f == 0:
                        (w_hi[s].wait if s else w_hi[s].wait_before)(e, b, marks["w_hi", s])
                        (w_lo[s].wait if s else w_lo[s].wait_before)(e, b, marks["w_lo", s, 0])
                        (dve.wait if s else dve.wait_before)(e, b, marks["xgT", s, KD // 2 - 1])
                    if n >= 2:
                        dve.wait(e, b, marks["up", n - 2])
                    else:
                        dve.wait_before(e, b, marks["up", n - 2 + 2 * KF])
                    for part in range(2):
                        cols = slice(part * F + f * P, part * F + (f + 1) * P)
                        for k in range(KD):
                            for n_pass, (pw, px) in enumerate(PASSES):
                                ins = e.matmul(gu_ps[i][:, part, :], wg[s][pw][:, k, cols], xgT[s][px][:, k, :],
                                               start=(k == 0 and n_pass == 0), stop=(k == KD - 1 and n_pass == len(PASSES) - 1))
                    ins.then_inc(pe.sem, 1)
                g.q["pe"].append(p)
                made = (pe, pe.did())
                def clip_gate(e, b, i=i, f=f, n=n, made=made):
                    made[0].wait(e, b, made[1])
                    if n >= 2:
                        dve.wait(e, b, marks["hid_f", n - 2])
                    else:
                        dve.wait_before(e, b, marks["hid_f", n - 2 + 2 * KF])
                    e.tensor_scalar(gate[i][:, :], gu_ps[i][:, 0, :], bg[s][:, f:f + 1], LIMIT, ALU.add, ALU.min).then_inc(dve.sem, 1)
                g.q["dve"].append(clip_gate)
                g1 = (dve, dve.did())
                s1 = g.step("act", [g1], lambda e, i=i: e.activation(sig[i][:, :], gate[i][:, :], ACT.Sigmoid, scale=ALPHA))
                u1 = g.step("dve", [made, (dve, bu1_on)], lambda e, i=i, f=f: e.tensor_scalar(
                    up[i][:, :], gu_ps[i][:, 1, :], bu1[s][:, f:f + 1], LIMIT + 1.0, ALU.add, ALU.min))
                marks["up", n] = u1[1]
                if f:
                    glu(s, f - 1, *pending, parts)
                if f > 1:
                    parts.pop(0)()
                pending = (s1, u1)
                if f + 1 < KF:
                    split_next(f + 1)
            glu(s, KF - 1, *pending, parts)
            for lo_part in parts:
                lo_part()

        def glu(s, f, s1, u1, parts):
            i = f % 2
            g2 = g.step("dve", [s1], lambda e: e.tensor_tensor(gate[i][:, :], gate[i][:, :], sig[i][:, :], ALU.mult))
            n = s * KF + f
            def h(e, b):
                if n >= 2:
                    dve.wait(e, b, marks["hid_of", n - 2])
                else:
                    dve.wait_before(e, b, marks["hid_of", n - 2 + 2 * KF])
                dve.wait(e, b, g2[1])
                e.scalar_tensor_tensor(out=hid_f[i][:, :], in0=up[i][:, :], scalar=1.0 - LIMIT, in1=gate[i][:, :],
                                       op0=ALU.max, op1=ALU.mult).then_inc(dve.sem, 1)
            g.q["dve"].append(h)
            made = marks["hid_f", n] = dve.did()
            def to_hi(e, b):
                (pe.wait if s else pe.wait_before)(e, b, marks["down", 1 - s])
                dve.wait(e, b, made)
                e.activation(hid[0][:, f, :], hid_f[i][:, :], ACT.Identity).then_inc(act.sem, 1)
            g.q["act"].append(to_hi)
            hi_made = (act, act.did())
            def lo_part():
                marks["hid_of", n] = g.step("dve", [hi_made], lambda e: e.tensor_tensor(
                    hid[1][:, f, :], hid_f[i][:, :], hid[0][:, f, :].bitcast(F32), ALU.subtract))[1]
            parts.append(lo_part)

        def down(s):
            for k in range(KF):
                for i in range(SUB):
                    def p(e, b, i=i, k=k):
                        if k == 0 and i == 0:
                            (w_lo[s].wait if s else w_lo[s].wait_before)(e, b, marks["w_lo", s, 1])
                        if k == 0 and s:
                            dve.wait(e, b, marks["y", 0, i])
                        elif k == 0:
                            dve.wait_before(e, b, marks["y", 1, i])
                        if i == 0:
                            dve.wait(e, b, marks["hid_of", s * KF + k])
                        for n_pass, (pw, px) in enumerate(PASSES):
                            ins = e.matmul(d_ps[i][:, :], hid[px][:, k, i * P:(i + 1) * P], wd[s][pw][:, k, :],
                                           start=(k == 0 and n_pass == 0), stop=(k == KF - 1 and n_pass == len(PASSES) - 1))
                        if k == KF - 1:
                            ins.then_inc(pe.sem, 1)
                    g.q["pe"].append(p)
                    if k == KF - 1:
                        done = marks["down", s] = pe.did()
                        rows_out(s, i, done)

        def rows_out(s, i, done):
            def d(e, b):
                pe.wait(e, b, done)
                store[s].wait_before(e, b, marks["store", s])
                e.tensor_tensor(y[s][:, i, :], d_ps[i][:, :], bd[s][:, :], ALU.add).then_inc(dve.sem, 1)
            g.q["dve"].append(d)
            marks["y", s, i] = marks["y", s] = dve.did()

        def store_rows(s):
            def f(e, b):
                dve.wait(e, b, marks["y", s], s_go)
                e.dma_start(y_dram[bass.ds(b * 2 + s, 1), :, :].rearrange("a (i p) n -> p (a i) n", p=P), y[s][:, :, :]).then_inc(store[s].sem, 16)
            g.q["act" if s else "sp"].append(f)
            marks["store", s] = store[s].did()

        fetch(head, head_gather, 0, 0, lambda e, b: None)
        turn_rows(head, head_gather, 0, lambda e, b, half: None)

        fetch(g, gather[1], 1, 1, lambda e, b: pe.wait_before(e, b, marks["turned", 1]))
        ahead = len(g.q["pool"])
        fetch(g, gather[0], 0, 2, lambda e, b: pe.wait_before(e, b, marks["turned", 0]))
        ahead = range(ahead, len(g.q["pool"]))
        load_bias(1, 1)
        load_raw(0, 2)
        make_lo(1, 1)
        gate_up(0, lambda k: make_hi(1, k, 1))
        turn_rows(g, gather[1], 1, lambda e, b, half: dve.wait_before(e, b, marks["xgT", 0, half]))
        down(0)
        sp_store = len(g.q["sp"])
        store_rows(0)
        first_tile = {n: len(g.q[n]) for n in g.q}
        load_bias(0, 2)
        load_raw(1, 3)
        make_lo(0, 2)
        gate_up(1, lambda k: make_hi(0, k, 2))
        turn_rows(g, gather[0], 0, lambda e, b, half: dve.wait(e, b, marks["xgT", 1, half]))
        down(1)
        store_rows(1)
        pairs = n_tiles // 2
        odd = n_tiles % 2
        assert odd

        with nc.Block() as block:
            @block.sync
            def _(e):
                issue_bias(e, 0, slice(0, 1))

            @block.gpsimd
            def _(e):
                head.pool.open(e)
                head.run("pool", e, 0)

            @block.tensor
            def _(e):
                head.pe.open(e)
                head.run("pe", e, 0)

            @block.scalar
            def _(e):
                head.act.open(e)
                e.wait_ge(s_raw[0], raw_load[0].per_turn)
                for k in range(KD):
                    split_hi(e, 0, k, w_hi[0].sem)
                head.run("act", e, 0)

            @block.vector
            def _(e):
                head.dve.open(e)
                for down in (0, 1):
                    for k in range(KD):
                        e.wait_ge(w_hi[0].sem, 2 * (k + 1))
                        split_lo(e, 0, k, w_lo[0].sem, down)
                head.run("dve", e, 0)

        with nc.Block() as block:
            @block.sync
            def _(e):
                for c in (bias_load[1], w_hi[1], w_lo[1], *store):
                    c.open(e)
                with e.Fori(0, pairs) as b:
                    g.run("sp", e, b)
                g.q["sp"][sp_store](e, pairs)
                store[0].wait(e, pairs, marks["store", 0])
                store[1].wait(e, pairs - 1, marks["store", 1])

            for name in ("pool", "dve", "act", "pe"):
                deco = {"pool": block.gpsimd, "dve": block.vector, "act": block.scalar, "pe": block.tensor}[name]

                @deco
                def _(e, name=name):
                    g.count[name].open(e)
                    with e.Fori(0, pairs) as b:
                        g.run(name, e, b)
                    for n, f in enumerate(g.q[name][:first_tile[name]]):
                        if name != "pool" or n not in ahead:
                            f(e, pairs)


def combine_stage(nc, x2_dram, y_dram, out, w12, pos, s_go):
    _, S, D = x2_dram.shape
    B = out.shape[0]
    T = S // P
    y_rows = y_dram.rearrange("a b d -> (a b) d")
    TT = 2 * T

    with ExitStack() as ctx:
        sb = lambda name, shape, dt=F32: ctx.enter_context(nc.sbuf_tensor(name, shape, dt))
        sem = lambda name: ctx.enter_context(nc.semaphore(name))
        g = Turn(sem, "mix")
        dve, pool, marks = g.dve, g.pool, g.marks
        res = [sb(f"res{i}", [P, T, D]) for i in range(2)]
        ya = sb("ya", [P, TOP_K, TT, D])
        idx = sb("idx", [P, TOP_K, TT], I32)
        w = sb("w", [P, TOP_K, TT])
        load = [Count(sem(f"s_res{i}"), 16) for i in range(2)]
        store = [Count(sem(f"s_out{i}"), 16) for i in range(2)]
        gathered = [Count(sem(f"s_ya{t}"), 16, ahead=0) for t in range(TT)]

        def copies():
            def f(e, b):
                dve.wait_before(e, b, marks["mixed", TT - 1])
                e.tensor_copy(w[:, :, :], w12[:, :, bass.ds(b * TT, TT)]).then_inc(pool.sem, 1)
                e.tensor_copy(idx[:, :, :], pos[:, :, bass.ds(b * TT, TT)]).then_inc(pool.sem, 1)
            g.q["pool"].append(f)
            marks["w"] = pool.did()
            marks["idx"] = pool.did()

        def gather(t):
            def f(e, b):
                if t == 0:
                    pool.wait(e, b, marks["idx"])
                dve.wait_before(e, b, marks["mixed", t], s_go)
                for s in range(TOP_K):
                    e.indirect_dma_start(out=ya[:, s, t, :], out_offset=None, in_=y_rows,
                                         in_offset=bass.IndirectOffsetOnAxis(ap=idx[:, s, t:t + 1].bitcast(U32), axis=0)).then_inc(gathered[t].sem, 16)
            g.q["pool"].append(f)
            for _ in range(TOP_K):
                marks["ya", t] = gathered[t].did()

        def load_residual(i):
            def f(e, b):
                store[i].wait_before(e, b, marks["store", i], s_go)
                e.dma_start(res[i][:, :, :], x2_dram[bass.ds(b * 2 + (i + 1), 1), :, :].rearrange("a (t p) n -> p (a t) n", p=P)).then_inc(load[i].sem, 16)
            g.q["sp"].append(f)
            marks["load", i] = load[i].did()

        def mix(t):
            i = t // T
            def f(e, b):
                load[i].wait(e, b, marks["load", i])
                gathered[t].wait(e, b, marks["ya", t])
                pool.wait(e, b, marks["w"])
                e.scalar_tensor_tensor(out=res[i][:, t % T, :], in0=ya[:, 0, t, :], scalar=w[:, 0, t:t + 1],
                                       in1=res[i][:, t % T, :], op0=ALU.mult, op1=ALU.add).then_inc(dve.sem, 1)
            g.q["dve"].append(f)
            m = (dve, dve.did())
            marks["mixed", t] = g.step("dve", [m], lambda e: e.scalar_tensor_tensor(
                out=res[i][:, t % T, :], in0=ya[:, 1, t, :], scalar=w[:, 1, t:t + 1],
                in1=res[i][:, t % T, :], op0=ALU.mult, op1=ALU.add))[1]

        def store_out(i):
            def f(e, b):
                dve.wait(e, b, marks["mixed", (i + 1) * T - 1], s_go)
                e.dma_start(out[bass.ds(b * 2 + i, 1), :, :].rearrange("a (t p) n -> p (a t) n", p=P), res[i][:, :, :]).then_inc(store[i].sem, 16)
            g.q["sp"].append(f)
            marks["store", i] = store[i].did()

        copies()
        load_residual(0)
        load_residual(1)
        for t in range(TT):
            gather(t)
            mix(t)
        store_out(0)
        store_out(1)

        with nc.Block() as block:
            @block.sync
            def _(e):
                for c in (*load, *store):
                    c.open(e)
                with e.Fori(0, B // 2) as b:
                    g.run("sp", e, b)
                for i in range(2):
                    store[i].wait(e, B // 2 - 1, marks["store", i])

            @block.gpsimd
            def _(e):
                pool.open(e)
                with e.Fori(0, B // 2) as b:
                    g.run("pool", e, b)

            @block.vector
            def _(e):
                dve.open(e)
                with e.Fori(0, B // 2) as b:
                    g.run("dve", e, b)


def build(nc, x, ctx_t, wq_t, bq, wk_t, bk, wv_t, bv, wo_t, bo, router_wt, router_b, w_gate_up, b_gate_up, w_down, b_down, out):
    B, S, D = x.shape
    E = router_wt.shape[1]
    T = S // P
    NT = B * T
    n_tiles = (TOP_K * B * S - E) // FTOK + E
    whole_turns = n_tiles + n_tiles % 2
    slots = whole_turns * (FTOK // P)
    x2_dram = nc.dram_tensor("x2_dram", (B + 1, S, D), F32, kind="Internal").ap()
    xln_dram = nc.dram_tensor("xln_dram", (B + 1, S, D), F32, kind="Internal").ap()
    y_dram = nc.dram_tensor("y_dram", (n_tiles, FTOK, D), F32, kind="Internal").ap()

    with ExitStack() as ctx:
        sb = lambda name, shape, dt=F32: ctx.enter_context(nc.sbuf_tensor(name, shape, dt))
        logits = sb("logits", [P, NT + T, E])
        ident = sb("ident", [P, P])
        w12 = sb("w12", [P, TOP_K, NT])
        pos = sb("pos", [P, TOP_K, NT], I32)
        tile_expert = sb("tile_expert", [1, whole_turns], I32)
        tile_changed = sb("tile_changed", [1, whole_turns], I32)
        token_of = sb("token_of", [P, slots], I32)
        s_ident = ctx.enter_context(nc.semaphore("s_ident"))
        s_go = ctx.enter_context(nc.semaphore("s_go"))

        with nc.Block() as block:
            @block.gpsimd
            def _(e):
                e.memset(ident[:, :], 0.0).then_inc(s_ident, 1)
                e.wait_ge(s_ident, 1)
                e.affine_select(out=ident[:, :], in_=ident[:, :], compare_op=ALU.not_equal, fill=1.0,
                                base=0, pattern=[[-1, P]], channel_multiplier=1).then_inc(s_ident, 1)
                e.wait_ge(s_ident, 2)
                e.sem_inc(s_go, 1)

        attention_stage(nc, x, ctx_t, (wq_t, wk_t, wv_t, wo_t), bq, bk, bv, bo, router_wt, router_b, x2_dram, xln_dram, logits, ident, s_go)

        D, F2, F = w_gate_up.shape[1], w_gate_up.shape[2], w_down.shape[1]
        raw = [(sb(f"raw_g{s}", [P, D // P, F2]), sb(f"raw_d{s}", [P, F // P, D])) for s in range(2)]
        s_raw = [ctx.enter_context(nc.semaphore(f"s_raw{s}")) for s in range(2)]

        def first_loads(e):
            for s in range(2):
                load_raw_weights(e, raw[s], w_gate_up, w_down, tile_expert, tile_changed, slice(s, s + 1), s_raw[s])

        routing_stage(nc, logits, T, w12, pos, tile_expert, tile_changed, token_of, whole_turns, first_loads)
        expert_stage(nc, raw, s_raw, xln_dram, y_dram, w_gate_up, w_down, b_gate_up, b_down, tile_expert, tile_changed, token_of, ident, n_tiles, s_go)
        combine_stage(nc, x2_dram, y_dram, out, w12, pos, s_go)


_INS = ["x", "ctx_t", "wq_t", "bq", "wk_t", "bk", "wv_t", "bv", "wo_t", "bo", "router_wt", "router_b",
        "w_gate_up", "b_gate_up", "w_down", "b_down"]


def kernel(**i):
    import numpy as np
    import concourse.bacc as bacc
    from concourse.bass_utils import run_bass_kernel_spmd

    lay = np.ascontiguousarray
    a = {k: np.asarray(v) for k, v in i.items()}
    column = lambda v: lay(v.reshape(-1, P).T)
    gub = a["L0_ffn_gate_up_bias"]
    arrays = {
        "x": lay(a["x"]),
        "ctx_t": lay(a["ctx_1024"].transpose(0, 2, 1)),
        "wq_t": lay(a["L0_xattn_Wq"].T), "wk_t": lay(a["L0_xattn_Wk"].T),
        "wv_t": lay(a["L0_xattn_Wv"].T), "wo_t": lay(a["L0_xattn_Wo"].T),
        "bq": column(a["L0_xattn_bq"]), "bk": column(a["L0_xattn_bk"]),
        "bv": lay(a["L0_xattn_bv"]), "bo": lay(a["L0_xattn_bo"]),
        "router_wt": lay(a["L0_ffn_router_weight"].T), "router_b": lay(a["L0_ffn_router_bias"]),
        "w_gate_up": lay(a["L0_ffn_gate_up_proj"]),
        "b_gate_up": lay(gub.reshape(gub.shape[0], -1, P).transpose(0, 2, 1)),
        "w_down": lay(a["L0_ffn_down_proj"]), "b_down": lay(a["L0_ffn_down_bias"]),
    }
    nc = bacc.Bacc("TRN2", target_bir_lowering=False, num_devices=1)
    args = [nc.dram_tensor(n, arrays[n].shape, mybir.dt.from_np(arrays[n].dtype), kind="ExternalInput").ap() for n in _INS]
    out = nc.dram_tensor("out", arrays["x"].shape, F32, kind="ExternalOutput").ap()
    build(nc, *args, out)
    r = run_bass_kernel_spmd(nc, [arrays], core_ids=[0])
    return r.results[0]["out"]
```
